# Optimizing a Trainium2 kernel written in Bass

```python
import numpy as np
import jax
import jax.numpy as jnp

def _softmax(x, axis=-1):
    return jax.nn.softmax(x, axis=axis)

def _gelu(x):
    return jax.nn.gelu(x, approximate=True)

def _silu(x):
    return jax.nn.silu(x)

def _sigmoid(x):
    return jax.nn.sigmoid(x)

def _layernorm(x, axis=-1, eps=1e-05):
    m = jnp.mean(x, axis=axis, keepdims=True)
    v = jnp.var(x, axis=axis, keepdims=True)
    return (x - m) / jnp.sqrt(v + eps)

def _scatter_add(tgt, idx, src, axis=0):
    return tgt.at[idx].add(src)

def _segment_sum(src, seg, n):
    return jax.ops.segment_sum(src, seg, n)
kernel_name = 'mk_flamingo_gated_d2_seqx_r4_42fb79'

def setup_inputs(seed: int=0):
    np.random.seed(seed)
    _w = jnp.asarray

    def _rec_inputs():
        import jax
        import jax.numpy as jnp
        _rk = jax.random.key(seed)
        x = -0.0002928 + 1 * jax.random.normal(jax.random.fold_in(_rk, 1), (32, 128, 256), jnp.float32)
        _lenS = 128 - jax.random.randint(jax.random.fold_in(_rk, 7), (32,), 0, max(1, 128 // 4) + 1, jnp.int32)
        _lenS2 = 128 - jax.random.randint(jax.random.fold_in(_rk, 8), (32,), 0, max(1, 128 // 4) + 1, jnp.int32)
        _ctx_1024P = jax.random.normal(jax.random.fold_in(_rk, 11), (32, 16, 256), jnp.float32)
        _ctx_1024c = jax.random.dirichlet(jax.random.fold_in(_rk, 511), 0.3 * jnp.ones((16,), jnp.float32), (32, 128))
        _ctx_1024t = jnp.einsum('bsk,bkd->bsd', _ctx_1024c, _ctx_1024P)
        _ctx_1024t = _ctx_1024t * jax.lax.rsqrt(jnp.mean(jnp.square(_ctx_1024t)) + 1e-12) * 0.953939
        ctx_1024 = -1.39393e-06 + 0.999914 * (_ctx_1024t + 0.3 * jax.random.normal(jax.random.fold_in(_rk, 611), (32, 128, 256), jnp.float32))
        fside_BxS2_0 = -0.00600047 + 0.990131 * jax.random.normal(jax.random.fold_in(_rk, 12), (32, 128), jnp.float32)
        _g = jax.random.normal(jax.random.fold_in(_rk, 9001), (2, 2), jnp.float32)
        _g = jnp.sign(_g) * jnp.maximum(jnp.abs(_g), 1.0) + (_g == 0) * 1.0
        g_xattn = _g[0]
        g_ffn = _g[1]
        return (x, ctx_1024, fside_BxS2_0, g_xattn, g_ffn)
    x, ctx_1024, fside_BxS2_0, g_xattn, g_ffn = _rec_inputs()

    def _L0_xattn_setup():
        import jax, jax.numpy as jnp
        import numpy as np
        D_MODEL = 256
        N_HEAD = 16
        D_HEAD = D_MODEL // N_HEAD

        def _split(x, B, L):
            return x.reshape(B, L, N_HEAD, D_HEAD).transpose(0, 2, 1, 3)
        key = jax.random.key(seed)
        ks = jax.random.split(key, 11)
        B, L = (2, 512)
        scale = 1.0 / np.sqrt(D_MODEL)
        inp = {'q': jax.random.normal(ks[0], (B, L, D_MODEL), jnp.float32), 'k': jax.random.normal(ks[1], (B, L, D_MODEL), jnp.float32), 'v': jax.random.normal(ks[2], (B, L, D_MODEL), jnp.float32), 'w_q': jax.random.normal(ks[3], (D_MODEL, D_MODEL), jnp.float32) * scale, 'b_q': jnp.zeros((D_MODEL,), jnp.float32), 'w_k': jax.random.normal(ks[4], (D_MODEL, D_MODEL), jnp.float32) * scale, 'b_k': jnp.zeros((D_MODEL,), jnp.float32), 'w_v': jax.random.normal(ks[5], (D_MODEL, D_MODEL), jnp.float32) * scale, 'b_v': jnp.zeros((D_MODEL,), jnp.float32), 'w_o': jax.random.normal(ks[6], (D_MODEL, D_MODEL), jnp.float32) * scale, 'b_o': jnp.zeros((D_MODEL,), jnp.float32)}
        return inp
    _L0_xattn_all = _L0_xattn_setup()
    _L0_xattn_in = {k: v for k, v in _L0_xattn_all.items() if k in ('w_q', 'b_q', 'w_k', 'b_k', 'w_v', 'b_v', 'w_o', 'b_o')}
    del _L0_xattn_all

    def _L0_ffn_setup():
        import jax, jax.numpy as jnp
        import numpy as np
        D = 256
        E = 8
        K = 2
        DF = 1024
        B, S = (2, 512)
        EPS_LN = 1e-05
        EPS_TOPK = 1e-08

        def _xavier(key, shape, fan_in, fan_out, dtype=jnp.float32):
            bound = float(np.sqrt(6.0 / (fan_in + fan_out)))
            return jax.random.uniform(key, shape, dtype, -bound, bound)
        key = jax.random.key(seed)
        kx, kg, k1, k2 = jax.random.split(key, 4)
        return {'x': jax.random.normal(kx, (B, S, D), jnp.float32), 'gamma': jnp.ones((D,), jnp.float32), 'beta': jnp.zeros((D,), jnp.float32), 'Wg': _xavier(kg, (E, D), D, E), 'bg': jnp.zeros((E,), jnp.float32), 'W1': _xavier(k1, (E, DF, D), D, DF), 'b1': jnp.zeros((E, DF), jnp.float32), 'W2': _xavier(k2, (E, D, DF), DF, D), 'b2': jnp.zeros((E, D), jnp.float32)}
    _L0_ffn_all = _L0_ffn_setup()
    _L0_ffn_in = {k: v for k, v in _L0_ffn_all.items() if k in ('gamma', 'beta', 'Wg', 'bg', 'W1', 'b1', 'W2', 'b2')}
    del _L0_ffn_all

    def _L1_xattn_setup():
        import jax, jax.numpy as jnp
        import numpy as np
        EMBED = 256
        NHEAD = 16
        HEAD_DIM = EMBED // NHEAD
        key = jax.random.key(seed)
        ks = jax.random.split(key, 8)
        B, SQ, SKV = (2, 512, 512)
        scale = 1.0 / np.sqrt(EMBED)
        return {'query': jax.random.normal(ks[0], (B, SQ, EMBED), dtype=jnp.float32), 'key': jax.random.normal(ks[1], (B, SKV, EMBED), dtype=jnp.float32), 'value': jax.random.normal(ks[2], (B, SKV, EMBED), dtype=jnp.float32), 'attention_bias': jax.random.normal(ks[3], (B, SKV), dtype=jnp.float32), 'Wq': jax.random.normal(ks[4], (EMBED, EMBED), dtype=jnp.float32) * scale, 'Wk': jax.random.normal(ks[5], (EMBED, EMBED), dtype=jnp.float32) * scale, 'Wv': jax.random.normal(ks[6], (EMBED, EMBED), dtype=jnp.float32) * scale, 'Wo': jax.random.normal(ks[7], (EMBED, EMBED), dtype=jnp.float32) * scale}
    _L1_xattn_all = _L1_xattn_setup()
    _L1_xattn_in = {k: v for k, v in _L1_xattn_all.items() if k in ('Wq', 'Wk', 'Wv', 'Wo')}
    del _L1_xattn_all

    def _L1_ffn_setup():
        import jax, jax.numpy as jnp
        import numpy as np
        B, L, D = (4, 512, 256)
        H = 16
        E = 16
        NS = 16
        S = NS // E
        F = 1024
        EPS = 1e-05

        def _layernorm(x, g, b):
            mu = jnp.mean(x, axis=-1, keepdims=True)
            var = jnp.mean(jnp.square(x - mu), axis=-1, keepdims=True)
            return (x - mu) * jax.lax.rsqrt(var + EPS) * g + b

        def _mha(q, k, v, Wq, bq, Wk, bk, Wv, bv, Wo, bo):
            Bq, Lq, Dm = q.shape
            dh = Dm // H
            qh = (q @ Wq + bq).reshape(Bq, Lq, H, dh)
            kh = (k @ Wk + bk).reshape(Bq, -1, H, dh)
            vh = (v @ Wv + bv).reshape(Bq, -1, H, dh)
            scores = jnp.einsum('bqhd,bkhd->bhqk', qh, kh) / jnp.asarray(np.sqrt(dh), q.dtype)
            attn = jax.nn.softmax(scores, axis=-1)
            out = jnp.einsum('bhqk,bkhd->bqhd', attn, vh).reshape(Bq, Lq, Dm)
            return out @ Wo + bo
        key = jax.random.key(seed)
        ks = jax.random.split(key, 32)
        s = 0.02
        d = {}
        d['x'] = jax.random.normal(ks[0], (B, L, D), jnp.float32)
        d['slot_query'] = jax.random.normal(ks[1], (1, NS, D), jnp.float32) * 0.01
        for i, nm in enumerate(['d_Wq', 'd_Wk', 'd_Wv', 'd_Wo']):
            d[nm] = jax.random.normal(ks[2 + i], (D, D), jnp.float32) * s
        for nm in ['d_bq', 'd_bk', 'd_bv', 'd_bo']:
            d[nm] = jnp.zeros((D,), jnp.float32)
        for i, nm in enumerate(['c_Wq', 'c_Wk', 'c_Wv', 'c_Wo']):
            d[nm] = jax.random.normal(ks[6 + i], (D, D), jnp.float32) * s
        for nm in ['c_bq', 'c_bk', 'c_bv', 'c_bo']:
            d[nm] = jnp.zeros((D,), jnp.float32)
        d['e_ln_g'] = jnp.ones((E, D), jnp.float32)
        d['e_ln_b'] = jnp.zeros((E, D), jnp.float32)
        d['e_W1'] = jax.random.normal(ks[10], (E, D, F), jnp.float32) * s
        d['e_b1'] = jnp.zeros((E, F), jnp.float32)
        d['e_Wg'] = jax.random.normal(ks[11], (E, D, F), jnp.float32) * s
        d['e_bg'] = jnp.zeros((E, F), jnp.float32)
        d['e_W2'] = jax.random.normal(ks[12], (E, F, D), jnp.float32) * s
        d['e_b2'] = jnp.zeros((E, D), jnp.float32)
        return d
    _L1_ffn_all = _L1_ffn_setup()
    _L1_ffn_in = {k: v for k, v in _L1_ffn_all.items() if k in ('slot_query', 'd_Wq', 'd_Wk', 'd_Wv', 'd_Wo', 'd_bq', 'd_bk', 'd_bv', 'd_bo', 'c_Wq', 'c_Wk', 'c_Wv', 'c_Wo', 'c_bq', 'c_bk', 'c_bv', 'c_bo', 'e_ln_g', 'e_ln_b', 'e_W1', 'e_b1', 'e_Wg', 'e_bg', 'e_W2', 'e_b2')}
    del _L1_ffn_all
    return {'x': x, 'ctx_1024': ctx_1024, 'fside_BxS2_0': fside_BxS2_0, 'g_xattn': g_xattn, 'g_ffn': g_ffn, 'L0_xattn_w_q': _L0_xattn_in['w_q'], 'L0_xattn_b_q': _L0_xattn_in['b_q'], 'L0_xattn_w_k': _L0_xattn_in['w_k'], 'L0_xattn_b_k': _L0_xattn_in['b_k'], 'L0_xattn_w_v': _L0_xattn_in['w_v'], 'L0_xattn_b_v': _L0_xattn_in['b_v'], 'L0_xattn_w_o': _L0_xattn_in['w_o'], 'L0_xattn_b_o': _L0_xattn_in['b_o'], 'L0_ffn_gamma': _L0_ffn_in['gamma'], 'L0_ffn_beta': _L0_ffn_in['beta'], 'L0_ffn_Wg': _L0_ffn_in['Wg'], 'L0_ffn_bg': _L0_ffn_in['bg'], 'L0_ffn_W1': _L0_ffn_in['W1'], 'L0_ffn_b1': _L0_ffn_in['b1'], 'L0_ffn_W2': _L0_ffn_in['W2'], 'L0_ffn_b2': _L0_ffn_in['b2'], 'L1_xattn_Wq': _L1_xattn_in['Wq'], 'L1_xattn_Wk': _L1_xattn_in['Wk'], 'L1_xattn_Wv': _L1_xattn_in['Wv'], 'L1_xattn_Wo': _L1_xattn_in['Wo'], 'L1_ffn_slot_query': _L1_ffn_in['slot_query'], 'L1_ffn_d_Wq': _L1_ffn_in['d_Wq'], 'L1_ffn_d_Wk': _L1_ffn_in['d_Wk'], 'L1_ffn_d_Wv': _L1_ffn_in['d_Wv'], 'L1_ffn_d_Wo': _L1_ffn_in['d_Wo'], 'L1_ffn_d_bq': _L1_ffn_in['d_bq'], 'L1_ffn_d_bk': _L1_ffn_in['d_bk'], 'L1_ffn_d_bv': _L1_ffn_in['d_bv'], 'L1_ffn_d_bo': _L1_ffn_in['d_bo'], 'L1_ffn_c_Wq': _L1_ffn_in['c_Wq'], 'L1_ffn_c_Wk': _L1_ffn_in['c_Wk'], 'L1_ffn_c_Wv': _L1_ffn_in['c_Wv'], 'L1_ffn_c_Wo': _L1_ffn_in['c_Wo'], 'L1_ffn_c_bq': _L1_ffn_in['c_bq'], 'L1_ffn_c_bk': _L1_ffn_in['c_bk'], 'L1_ffn_c_bv': _L1_ffn_in['c_bv'], 'L1_ffn_c_bo': _L1_ffn_in['c_bo'], 'L1_ffn_e_ln_g': _L1_ffn_in['e_ln_g'], 'L1_ffn_e_ln_b': _L1_ffn_in['e_ln_b'], 'L1_ffn_e_W1': _L1_ffn_in['e_W1'], 'L1_ffn_e_b1': _L1_ffn_in['e_b1'], 'L1_ffn_e_Wg': _L1_ffn_in['e_Wg'], 'L1_ffn_e_bg': _L1_ffn_in['e_bg'], 'L1_ffn_e_W2': _L1_ffn_in['e_W2'], 'L1_ffn_e_b2': _L1_ffn_in['e_b2']}

def reference(x, ctx_1024, fside_BxS2_0, g_xattn, g_ffn, L0_xattn_w_q, L0_xattn_b_q, L0_xattn_w_k, L0_xattn_b_k, L0_xattn_w_v, L0_xattn_b_v, L0_xattn_w_o, L0_xattn_b_o, L0_ffn_gamma, L0_ffn_beta, L0_ffn_Wg, L0_ffn_bg, L0_ffn_W1, L0_ffn_b1, L0_ffn_W2, L0_ffn_b2, L1_xattn_Wq, L1_xattn_Wk, L1_xattn_Wv, L1_xattn_Wo, L1_ffn_slot_query, L1_ffn_d_Wq, L1_ffn_d_Wk, L1_ffn_d_Wv, L1_ffn_d_Wo, L1_ffn_d_bq, L1_ffn_d_bk, L1_ffn_d_bv, L1_ffn_d_bo, L1_ffn_c_Wq, L1_ffn_c_Wk, L1_ffn_c_Wv, L1_ffn_c_Wo, L1_ffn_c_bq, L1_ffn_c_bk, L1_ffn_c_bv, L1_ffn_c_bo, L1_ffn_e_ln_g, L1_ffn_e_ln_b, L1_ffn_e_W1, L1_ffn_e_b1, L1_ffn_e_Wg, L1_ffn_e_bg, L1_ffn_e_W2, L1_ffn_e_b2):
    import jax
    import jax.numpy as jnp

    def _L0_xattn_ref(q, k, v, w_q, b_q, w_k, b_k, w_v, b_v, w_o, b_o):
        import jax, jax.numpy as jnp
        import numpy as np
        D_MODEL = 256
        N_HEAD = 16
        D_HEAD = D_MODEL // N_HEAD

        def _split(x, B, L):
            return x.reshape(B, L, N_HEAD, D_HEAD).transpose(0, 2, 1, 3)
        B, L, _ = q.shape
        qh = _split(q @ w_q + b_q, B, L)
        kh = _split(k @ w_k + b_k, B, L)
        vh = _split(v @ v.dtype.type(0) + v @ w_v + b_v, B, L) if False else _split(v @ w_v + b_v, B, L)
        scale = 1.0 / np.sqrt(D_HEAD).astype(np.float32)
        scores = jnp.einsum('bhqd,bhkd->bhqk', qh, kh) * scale
        attn = jax.nn.softmax(scores, axis=-1)
        out = jnp.einsum('bhqk,bhkd->bhqd', attn, vh)
        out = out.transpose(0, 2, 1, 3).reshape(B, L, D_MODEL)
        return out @ w_o + b_o

    def _L0_ffn_ref(x, gamma, beta, Wg, bg, W1, b1, W2, b2):
        import jax, jax.numpy as jnp
        import numpy as np
        D = 256
        E = 8
        K = 2
        DF = 1024
        B, S = (2, 512)
        EPS_LN = 1e-05
        EPS_TOPK = 1e-08

        def _xavier(key, shape, fan_in, fan_out, dtype=jnp.float32):
            bound = float(np.sqrt(6.0 / (fan_in + fan_out)))
            return jax.random.uniform(key, shape, dtype, -bound, bound)
        b, s, d = x.shape
        mu = jnp.mean(x, axis=-1, keepdims=True)
        var = jnp.mean((x - mu) ** 2, axis=-1, keepdims=True)
        xn = (x - mu) / jnp.sqrt(var + EPS_LN) * gamma + beta
        xf = xn.reshape(-1, d)
        logits = xf @ Wg.T + bg
        probs = jax.nn.softmax(logits, axis=-1)
        tp, ti = jax.lax.top_k(probs, K)
        tp = tp / (jnp.sum(tp, axis=-1, keepdims=True) + EPS_TOPK)
        w = jnp.sum(jax.nn.one_hot(ti, E, dtype=xf.dtype) * tp[..., None], axis=1)
        h = jax.nn.gelu(jnp.einsum('td,efd->tef', xf, W1) + b1, approximate=False)
        y = jnp.einsum('tef,edf->ted', h, W2) + b2
        out = jnp.einsum('ted,te->td', y, w)
        return x + out.reshape(b, s, d)

    def _L1_xattn_ref(query, key, value, attention_bias, Wq, Wk, Wv, Wo):
        import jax, jax.numpy as jnp
        import numpy as np
        EMBED = 256
        NHEAD = 16
        HEAD_DIM = EMBED // NHEAD
        B, SQ, _ = query.shape
        SKV = key.shape[1]

        def proj(x, W, S):
            return (x @ W.T).reshape(B, S, NHEAD, HEAD_DIM).transpose(0, 2, 1, 3)
        q = proj(query, Wq, SQ)
        k = proj(key, Wk, SKV)
        v = proj(value, Wv, SKV)
        scores = jnp.einsum('bhqd,bhkd->bhqk', q, k) / np.sqrt(HEAD_DIM)
        scores = scores + attention_bias[:, None, None, :]
        probs = jax.nn.softmax(scores, axis=-1)
        out = jnp.einsum('bhqk,bhkd->bhqd', probs, v)
        out = out.transpose(0, 2, 1, 3).reshape(B, SQ, EMBED)
        return out @ Wo.T

    def _L1_ffn_ref(x, slot_query, d_Wq, d_Wk, d_Wv, d_Wo, d_bq, d_bk, d_bv, d_bo, c_Wq, c_Wk, c_Wv, c_Wo, c_bq, c_bk, c_bv, c_bo, e_ln_g, e_ln_b, e_W1, e_b1, e_Wg, e_bg, e_W2, e_b2):
        import jax, jax.numpy as jnp
        import numpy as np
        B, L, D = (4, 512, 256)
        H = 16
        E = 16
        NS = 16
        S = NS // E
        F = 1024
        EPS = 1e-05

        def _layernorm(x, g, b):
            mu = jnp.mean(x, axis=-1, keepdims=True)
            var = jnp.mean(jnp.square(x - mu), axis=-1, keepdims=True)
            return (x - mu) * jax.lax.rsqrt(var + EPS) * g + b

        def _mha(q, k, v, Wq, bq, Wk, bk, Wv, bv, Wo, bo):
            Bq, Lq, Dm = q.shape
            dh = Dm // H
            qh = (q @ Wq + bq).reshape(Bq, Lq, H, dh)
            kh = (k @ Wk + bk).reshape(Bq, -1, H, dh)
            vh = (v @ Wv + bv).reshape(Bq, -1, H, dh)
            scores = jnp.einsum('bqhd,bkhd->bhqk', qh, kh) / jnp.asarray(np.sqrt(dh), q.dtype)
            attn = jax.nn.softmax(scores, axis=-1)
            out = jnp.einsum('bhqk,bkhd->bqhd', attn, vh).reshape(Bq, Lq, Dm)
            return out @ Wo + bo
        Bx = x.shape[0]
        q = jnp.broadcast_to(slot_query, (Bx, NS, D))
        o = q + _mha(q, x, x, d_Wq, d_bq, d_Wk, d_bk, d_Wv, d_bv, d_Wo, d_bo)
        os = o.reshape(Bx, E, S, D)
        h = _layernorm(os, e_ln_g[None, :, None, :], e_ln_b[None, :, None, :])
        u = jax.nn.silu(jnp.einsum('besd,edf->besf', h, e_W1) + e_b1[None, :, None, :])
        g = jax.nn.silu(jnp.einsum('besd,edf->besf', h, e_Wg) + e_bg[None, :, None, :])
        y = jnp.einsum('besf,efd->besd', u * g, e_W2) + e_b2[None, :, None, :]
        o = o + y.reshape(Bx, NS, D)
        out = _mha(x, o, o, c_Wq, c_bq, c_Wk, c_bk, c_Wv, c_bv, c_Wo, c_bo)
        return out
    x = x + jnp.tanh(g_xattn[0]) * _L0_xattn_ref(_layernorm(x, axis=-1), ctx_1024, ctx_1024, L0_xattn_w_q, L0_xattn_b_q, L0_xattn_w_k, L0_xattn_b_k, L0_xattn_w_v, L0_xattn_b_v, L0_xattn_w_o, L0_xattn_b_o)
    x = x + jnp.tanh(g_ffn[0]) * _L0_ffn_ref(_layernorm(x, axis=-1), L0_ffn_gamma, L0_ffn_beta, L0_ffn_Wg, L0_ffn_bg, L0_ffn_W1, L0_ffn_b1, L0_ffn_W2, L0_ffn_b2)
    x = x + jnp.tanh(g_xattn[1]) * _L1_xattn_ref(_layernorm(x, axis=-1), ctx_1024, ctx_1024, fside_BxS2_0, L1_xattn_Wq, L1_xattn_Wk, L1_xattn_Wv, L1_xattn_Wo)
    x = x + jnp.tanh(g_ffn[1]) * _L1_ffn_ref(_layernorm(x, axis=-1), L1_ffn_slot_query, L1_ffn_d_Wq, L1_ffn_d_Wk, L1_ffn_d_Wv, L1_ffn_d_Wo, L1_ffn_d_bq, L1_ffn_d_bk, L1_ffn_d_bv, L1_ffn_d_bo, L1_ffn_c_Wq, L1_ffn_c_Wk, L1_ffn_c_Wv, L1_ffn_c_Wo, L1_ffn_c_bq, L1_ffn_c_bk, L1_ffn_c_bv, L1_ffn_c_bo, L1_ffn_e_ln_g, L1_ffn_e_ln_b, L1_ffn_e_W1, L1_ffn_e_b1, L1_ffn_e_Wg, L1_ffn_e_bg, L1_ffn_e_W2, L1_ffn_e_b2)
    return x

_drawn_inputs = setup_inputs


def setup_inputs(seed=0):
    import zlib

    import numpy as np

    out = dict(_drawn_inputs(seed))
    spreads = {'g_ffn': (-1.0, 0.6),
     'L0_xattn_b_q': (0.0, 0.1),
     'L0_xattn_b_k': (0.0, 2.0),
     'L0_xattn_b_v': (0.0, 0.1),
     'L0_xattn_b_o': (0.0, 0.1),
     'L0_ffn_gamma': (1.0, 0.2),
     'L0_ffn_beta': (0.0, 0.1),
     'L0_ffn_bg': (0.0, 0.1),
     'L0_ffn_b1': (0.0, 0.1),
     'L0_ffn_b2': (0.0, 0.1),
     'L1_ffn_d_bq': (0.0, 0.8),
     'L1_ffn_d_bk': (0.0, 2.0),
     'L1_ffn_d_bv': (0.0, 0.8),
     'L1_ffn_d_bo': (0.0, 0.705),
     'L1_ffn_c_bq': (0.0, 0.8),
     'L1_ffn_c_bk': (0.0, 2.0),
     'L1_ffn_c_bv': (0.0, 2.0),
     'L1_ffn_c_bo': (0.0, 0.8),
     'L1_ffn_e_ln_g': (1.0, 0.6),
     'L1_ffn_e_ln_b': (0.0, 0.8),
     'L1_ffn_e_b1': (0.0, 0.8),
     'L1_ffn_e_bg': (0.0, 0.8),
     'L1_ffn_e_b2': (0.0, 0.8)}
    factors = {'L1_ffn_slot_query': 8.0,
     'L1_ffn_d_Wq': 8.0,
     'L1_ffn_d_Wk': 8.0,
     'L1_ffn_d_Wv': 6.12,
     'L1_ffn_d_Wo': 5.767,
     'L1_ffn_c_Wq': 8.0,
     'L1_ffn_c_Wk': 8.0,
     'L1_ffn_c_Wv': 3.861,
     'L1_ffn_e_W1': 8.0,
     'L1_ffn_e_Wg': 8.0,
     'L1_ffn_e_W2': 8.0}
    for name, (base, spread) in spreads.items():
        noise = np.random.default_rng([zlib.crc32(name.encode()), seed]).standard_normal(out[name].shape)
        drawn = base * np.exp(spread * noise) if base else spread * noise
        out[name] = jnp.asarray(drawn.astype(out[name].dtype))
    for name, factor in factors.items():
        out[name] = (out[name] * factor).astype(out[name].dtype)
    return out
```

```python
from contextlib import ExitStack

import numpy as np
import concourse.bass as bass
from concourse import mybir

ALU = mybir.AluOpType
ACT = mybir.ActivationFunctionType
AX = mybir.AxisListType.X
F32 = mybir.dt.float32
I32 = mybir.dt.int32
U32 = mybir.dt.uint32

P = 128
B, D, H = 32, 256, 16
DH = D // H
C = D // P
HC = H // C
G = 4
E0, F0 = 8, 1024
E1, F1, NS = 16, 1024, 16
UNITS = 2 * B + E0
RING = 3
SETS = 3
ARENA = 34168
EPS = 1e-5
QSCALE = 0.25

CONSTS = {"ident": 128, "tri": 128, "mask8": 8, "iota8": 8, "thr": 32, "iotau": UNITS}
WEIGHTS = ["q0", "k0", "v0", "o0", "q1", "k1", "v1", "o1", "dv", "do", "cq", "ck", "cv", "co"]
ROWS = ["bv0", "bo0", "gamma", "beta", "dbv", "dbo", "cbv", "cbo"]
COLS = ["bq0", "bk0", "dbq", "dbk", "cbq", "cbk"]


class Track:

    def __init__(self, sem, steps, items, base=0):
        self.sem, self.steps, self.items, self.base = sem, steps, items, base

    def at(self, item, step):
        if isinstance(item, int):
            item = min(item, self.items - 1)
        return item * len(self.steps) + (self.steps.index(step) + 1 + self.base)


def build(nc, a, out):
    ctx = ExitStack()
    with ctx:
        def sb(name, shape, dt=F32):
            return ctx.enter_context(nc.sbuf_tensor(name, shape, dt))

        def sem(name):
            return ctx.enter_context(nc.semaphore(name))

        def track(name, steps, items=B, base=0):
            return Track(sem(name), steps.split(), items, base)

        x_all = sb("x_all", [P, B, D])
        w_sb = sb("w_sb", [P, len(WEIGHTS), C, D])
        row_sb = sb("row_sb", [P, len(ROWS), D])
        col_sb = sb("col_sb", [P, len(COLS), C])
        const = sb("const", [P, sum(CONSTS.values())])
        wg_sb = sb("wg_sb", [P, C, E0])
        bg_sb = sb("bg_sb", [P, E0])
        gates = sb("gates", [P, 4])
        tg = sb("tg", [P, 4])
        qcol = sb("qcol", [P, 3, C])
        eps_sb = sb("eps_sb", [P, 1])
        mhalf = sb("mhalf", [P, 1])
        ones = sb("ones", [P, P])
        top_val = sb("top_val", [P, B, 8])
        top_idx = sb("top_idx", [P, B, 2])
        top8 = sb("top8", [P, 8])
        idx8 = sb("idx8", [P, 8], U32)
        slot_i = sb("slot_i", [P, 2, B], I32)
        wts = sb("wts", [P, 2, B])
        unit_e = sb("unit_e", [1, UNITS], I32)
        unit_r = sb("unit_r", [1, UNITS], I32)
        cend_i = sb("cend_i", [1, E0], I32)
        zero = sb("zero", [P, D])
        arena = sb("arena", [P, ARENA])
        cv = {}
        at = 0
        for n, w in CONSTS.items():
            cv[n] = const[:, at:at + w]
            at += w
        w = {n: w_sb[:, i] for i, n in enumerate(WEIGHTS)}
        row = {n: row_sb[:, i] for i, n in enumerate(ROWS)}
        col = {n: col_sb[:, i] for i, n in enumerate(COLS)}

        place = [0]

        def carve(*shape):
            n = int(np.prod(shape))
            v = arena[:, place[0]:place[0] + n]
            place[0] += n
            if len(shape) > 1:
                names = [f"d{i}" for i in range(len(shape))]
                v = v.rearrange(f"p ({' '.join(names)}) -> p {' '.join(names)}", **dict(zip(names[1:], shape[1:])))
            return v

        ctxT = carve(2, C, P)
        xh = carve(2, D)
        xT = carve(C, P)
        kT = carve(C, P)
        qT = carve(2, C, P)
        kbd = carve(2 * C, HC, P)
        pr = carve(2, G, 512)
        pT = carve(2, 512)
        vaug = carve(2, H, DH + 1)
        att = carve(D)
        aT = carve(C, P)
        tmp = att
        xo = carve(D)
        xh3 = carve(D)
        xg = carve(D)
        xnT = carve(C, P)
        xc = carve(D)
        stat = carve(3, 6)
        mv = carve(3, 2)
        rstd = carve(3, 2)
        mx = carve(2, G)
        rden = carve(H)
        lg = carve(E0)
        attention_end = place[0]
        ring = carve(RING, 2 * C * F0 + 0)
        xn_all = carve(B, D)
        assert place[0] <= ARENA, place[0]
        after_ring = place[0] - B * D
        place[0] = 0
        b1_sb = carve(E0, F0)
        b2_sb = carve(E0, D)
        moe_rows_end = place[0]
        place[0] = after_ring
        xs = carve(2, D)
        xsT = carve(2, C, P)
        hid = carve(2, F0)
        hidT = carve(2, F0 // P, P)
        yb = carve(2, D)
        assert place[0] <= after_ring + B * D
        place[0] = moe_rows_end
        idxf = carve(B, 2)
        oh = carve(2, B, E0)
        msk = carve(B, E0)
        tot = carve(B, E0)
        inc = carve(B, E0)
        pos = carve(B, E0)
        ohp = carve(B, E0)
        posf = carve(2, B)
        blk = carve(E0, B)
        nblk = carve(E0)
        cend = carve(E0)
        basev = carve(E0)
        ucmp = carve(UNITS, E0)
        uexp = carve(UNITS)
        urng = carve(UNITS)
        ex = carve(B, 8)
        zs = carve(B)
        s2 = carve(B)
        den = carve(B)
        rr = carve(B)
        urng2 = carve(UNITS)
        assert place[0] <= attention_end, (place[0], attention_end)
        place[0] = attention_end
        wset = carve(SETS, 4, F1)
        oT_all = carve(C, NS, B)
        layer1_shared_end = place[0]
        yg = carve(2, 2, D)
        idx_cur = carve(2, 2).bitcast(I32)
        fs = carve(2, P)
        sbias = carve(2, 512)
        dVb = carve(2, D)
        sc = carve(C, P)
        pn = carve(C, P)
        pnT = carve(C, P)
        mk = carve(C, HC, NS)
        smx = carve(2)
        snx = carve(2)
        sz = carve(2)
        srz = carve(2)
        qa = carve(C, D)
        qac = carve(C)
        x3T = carve(C, P)
        assert place[0] <= ARENA, place[0]
        prep_w = pr.rearrange("p u g t -> p (u g t)")[:, 0:2 * C * D].rearrange("p (n c d) -> p n c d", n=2, c=C)
        slotT = ctxT[:, 0, 0, 0:C * NS].rearrange("p (c s) -> p c s", c=C)
        sqT = ctxT[:, 0, 1, 0:C * NS].rearrange("p (c s) -> p c s", c=C)
        qbd = kbd[:, 0:C, 0, :].rearrange("p c (h s) -> p c h s", h=HC)
        place[0] = 0
        sel = carve(4, P)
        small = carve(4, D)
        bias1 = carve(2, F1)
        orow = carve(4, D)
        hrow = carve(D)
        hT = carve(C, 4, P)
        us = carve(F1)
        gs = carve(F1)
        ugT = carve(F1 // P, P)
        oT2 = carve(C, NS, B)
        kTall = carve(C, NS, B)
        st1 = carve(6)
        mv1 = carve(2)
        rs1 = carve(2)
        slots_end = place[0]
        assert slots_end <= attention_end, (slots_end, attention_end)
        place[0] = attention_end
        x3l = carve(2, C, P)
        cqT = carve(2, C, P)
        orep = carve(2, C, HC, NS)
        ckb = carve(2, C, HC, NS)
        cvb = carve(2, D)
        cvbd = carve(2, C, P)
        csc = carve(2, D)
        cpn = carve(D)
        cpT = carve(C, P)
        caT = carve(C, P)
        ctmp = carve(D)
        cout = carve(2, D)
        cmx = carve(H)
        csm = carve(H)
        assert place[0] <= layer1_shared_end

        ps = [ctx.enter_context(nc.psum_tensor(f"ps{i}", [P, 512], F32)) for i in range(8)]

        xs_dram = nc.dram_tensor("xs_rows", (UNITS * P, D), F32, kind="Internal").ap()
        x3T_dram = nc.dram_tensor("x3_transposed", (B, P, C * P), F32, kind="Internal").ap()
        ys_dram = nc.dram_tensor("ys_rows", (UNITS * P, D), F32, kind="Internal").ap()

        ld_const, zeroed, zdone, scattered = sem("ld_const"), sem("zeroed"), sem("zdone"), sem("scattered")
        ld_w = sem("ld_w")
        passed = sem("passed")
        setup_v, setup_a = sem("setup_v"), sem("setup_a")
        ld_x = [sem("ld_x0"), sem("ld_x1")]

        def before(eng, s, value):
            if not isinstance(value, int) or value > 0:
                eng.wait_ge(s, value)

        def settled(eng):
            eng.sem_inc(passed, 1)

        def dma_at(i, u, n=1):
            return (i - u) * (8 * n) + 16 * n

        def pipeline(eng, body, first=-2, last=B + 4, steady=(4, B - 2)):
            for k in range(first, steady[0]):
                body(k, k % 2)
            with eng.Fori(steady[0] // 2, steady[1] // 2) as j:
                body(2 * j, 0)
                body(2 * j + 1, 1)
            for k in range(steady[1], last):
                body(k, k % 2)

        def valid(i):
            return not isinstance(i, int) or 0 <= i < B

        def attention(L):
            n = f"a{L}_"
            A = L == 0
            last_k, steady = (B + 4, (4, B - 2)) if A else (B + 5, (6, B - 2))
            wq, wk, wv, wo = (w[f"{c}{L}"] for c in "qkvo")
            ld_ctx = [sem(n + "ld_ctx0"), sem(n + "ld_ctx1")]
            pre_p = track(n + "pre_p", "xT K Q V")
            sc_p = track(n + "sc_p", "0 1 2 3")
            tr_p = track(n + "tr_p", "0 1 2 3")
            pv_p = track(n + "pv_p", "0 1 2 3")
            out_p = track(n + "out_p", "oT O")
            pre_a = track(n + "pre_a", "xT K Q")
            ex_a = track(n + "ex_a", "0 1 2 3")
            tr_a = track(n + "tr_a", "0 1 2 3")
            out_a = track(n + "out_a", "oT")
            ln_v = track(n + "ln_v", "stats mean xh")
            v_v = track(n + "v_v", "V")
            sc_v = track(n + "sc_v", "m0 s0 m1 s1 m2 s2 m3 s3" if A else "a0 m0 a1 m1 a2 m2 a3 m3")
            out_v = track(n + "out_v", "den att t x")
            ln_g = track(n + "ln_g", "var rstd")
            keep_a = track(n + "keep_a", "x")
            kb_g = track(n + "kb_g", "0 1")
            rd = ("s" if A else "a")
            if A:
                rt_p = track(n + "rt_p", "xnT lg")
                rt_a = track(n + "rt_a", "xnT")
                rt_v = track(n + "rt_v", "lg top idx keep_top keep_idx")
                n2_v = track(n + "n2_v", "stats mean xo res stats3 mean3 xh3")
                n2_g = track(n + "n2_g", "var rstd var3 rstd3 gamma xn")
            else:
                sub_g = track(n + "sub_g", "0 1 2 3")
                gidx_g = track(n + "gidx_g", "idx")
                ld_y = [sem(n + "ld_y0"), sem(n + "ld_y1")]
                ld_fs = [sem(n + "ld_fs0"), sem(n + "ld_fs1")]
                mix_v = track(n + "mix_v", "y0 y1")
                n4_v = track(n + "n4_v", "stats mean xh")
                n4_g = track(n + "n4_g", "var rstd")
                x1_p = track(n + "x1_p", "xT s V")
                x1_a = track(n + "x1_a", "xT e0 e1")
                x1_v = track(n + "x1_v", "s0 s1 neg V")
                x2_p = track(n + "x2_p", "pT av")
                x2_a = track(n + "x2_a", "pT")
                x2_v = track(n + "x2_v", "rz pn mask sum")
                st_x3 = [sem(n + "st_x3_0"), sem(n + "st_x3_1")]

            def flat(t, i, g, back):
                return i * 4 + g + 1 - back

            def sync(sp):
                for u in range(2):
                    sp.dma_start(ctxT[:, u].rearrange("p c t -> p (c t)"), a["ctxT"][u]).then_inc(ld_ctx[u], 16)
                    if not A:
                        sp.dma_start(fs[:, u], a["fside"][u:u + 1, :].partition_broadcast(P)).then_inc(ld_fs[u], 16)

                def body(k, u):
                    if not A and valid(k + 1) and (not isinstance(k, int) or k >= 1):
                        sp.wait_ge(sc_v.sem, sc_v.at(k - 1, "a3"))
                        sp.dma_start(fs[:, 1 - u], a["fside"][bass.ds(k + 1, 1), :].partition_broadcast(P))\
                            .then_inc(ld_fs[1 - u], 16)
                    if not A and valid(k - 4):
                        sp.wait_ge(x1_a.sem, x1_a.at(k - 4, "xT"))
                        sp.dma_start(x3T_dram[k - 4], x3T.rearrange("p c t -> p (c t)")).then_inc(st_x3[u], 16)
                    if A and valid(k + 4) and (not isinstance(k, int) or k >= -2):
                        i = k + 4
                        before(sp, ln_v.sem, ln_v.at(k + 2, "stats"))
                        sp.dma_start(x_all[:, i], a["x"][i]).then_inc(ld_x[u], 16)
                    if valid(k + 3) and (not isinstance(k, int) or k + 3 >= 2):
                        i = k + 3
                        before(sp, pre_p.sem, pre_p.at(k + 1, "V"))
                        sp.dma_start(ctxT[:, 1 - u].rearrange("p c t -> p (c t)"), a["ctxT"][i]).then_inc(ld_ctx[1 - u], 16)
                pipeline(sp, body, first=-2, last=B - 2 if A else B + 4, steady=(4 if A else 6, B - 4))
                if not A:
                    for s in st_x3:
                        sp.wait_ge(s, 8 * B)

            def tensor(pe):
                def weighted_values(k, u, g):
                    pe.wait_ge(tr_a.sem, tr_a.at(k, str(g)))
                    if g == 0:
                        pe.wait_ge(v_v.sem, v_v.at(k, "V"))
                        before(pe, out_v.sem, out_v.at(k - 1, "att"))
                    for h in range(G):
                        hh = g * G + h
                        last = nc.tensor.matmul(ps[4][:, hh * (DH + 1):(hh + 1) * (DH + 1)],
                                                pT[:, g % 2, h * P:(h + 1) * P], vaug[:, u, hh, :],
                                                start=True, stop=True)
                    last.then_inc(pv_p.sem, 1)

                def body(k, u):
                    for g in range(G):
                        if valid(k - 1):
                            pe.wait_ge(ex_a.sem, ex_a.at(k - 1, str(g)))
                            before(pe, tr_a.sem, flat(tr_a, k - 1, g, 2))
                            for h in range(G):
                                last = nc.tensor.transpose(ps[2 + g % 2][:, h * P:(h + 1) * P],
                                                           pr[:, 1 - u, g, h * P:(h + 1) * P], cv["ident"])
                            last.then_inc(tr_p.sem, 1)
                        if valid(k):
                            pe.wait_ge(pre_a.sem, pre_a.at(k, "Q"))
                            pe.wait_ge(kb_g.sem, kb_g.at(k, str(g // 2)))
                            before(pe, sc_v.sem, sc_v.at(k, f"{rd}{g}") - 4)
                            c, r = g // 2, (g % 2) * 4
                            nc.tensor.matmul(ps[g % 2][:, :], qT[:, u, c, :],
                                             kbd[:, C * u + c, r:r + 4, :],
                                             start=True, stop=True).then_inc(sc_p.sem, 1)
                        if g > 0 and valid(k - 1):
                            weighted_values(k - 1, 1 - u, g - 1)
                        if valid(k + 1):
                            i, o = k + 1, 1 - u
                            if g == 0:
                                pe.wait_ge(ln_v.sem, ln_v.at(i, "xh"))
                                before(pe, v_v.sem, v_v.at(k, "V"))
                                if not A:
                                    before(pe, x2_v.sem, x2_v.at(k - 6, "mask"))
                                for c in range(C):
                                    last = nc.tensor.transpose(ps[5][:, c * P:(c + 1) * P],
                                                               xh[:, o, c * P:(c + 1) * P], cv["ident"])
                                last.then_inc(pre_p.sem, 1)
                                pe.wait_ge(ld_ctx[o], dma_at(i, o))
                                before(pe, pre_a.sem, pre_a.at(k, "Q"))
                                for m in range(C):
                                    for c in range(C):
                                        last = nc.tensor.matmul(ps[6][:, m * P:(m + 1) * P],
                                                                wk[:, c, m * P:(m + 1) * P], ctxT[:, o, c, :],
                                                                start=c == 0, stop=c == C - 1)
                                last.then_inc(pre_p.sem, 1)
                            if g == 2:
                                pe.wait_ge(pre_a.sem, pre_a.at(i, "K"))
                                if not A:
                                    before(pe, x2_a.sem, x2_a.at(k - 5, "pT"))
                                for m in range(C):
                                    for c in range(C):
                                        last = nc.tensor.matmul(ps[6][:, m * P:(m + 1) * P],
                                                                wq[:, c, m * P:(m + 1) * P], xT[:, c, :],
                                                                start=c == 0, stop=c == C - 1)
                                last.then_inc(pre_p.sem, 1)
                            if g == 3:
                                pe.wait_ge(pre_a.sem, pre_a.at(i, "xT"))
                                if not A:
                                    before(pe, x1_v.sem, x1_v.at(k - 4, "V"))
                                for c in range(C):
                                    last = nc.tensor.matmul(ps[5][:, 0:D], ctxT[:, o, c, :], wv[:, c, :],
                                                            start=c == 0, stop=c == C - 1)
                                last.then_inc(pre_p.sem, 1)
                        if A and valid(k - 4):
                            i = k - 4
                            if g == 0:
                                pe.wait_ge(n2_g.sem, n2_g.at(i, "xn"))
                                before(pe, out_v.sem, out_v.at(k - 3, "t"))
                                for c in range(C):
                                    last = nc.tensor.transpose(ps[7][:, c * P:(c + 1) * P],
                                                               xc[:, c * P:(c + 1) * P], cv["ident"])
                                last.then_inc(rt_p.sem, 1)
                            if g == 1:
                                pe.wait_ge(rt_a.sem, rt_a.at(i, "xnT"))
                                for c in range(C):
                                    last = nc.tensor.matmul(ps[7][:, 0:E0], xnT[:, c, :], wg_sb[:, c, :],
                                                            start=c == 0, stop=c == C - 1)
                                last.then_inc(rt_p.sem, 1)
                        if not A and valid(k - 4):
                            i = k - 4
                            if g == 0:
                                pe.wait_ge(n4_v.sem, n4_v.at(i, "xh"))
                                before(pe, out_v.sem, out_v.at(k - 3, "t"))
                                for c in range(C):
                                    last = nc.tensor.transpose(ps[7][:, c * P:(c + 1) * P],
                                                               xc[:, c * P:(c + 1) * P], cv["ident"])
                                last.then_inc(x1_p.sem, 1)
                            if g == 1:
                                pe.wait_ge(x1_a.sem, x1_a.at(i, "xT"))
                                for m in range(C):
                                    for c in range(C):
                                        last = nc.tensor.matmul(ps[7][:, D + m * P:D + (m + 1) * P],
                                                                qa[:, c, m * P:(m + 1) * P], x3T[:, c, :],
                                                                start=c == 0, stop=c == C - 1)
                                last.then_inc(x1_p.sem, 1)
                                before(pe, pre_a.sem, pre_a.at(k + 1, "xT"))
                                before(pe, v_v.sem, v_v.at(k, "V"))
                                before(pe, x2_v.sem, x2_v.at(k - 6, "mask"))
                                for c in range(C):
                                    last = nc.tensor.matmul(ps[5][:, D:2 * D], x3T[:, c, :], w["dv"][:, c, :],
                                                            start=c == 0, stop=c == C - 1)
                                last.then_inc(x1_p.sem, 1)
                        if not A and valid(k - 5):
                            i = k - 5
                            if g == 1:
                                pe.wait_ge(x2_v.sem, x2_v.at(i, "pn"))
                                before(pe, pre_a.sem, pre_a.at(k + 1, "K"))
                                for c in range(C):
                                    last = nc.tensor.transpose(ps[6][:, D + c * P:D + (c + 1) * P],
                                                               pn[:, c, :], cv["ident"])
                                last.then_inc(x2_p.sem, 1)
                            if g == 3:
                                pe.wait_ge(x2_a.sem, x2_a.at(i, "pT"))
                                before(pe, x1_v.sem, x1_v.at(k - 4, "V"))
                                before(pe, pre_a.sem, pre_a.at(k + 1, "xT"))
                                for m in range(C):
                                    last = nc.tensor.matmul(ps[5][:, D + m * P:D + (m + 1) * P],
                                                            dVb[:, 1 - u, m * P:(m + 1) * P],
                                                            pnT[:, m, :], start=True, stop=True)
                                last.then_inc(x2_p.sem, 1)
                        if valid(k - 2):
                            i = k - 2
                            if g == 2:
                                pe.wait_ge(out_v.sem, out_v.at(i, "att"))
                                if A:
                                    before(pe, rt_v.sem, rt_v.at(k - 4, "lg"))
                                else:
                                    before(pe, x1_v.sem, x1_v.at(k - 4, "s1"))
                                for c in range(C):
                                    last = nc.tensor.transpose(ps[7][:, c * P:(c + 1) * P],
                                                               att[:, c * P:(c + 1) * P], cv["ident"])
                                last.then_inc(out_p.sem, 1)
                            if g == 3:
                                pe.wait_ge(out_a.sem, out_a.at(i, "oT"))
                                for c in range(C):
                                    last = nc.tensor.matmul(ps[7][:, D:2 * D], aT[:, c, :], wo[:, c, :],
                                                            start=c == 0, stop=c == C - 1)
                                last.then_inc(out_p.sem, 1)
                        if g == 3 and valid(k - 1):
                            weighted_values(k - 1, 1 - u, 3)
                pipeline(pe, body, last=last_k, steady=steady)

            def scalar(act):
                def body(k, u):
                    for g in range(G):
                        if valid(k - 1):
                            act.wait_ge(tr_p.sem, tr_p.at(k - 1, str(g)))
                            before(act, pv_p.sem, flat(pv_p, k - 1, g, 2))
                            nc.scalar.copy(pT[:, g % 2, :], ps[2 + g % 2][:, :]).then_inc(tr_a.sem, 1)
                        i, e, v = (k, g - 1, u) if g else (k - 1, G - 1, 1 - u)
                        if valid(i):
                            if A:
                                act.wait_ge(sc_v.sem, sc_v.at(i, f"s{e}"))
                            else:
                                act.wait_ge(sub_g.sem, sub_g.at(i, str(e)))
                            nc.scalar.activation(pr[:, v, e, :], pr[:, v, e, :], ACT.Exp).then_inc(ex_a.sem, 1)
                        if valid(k + 1):
                            i, o = k + 1, 1 - u
                            if g == 0:
                                act.wait_ge(pre_p.sem, pre_p.at(i, "xT"))
                                before(act, pre_p.sem, pre_p.at(k, "Q"))
                                nc.scalar.copy(xT.rearrange("p c t -> p (c t)"), ps[5][:, 0:D]).then_inc(pre_a.sem, 1)
                                act.wait_ge(pre_p.sem, pre_p.at(i, "K"))
                                before(act, kb_g.sem, kb_g.at(k, "1"))
                                for c in range(C):
                                    last = nc.scalar.activation(kT[:, c, :], ps[6][:, c * P:(c + 1) * P], ACT.Identity,
                                                                bias=col["bk0"][:, c:c + 1] if A else 0.0)
                                last.then_inc(pre_a.sem, 1)
                        if not A and g == 1 and valid(k - 5):
                            act.wait_ge(x2_p.sem, x2_p.at(k - 5, "pT"))
                            before(act, pre_p.sem, pre_p.at(k + 1, "K"))
                            before(act, x2_p.sem, x2_p.at(k - 6, "av"))
                            nc.scalar.copy(pnT.rearrange("p c t -> p (c t)"), ps[6][:, D:2 * D]).then_inc(x2_a.sem, 1)
                        if A and g == 0 and valid(k - 4):
                            act.wait_ge(rt_p.sem, rt_p.at(k - 4, "xnT"))
                            nc.scalar.copy(xnT.rearrange("p c t -> p (c t)"), ps[7][:, 0:D]).then_inc(rt_a.sem, 1)
                            nc.scalar.copy(xn_all[:, k - 4, :], xc).then_inc(keep_a.sem, 1)
                        if not A and g == 0 and valid(k - 4):
                            act.wait_ge(x1_p.sem, x1_p.at(k - 4, "xT"))
                            before(act, x1_p.sem, x1_p.at(k - 5, "V"))
                            before(act, st_x3[1 - u], dma_at(k - 5, 1 - u) if not isinstance(k, int) or k >= 5 else 0)
                            nc.scalar.copy(x3T.rearrange("p c t -> p (c t)"), ps[7][:, 0:D]).then_inc(x1_a.sem, 1)
                        if g == 2 and valid(k - 2):
                            act.wait_ge(out_p.sem, out_p.at(k - 2, "oT"))
                            before(act, out_p.sem, out_p.at(k - 3, "O"))
                            nc.scalar.copy(aT.rearrange("p c t -> p (c t)"), ps[7][:, 0:D]).then_inc(out_a.sem, 1)
                        if g == 2 and valid(k + 1):
                            i, o = k + 1, 1 - u
                            act.wait_ge(pre_p.sem, pre_p.at(i, "Q"))
                            before(act, sc_p.sem, sc_p.at(k - 1, "3"))
                            for c in range(C):
                                last = nc.scalar.activation(qT[:, o, c, :], ps[6][:, c * P:(c + 1) * P], ACT.Identity,
                                                            bias=qcol[:, 0, c:c + 1] if A else 0.0, scale=QSCALE)
                            last.then_inc(pre_a.sem, 1)
                        if not A and g == 3 and valid(k - 4):
                            act.wait_ge(x1_v.sem, x1_v.at(k - 4, "neg"))
                            before(act, x2_v.sem, x2_v.at(k - 5, "pn"))
                            for c in range(C):
                                nc.scalar.activation(sc[:, c, :], sc[:, c, :], ACT.Exp, bias=snx[:, c:c + 1],
                                                     accum_out=sz[:, c:c + 1]).then_inc(x1_a.sem, 1)
                pipeline(act, body, last=last_k, steady=steady)

            def vector(dve):
                def body(k, u):
                    for g in range(G):
                        if g == 0 and valid(k - 2):
                            i = k - 2
                            dve.wait_ge(pv_p.sem, pv_p.at(i, "3"))
                            pv = ps[4][:, 0:H * (DH + 1)].rearrange("p (h d) -> p h d", h=H)
                            nc.vector.reciprocal(rden, pv[:, :, DH]).then_inc(out_v.sem, 1)
                            dve.wait_ge(out_v.sem, out_v.at(i, "den"))
                            before(dve, out_p.sem, out_p.at(k - 3, "oT"))
                            nc.vector.tensor_tensor(att.rearrange("p (h d) -> p h d", h=H), pv[:, :, 0:DH],
                                                    rden[:, :, None].to_broadcast([P, H, DH]), ALU.mult)\
                                .then_inc(out_v.sem, 1)
                        if valid(k):
                            s = ps[g % 2][:, :].rearrange("p (h t) -> p h t", h=G)
                            dst = pr[:, u, g, :].rearrange("p (h t) -> p h t", h=G)
                            m = mx[:, g % 2, :]
                            dve.wait_ge(sc_p.sem, sc_p.at(k, str(g)))
                            if A:
                                nc.vector.tensor_reduce(m, s, AX, ALU.max).then_inc(sc_v.sem, 1)
                                dve.wait_ge(sc_v.sem, sc_v.at(k, f"m{g}"))
                                before(dve, tr_p.sem, tr_p.at(k - 2, str(g)))
                                nc.vector.tensor_tensor(dst, s, m[:, :, None].to_broadcast([P, G, P]),
                                                        ALU.subtract).then_inc(sc_v.sem, 1)
                            else:
                                if g == 0:
                                    dve.wait_ge(ld_fs[u], dma_at(k, u))
                                before(dve, sub_g.sem, flat(sub_g, k, g, 2))
                                sbv = sbias[:, g % 2, :].rearrange("p (h t) -> p h t", h=G)
                                nc.vector.tensor_tensor(sbv, s, fs[:, u, None, :].to_broadcast([P, G, P]),
                                                        ALU.add).then_inc(sc_v.sem, 1)
                                dve.wait_ge(sc_v.sem, sc_v.at(k, f"a{g}"))
                                nc.vector.tensor_reduce(m, sbv, AX, ALU.max).then_inc(sc_v.sem, 1)
                        if g == 0 and not A and valid(k + 2):
                            i = k + 2
                            dve.wait_ge(ld_y[u], dma_at(i, u, 2))
                            for c in range(2):
                                nc.vector.scalar_tensor_tensor(out=x_all[:, i], in0=yg[:, u, c, :],
                                                               scalar=wts[:, c, bass.ds(i, 1)], in1=x_all[:, i],
                                                               op0=ALU.mult, op1=ALU.add).then_inc(mix_v.sem, 1)
                                dve.wait_ge(mix_v.sem, mix_v.at(i, f"y{c}"))
                        if not A and g == 0 and valid(k - 5):
                            i = k - 5
                            dve.wait_ge(x1_a.sem, x1_a.at(i, "e1"))
                            nc.vector.reciprocal(srz, sz).then_inc(x2_v.sem, 1)
                            dve.wait_ge(x2_v.sem, x2_v.at(i, "rz"))
                            nc.vector.tensor_tensor(pn, sc, srz[:, :, None].to_broadcast([P, C, P]), ALU.mult)\
                                .then_inc(x2_v.sem, 1)
                        if A and valid(k - 3):
                            i = k - 3
                            if g == 0:
                                dve.wait_ge(out_v.sem, out_v.at(i, "x"))
                                settled(dve)
                                nc.vector.bn_stats(stat[:, 1, :], x_all[:, i]).then_inc(n2_v.sem, 1)
                                dve.wait_ge(n2_v.sem, n2_v.at(i, "stats"))
                                settled(dve)
                                nc.vector.bn_aggr(mv[:, 1, :], stat[:, 1, :]).then_inc(n2_v.sem, 1)
                            if g == 1:
                                dve.wait_ge(n2_g.sem, n2_g.at(i, "rstd"))
                                nc.vector.tensor_scalar(xo, x_all[:, i], mv[:, 1, 0:1], rstd[:, 1, 1:2],
                                                        ALU.subtract, ALU.mult).then_inc(n2_v.sem, 1)
                                dve.wait_ge(n2_v.sem, n2_v.at(i, "xo"))
                                nc.vector.scalar_tensor_tensor(out=x_all[:, i], in0=xo, scalar=tg[:, 2:3],
                                                               in1=x_all[:, i], op0=ALU.mult, op1=ALU.add)\
                                    .then_inc(n2_v.sem, 1)
                                nc.vector.bn_stats(stat[:, 2, :], xo).then_inc(n2_v.sem, 1)
                                dve.wait_ge(n2_v.sem, n2_v.at(i, "stats3"))
                                settled(dve)
                                nc.vector.bn_aggr(mv[:, 2, :], stat[:, 2, :]).then_inc(n2_v.sem, 1)
                            if g == 3:
                                dve.wait_ge(n2_g.sem, n2_g.at(i, "rstd3"))
                                before(dve, n2_g.sem, n2_g.at(i - 1, "gamma"))
                                nc.vector.tensor_scalar(xh3, xo, mv[:, 2, 0:1], rstd[:, 2, 1:2],
                                                        ALU.subtract, ALU.mult).then_inc(n2_v.sem, 1)
                        if not A and valid(k - 3):
                            i = k - 3
                            if g == 0:
                                dve.wait_ge(out_v.sem, out_v.at(i, "x"))
                                settled(dve)
                                nc.vector.bn_stats(stat[:, 1, :], x_all[:, i]).then_inc(n4_v.sem, 1)
                                dve.wait_ge(n4_v.sem, n4_v.at(i, "stats"))
                                settled(dve)
                                nc.vector.bn_aggr(mv[:, 1, :], stat[:, 1, :]).then_inc(n4_v.sem, 1)
                            if g == 2:
                                dve.wait_ge(n4_g.sem, n4_g.at(i, "rstd"))
                                before(dve, x1_p.sem, x1_p.at(i - 1, "xT"))
                                nc.vector.tensor_scalar(xc, x_all[:, i], mv[:, 1, 0:1], rstd[:, 1, 1:2],
                                                        ALU.subtract, ALU.mult).then_inc(n4_v.sem, 1)
                        if valid(k + 2):
                            i = k + 2
                            if g == 1:
                                if A:
                                    dve.wait_ge(ld_x[u], dma_at(i, u))
                                settled(dve)
                                nc.vector.bn_stats(stat[:, 0, :], x_all[:, i]).then_inc(ln_v.sem, 1)
                                dve.wait_ge(ln_v.sem, ln_v.at(i, "stats"))
                                settled(dve)
                                nc.vector.bn_aggr(mv[:, 0, :], stat[:, 0, :]).then_inc(ln_v.sem, 1)
                            if g == 2:
                                dve.wait_ge(ln_g.sem, ln_g.at(i, "rstd"))
                                before(dve, pre_p.sem, pre_p.at(k, "xT"))
                                nc.vector.tensor_scalar(xh[:, u, :], x_all[:, i], mv[:, 0, 0:1], rstd[:, 0, 1:2],
                                                        ALU.subtract, ALU.mult).then_inc(ln_v.sem, 1)
                        if A and g == 1 and valid(k - 4):
                            i = k - 4
                            dve.wait_ge(rt_p.sem, rt_p.at(i, "lg"))
                            nc.vector.tensor_tensor(lg, ps[7][:, 0:E0], bg_sb[:, :], ALU.add).then_inc(rt_v.sem, 1)
                            dve.wait_ge(rt_v.sem, rt_v.at(i, "lg"))
                            settled(dve)
                            nc.vector.max(top8[:, :], lg).then_inc(rt_v.sem, 1)
                            dve.wait_ge(rt_v.sem, rt_v.at(i, "top"))
                            settled(dve)
                            nc.vector.max_index(idx8[:, :], top8[:, :], lg).then_inc(rt_v.sem, 1)
                            nc.vector.tensor_copy(top_val[:, i, :], top8[:, :]).then_inc(rt_v.sem, 1)
                            dve.wait_ge(rt_v.sem, rt_v.at(i, "idx"))
                            nc.vector.tensor_copy(top_idx[:, i, :], idx8[:, 0:2]).then_inc(rt_v.sem, 1)
                        if not A and g == 1 and valid(k - 4):
                            i = k - 4
                            dve.wait_ge(x1_p.sem, x1_p.at(i, "s"))
                            before(dve, x2_v.sem, x2_v.at(k - 5, "pn"))
                            for c in range(C):
                                nc.vector.tensor_scalar(sc[:, c, :], ps[7][:, D + c * P:D + (c + 1) * P],
                                                        qac[:, c:c + 1], None, ALU.add, ALU.max,
                                                        accum_out=smx[:, c:c + 1]).then_inc(x1_v.sem, 1)
                            dve.wait_ge(x1_v.sem, x1_v.at(i, "s1"))
                            nc.vector.tensor_scalar(snx, smx, -1.0, None, ALU.mult).then_inc(x1_v.sem, 1)
                        if not A and g == 2 and valid(k - 4):
                            i = k - 4
                            dve.wait_ge(x1_p.sem, x1_p.at(i, "V"))
                            nc.vector.tensor_tensor(dVb[:, u, :], ps[5][:, D:2 * D], row["dbv"], ALU.add)\
                                .then_inc(x1_v.sem, 1)
                        if not A and g == 3 and valid(k - 5):
                            i = k - 5
                            dve.wait_ge(x2_p.sem, x2_p.at(i, "av"))
                            before(dve, pre_p.sem, pre_p.at(k + 1, "V"))
                            nc.vector.tensor_tensor(mk, ps[5][:, D:2 * D].rearrange("p (c h s) -> p c h s", c=C, h=HC),
                                                    cv["mask8"][:, None, :, None].to_broadcast([P, C, HC, NS]),
                                                    ALU.mult).then_inc(x2_v.sem, 1)
                            dve.wait_ge(x2_v.sem, x2_v.at(i, "mask"))
                            nc.vector.tensor_reduce(oT_all[:, :, :, i], mk.rearrange("p c h s -> p c s h"), AX, ALU.add)\
                                .then_inc(x2_v.sem, 1)
                        if g == 3 and valid(k - 2):
                            i = k - 2
                            dve.wait_ge(out_p.sem, out_p.at(i, "O"))
                            if A:
                                nc.vector.tensor_tensor(tmp, ps[7][:, D:2 * D], row["bo0"], ALU.add)\
                                    .then_inc(out_v.sem, 1)
                            else:
                                nc.vector.tensor_copy(tmp, ps[7][:, D:2 * D]).then_inc(out_v.sem, 1)
                            dve.wait_ge(out_v.sem, out_v.at(i, "t"))
                            nc.vector.scalar_tensor_tensor(out=x_all[:, i], in0=tmp, scalar=tg[:, L:L + 1],
                                                           in1=x_all[:, i], op0=ALU.mult, op1=ALU.add)\
                                .then_inc(out_v.sem, 1)
                        if g == 3 and valid(k + 1):
                            i, o = k + 1, 1 - u
                            dve.wait_ge(pre_p.sem, pre_p.at(i, "V"))
                            before(dve, pv_p.sem, pv_p.at(k - 1, "3"))
                            if not A:
                                before(dve, x2_p.sem, x2_p.at(k - 5, "av"))
                            src = ps[5][:, 0:D].rearrange("p (h d) -> p h d", h=H)
                            if A:
                                nc.vector.tensor_tensor(vaug[:, o, :, 0:DH], src,
                                                        row["bv0"].rearrange("p (h d) -> p h d", h=H), ALU.add)\
                                    .then_inc(v_v.sem, 1)
                            else:
                                nc.vector.tensor_copy(vaug[:, o, :, 0:DH], src).then_inc(v_v.sem, 1)
                pipeline(dve, body, last=last_k, steady=steady)

            def gpsimd(pool):
                def rsqrt(t, j, i, vname, rname):
                    nc.gpsimd.tensor_tensor(rstd[:, j, 0:1], mv[:, j, 1:2], eps_sb[:, :], ALU.add).then_inc(t.sem, 1)
                    pool.wait_ge(t.sem, t.at(i, vname))
                    nc.gpsimd.tensor_tensor(rstd[:, j, 1:2], rstd[:, j, 0:1], mhalf[:, :], ALU.pow).then_inc(t.sem, 1)

                def gather(i, u):
                    before(pool, mix_v.sem, mix_v.at(i - 2, "y1"))
                    nc.gpsimd.tensor_copy(idx_cur[:, u, :], slot_i[:, :, i]).then_inc(gidx_g.sem, 1)
                    pool.wait_ge(gidx_g.sem, gidx_g.at(i, "idx"))
                    settled(pool)
                    for c in range(2):
                        nc.gpsimd.indirect_dma_start(out=yg[:, u, c, :], out_offset=None, in_=ys_dram[:, :],
                                                     in_offset=bass.IndirectOffsetOnAxis(ap=idx_cur[:, u, c:c + 1].bitcast(U32), axis=0))\
                            .then_inc(ld_y[u], 16)

                def body(k, u):
                    if A and valid(k - 3):
                        i = k - 3
                        pool.wait_ge(n2_v.sem, n2_v.at(i, "mean"))
                        rsqrt(n2_g, 1, i, "var", "rstd")
                    if not A and valid(k):
                        sub(k, u, 0)
                    if not A and valid(k + 3) and (not isinstance(k, int) or k >= -1):
                        gather(k + 3, 1 - u)
                    if not A and valid(k - 3):
                        pool.wait_ge(n4_v.sem, n4_v.at(k - 3, "mean"))
                        rsqrt(n4_g, 1, k - 3, "var", "rstd")
                    if A and valid(k + 1):
                        kblock(k + 1, 1 - u, 0)
                    if A and valid(k - 3):
                        i = k - 3
                        pool.wait_ge(n2_v.sem, n2_v.at(i, "mean3"))
                        rsqrt(n2_g, 2, i, "var3", "rstd3")
                    if not A and valid(k):
                        sub(k, u, 1)
                    if valid(k + 2):
                        i = k + 2
                        pool.wait_ge(ln_v.sem, ln_v.at(i, "mean"))
                        rsqrt(ln_g, 0, i, "var", "rstd")
                    if not A and valid(k + 1):
                        kblock(k + 1, 1 - u, 0)
                    if not A and valid(k):
                        sub(k, u, 2)
                    if valid(k + 1):
                        kblock(k + 1, 1 - u, 1)
                    if not A and valid(k):
                        sub(k, u, 3)
                    if A and valid(k - 3):
                        i = k - 3
                        pool.wait_ge(n2_v.sem, n2_v.at(i, "xh3"))
                        nc.gpsimd.tensor_tensor(xg, xh3, row["gamma"], ALU.mult).then_inc(n2_g.sem, 1)
                        pool.wait_ge(n2_g.sem, n2_g.at(i, "gamma"))
                        before(pool, rt_p.sem, rt_p.at(i - 1, "xnT"))
                        before(pool, keep_a.sem, keep_a.at(i - 1, "x"))
                        nc.gpsimd.tensor_tensor(xc, xg, row["beta"], ALU.add).then_inc(n2_g.sem, 1)

                def sub(k, u, g):
                    pool.wait_ge(sc_v.sem, sc_v.at(k, f"m{g}"))
                    before(pool, tr_p.sem, tr_p.at(k - 2, str(g)))
                    nc.gpsimd.tensor_tensor(pr[:, u, g, :].rearrange("p (h t) -> p h t", h=G),
                                            sbias[:, g % 2, :].rearrange("p (h t) -> p h t", h=G),
                                            mx[:, g % 2, :, None].to_broadcast([P, G, P]), ALU.subtract)\
                        .then_inc(sub_g.sem, 1)

                def kblock(i, u, c):
                    pool.wait_ge(pre_a.sem, pre_a.at(i, "K"))
                    before(pool, sc_p.sem, sc_p.at(i - 2, str(2 * c + 1)))
                    nc.gpsimd.tensor_tensor(kbd[:, C * u + c], kT[:, c, None, :].to_broadcast([P, HC, P]),
                                            cv["mask8"][:, :, None].to_broadcast([P, HC, P]), ALU.mult)\
                        .then_inc(kb_g.sem, 1)

                if not A:
                    gather(0, 0)
                    gather(1, 1)
                pipeline(pool, body, last=last_k, steady=(4 if A else 6, B - 2 if A else B - 4))

            return sync, tensor, scalar, vector, gpsimd

        ld_ring = [sem(f"ld_ring{i}") for i in range(RING)]
        ld_ring_sw = [sem(f"ld_ring_sw{i}") for i in range(RING)]
        ld_rows = sem("ld_rows")
        route_v, route_p, route_a = sem("route_v"), sem("route_p"), sem("route_a")
        dn_p = track("m0_dn_p", "y", UNITS, base=1)

        def routing():
            def sync(sp):
                sp.dma_start(b1_sb.rearrange("p e f -> p (e f)"), a["b1"].partition_broadcast(P)).then_inc(ld_rows, 16)
                sp.dma_start(b2_sb.rearrange("p e f -> p (e f)"), a["b2"].partition_broadcast(P)).then_inc(ld_rows, 16)

            def vector(dve):
                n = [0]

                def link(ins):
                    n[0] += 1
                    ins.then_inc(route_v, 1)
                    dve.wait_ge(route_v, n[0])

                def be(v):
                    return v[:, :, None].to_broadcast([P, B, E0])

                tt = nc.vector.tensor_tensor
                link(nc.vector.tensor_copy(idxf, top_idx[:, :, :]))
                for c in range(2):
                    link(tt(oh[:, c], idxf[:, :, c:c + 1].to_broadcast([P, B, E0]),
                            cv["iota8"][:, None, :].to_broadcast([P, B, E0]), ALU.is_equal))
                link(tt(msk, oh[:, 0], oh[:, 1], ALU.add))
                link(tt(ex, top_val[:, :, :], be(top_val[:, :, 0]), ALU.subtract))
                mask_ready = n[0]
                dve.wait_ge(route_a, 1)
                link(nc.vector.tensor_reduce(zs, ex, AX, ALU.add))
                link(tt(s2, ex[:, :, 0], ex[:, :, 1], ALU.add))
                link(nc.vector.scalar_tensor_tensor(out=den, in0=zs, scalar=1e-8, in1=s2, op0=ALU.mult, op1=ALU.add))
                link(nc.vector.reciprocal(rr, den))
                link(nc.vector.tensor_scalar(rr, rr, tg[:, 2:3], None, ALU.mult))
                for c in range(2):
                    link(tt(wts[:, c, :], ex[:, :, c], rr, ALU.mult))
                dve.wait_ge(route_p, 2)
                link(nc.vector.tensor_copy(tot.rearrange("p b e -> p (b e)"), ps[1][:, 0:B * E0]))
                for e in range(E0):
                    link(nc.vector.tensor_tensor_scan(inc[:, :, e], ones[:, 0:B], tot[:, :, e], 0.0, ALU.mult, ALU.add))
                link(tt(blk, inc[:, B - 1, :, None].to_broadcast([P, E0, B]),
                        cv["thr"][:, None, :].to_broadcast([P, E0, B]), ALU.is_gt))
                link(nc.vector.tensor_reduce(nblk, blk, AX, ALU.add))
                link(nc.vector.tensor_tensor_scan(cend, ones[:, 0:E0], nblk, 0.0, ALU.mult, ALU.add))
                link(tt(basev, cend, nblk, ALU.subtract))
                link(nc.vector.tensor_scalar(basev, basev, float(P), None, ALU.mult))
                link(nc.vector.tensor_scalar(cend_i[:, :], cend[0:1, :], float(dn_p.base), None, ALU.add))
                link(tt(pos, inc, tot, ALU.subtract))
                link(tt(pos, ps[0][:, 0:B * E0].rearrange("p (b e) -> p b e", e=E0), pos, ALU.add))
                link(tt(pos, pos, basev[:, None, :].to_broadcast([P, B, E0]), ALU.add))
                for c in range(2):
                    link(tt(ohp, oh[:, c], pos, ALU.mult))
                    link(nc.vector.tensor_reduce(posf[:, c, :], ohp, AX, ALU.add))
                link(nc.vector.tensor_copy(slot_i[:, :, :], posf))
                link(tt(ucmp, cv["iotau"][:, :, None].to_broadcast([P, UNITS, E0]),
                        cend[:, None, :].to_broadcast([P, UNITS, E0]), ALU.is_ge))
                link(nc.vector.tensor_reduce(uexp, ucmp, AX, ALU.add))
                link(nc.vector.tensor_scalar(uexp, uexp, float(E0 - 1), None, ALU.min))
                link(nc.vector.tensor_copy(unit_e[:, :], uexp[0:1, :]))
                link(nc.vector.tensor_scalar(urng, uexp, float(RING), None, ALU.is_ge))
                link(nc.vector.tensor_scalar(urng2, uexp, float(2 * RING), None, ALU.is_ge))
                link(tt(urng, urng, urng2, ALU.add))
                link(nc.vector.scalar_tensor_tensor(out=urng, in0=urng, scalar=-float(RING), in1=uexp,
                                                    op0=ALU.mult, op1=ALU.add))
                link(nc.vector.tensor_copy(unit_r[:, :], urng[0:1, :]))
                nc.vector.tensor_copy(zs, rr).then_inc(route_done, 1)

            def tensor(pe):
                pe.wait_ge(route_v, 4)
                m = msk.rearrange("p b e -> p (b e)")
                nc.tensor.matmul(ps[0][:, 0:B * E0], cv["tri"], m, start=True, stop=True).then_inc(route_p, 1)
                nc.tensor.matmul(ps[1][:, 0:B * E0], ones[:, :], m, start=True, stop=True).then_inc(route_p, 1)

            def scalar(act):
                act.wait_ge(route_v, 5)
                nc.scalar.activation(ex.rearrange("p b e -> p (b e)"), ex.rearrange("p b e -> p (b e)"), ACT.Exp)\
                    .then_inc(route_a, 1)

            def gpsimd(pool):
                pool.sem_inc(dn_p.sem, dn_p.base)
                pool.wait_ge(route_done, 1)
                pool.wait_ge(zeroed, 16)
                for c in range(2):
                    for b in range(B):
                        nc.gpsimd.indirect_dma_start(
                            out=xs_dram[:, :], out_offset=bass.IndirectOffsetOnAxis(ap=slot_i[:, c, b:b + 1].bitcast(U32), axis=0),
                            in_=xn_all[:, b, :], in_offset=None).then_inc(scattered, 16)
                pool.wait_ge(scattered, 16 * 2 * B)
            return sync, tensor, scalar, vector, gpsimd

        route_done = sem("route_done")

        def moe0():
            ld_xs = [sem("ld_xs0"), sem("ld_xs1")]
            st_ys = [sem("st_ys0"), sem("st_ys1")]
            ring_ready = sem("ring_ready")
            x_p = track("m0_x_p", "x", UNITS)
            up_p = track("m0_up_p", "h0 h1", UNITS)
            tp_p = track("m0_tp_p", "a b", UNITS)
            x_a = track("m0_x_a", "x", UNITS)
            ge_a = track("m0_ge_a", "h0 h1", UNITS)
            tp_a = track("m0_tp_a", "a", UNITS)
            b1_v = track("m0_b1_v", "h0 h1", UNITS)
            tp_v = track("m0_tp_v", "b", UNITS)
            y_v = track("m0_y_v", "y", UNITS)
            up_banks = [(1, 2), (6, 7)]
            FC = F0 // P

            def ok(i):
                return not isinstance(i, int) or 0 <= i < UNITS

            def units(eng, body, first=-1, last=UNITS + 1, steady=(2, UNITS - 2)):
                pipeline(eng, body, first, last, steady)

            def sync(sp):
                for u in range(2):
                    sp.dma_start(xs[:, u, :], xs_dram[u * P:(u + 1) * P, :]).then_inc(ld_xs[u], 16)

                def body(j, u):
                    if ok(j + 2) and (not isinstance(j, int) or j >= 0):
                        before(sp, x_p.sem, x_p.at(j, "x"))
                        sp.dma_start(xs[:, u, :], xs_dram[bass.ds((j + 2) * P, P), :]).then_inc(ld_xs[u], 16)
                    if ok(j - 1):
                        sp.wait_ge(y_v.sem, y_v.at(j - 1, "y"))
                        sp.dma_start(ys_dram[bass.ds((j - 1) * P, P), :], yb[:, 1 - u, :]).then_inc(st_ys[1 - u], 16)
                units(sp, body)
                for u in range(2):
                    sp.wait_ge(st_ys[u], 8 * UNITS)

            def gpsimd(pool):
                for e in range(E0):
                    if e >= RING:
                        units_done = pool.value_load(cend_i[0:1, e - RING:e - RING + 1], min_val=1, max_val=UNITS + 1)
                        pool.wait_ge(dn_p.sem, units_done)
                        settled(pool)
                        pool.dma_start(ring[:, e % RING, :], a["w12"][e]).then_inc(ld_ring_sw[e % RING], 16)
                        pool.wait_ge(ld_ring_sw[e % RING], 16 * (e // RING))
                    else:
                        pool.wait_ge(ld_ring[e], 16)
                    pool.sem_inc(ring_ready, 1)

            def tensor(pe):
                def body(j, u):
                    if ok(j):
                        e = pe.value_load(unit_e[0:1, bass.ds(j, 1)], min_val=0, max_val=E0 - 1)
                        r = pe.value_load(unit_r[0:1, bass.ds(j, 1)], min_val=0, max_val=RING - 1)
                        pe.wait_ge(x_a.sem, x_a.at(j, "x"))
                        pe.wait_ge(ring_ready, e + 1)
                        for h in range(2):
                            before(pe, b1_v.sem, b1_v.at(j - 2, f"h{h}"))
                            for c in range(C):
                                last = nc.tensor.matmul(ps[up_banks[u][h]][:, :], xsT[:, u, c, :],
                                                        ring[:, bass.ds(r, 1), c * F0 + h * 512:c * F0 + (h + 1) * 512],
                                                        start=c == 0, stop=c == C - 1)
                            last.then_inc(up_p.sem, 1)
                    if ok(j - 1):
                        for q, bank in ((0, 3), (1, 4)):
                            pe.wait_ge(ge_a.sem, ge_a.at(j - 1, f"h{q}"))
                            if q == 0:
                                before(pe, tp_a.sem, tp_a.at(j - 2, "a"))
                            else:
                                before(pe, tp_v.sem, tp_v.at(j - 2, "b"))
                            for f in range(4):
                                last = nc.tensor.transpose(ps[bank][:, f * P:(f + 1) * P],
                                                           hid[:, 1 - u, (4 * q + f) * P:(4 * q + f + 1) * P], cv["ident"])
                            last.then_inc(tp_p.sem, 1)
                    if ok(j + 1):
                        pe.wait_ge(ld_xs[1 - u], dma_at(j + 1, 1 - u))
                        before(pe, x_a.sem, x_a.at(j, "x"))
                        for c in range(C):
                            last = nc.tensor.transpose(ps[0][:, c * P:(c + 1) * P], xs[:, 1 - u, c * P:(c + 1) * P],
                                                       cv["ident"])
                        last.then_inc(x_p.sem, 1)
                    if ok(j - 1):
                        r = pe.value_load(unit_r[0:1, bass.ds(j - 1, 1)], min_val=0, max_val=RING - 1)
                        before(pe, y_v.sem, y_v.at(j - 2, "y"))
                        for f in range(FC):
                            if f == 0:
                                pe.wait_ge(tp_a.sem, tp_a.at(j - 1, "a"))
                            if f == FC // 2:
                                pe.wait_ge(tp_v.sem, tp_v.at(j - 1, "b"))
                            o = C * F0 + f * D
                            last = nc.tensor.matmul(ps[5][:, 0:D], hidT[:, 1 - u, f, :], ring[:, bass.ds(r, 1), o:o + D],
                                                    start=f == 0, stop=f == FC - 1)
                        last.then_inc(dn_p.sem, 1)
                units(pe, body)

            def scalar(act):
                def body(j, u):
                    if ok(j - 1):
                        act.wait_ge(tp_p.sem, tp_p.at(j - 1, "a"))
                        before(act, dn_p.sem, dn_p.at(j - 3, "y"))
                        nc.scalar.copy(hidT[:, 1 - u, 0:4, :], ps[3][:, :]).then_inc(tp_a.sem, 1)
                    if ok(j + 1):
                        act.wait_ge(x_p.sem, x_p.at(j + 1, "x"))
                        before(act, up_p.sem, up_p.at(j - 1, "h1"))
                        nc.scalar.copy(xsT[:, 1 - u, :, :], ps[0][:, 0:D]).then_inc(x_a.sem, 1)
                    if ok(j):
                        for h in range(2):
                            act.wait_ge(b1_v.sem, b1_v.at(j, f"h{h}"))
                            v = hid[:, u, h * 512:(h + 1) * 512]
                            nc.scalar.activation(v, v, ACT.Gelu).then_inc(ge_a.sem, 1)
                units(act, body)

            def vector(dve):
                dve.wait_ge(ld_rows, 32)

                def body(j, u):
                    if ok(j):
                        e = dve.value_load(unit_e[0:1, bass.ds(j, 1)], min_val=0, max_val=E0 - 1)
                        for h in range(2):
                            dve.wait_ge(up_p.sem, up_p.at(j, f"h{h}"))
                            before(dve, tp_p.sem, tp_p.at(j - 2, "ab"[h]))
                            nc.vector.tensor_tensor(hid[:, u, h * 512:(h + 1) * 512], ps[up_banks[u][h]][:, :],
                                                    b1_sb[:, bass.ds(e, 1), h * 512:(h + 1) * 512].rearrange("p o f -> p (o f)"),
                                                    ALU.add).then_inc(b1_v.sem, 1)
                    if ok(j - 1):
                        dve.wait_ge(tp_p.sem, tp_p.at(j - 1, "b"))
                        before(dve, dn_p.sem, dn_p.at(j - 3, "y"))
                        nc.vector.tensor_copy(hidT[:, 1 - u, 4:8, :].rearrange("p f t -> p (f t)"), ps[4][:, :])\
                            .then_inc(tp_v.sem, 1)
                        e = dve.value_load(unit_e[0:1, bass.ds(j - 1, 1)], min_val=0, max_val=E0 - 1)
                        dve.wait_ge(dn_p.sem, dn_p.at(j - 1, "y"))
                        before(dve, st_ys[1 - u], dma_at(j - 3, 1 - u) if not isinstance(j, int) or j >= 3 else 0)
                        nc.vector.tensor_tensor(yb[:, 1 - u, :], ps[5][:, 0:D],
                                                b2_sb[:, bass.ds(e, 1), :].rearrange("p o f -> p (o f)"), ALU.add)\
                            .then_inc(y_v.sem, 1)
                units(dve, body)
            return sync, tensor, scalar, vector, gpsimd

        ld_prep, ld_set, ld_slots = sem("ld_prep"), [sem(f"ld_set{i}") for i in range(SETS)], sem("ld_slots")
        prep_p, prep_v = sem("prep_p"), sem("prep_v")

        def prepare():
            def sync(sp):
                for n, name in enumerate(("dq", "dkT")):
                    sp.dma_start(prep_w[:, n].rearrange("p c d -> p (c d)"), a[name]).then_inc(ld_prep, 16)
                sp.dma_start(slotT, a["slotT"].rearrange("p (c s) -> p c s", c=C)).then_inc(ld_prep, 16)
                for n in range(SETS):
                    sp.dma_start(wset[:, n].rearrange("p e f -> p (e f)"), a["wset"][n]).then_inc(ld_set[n], 16)

            def tensor(pe):
                pe.wait_ge(ld_prep, 48)
                for m in range(C):
                    for c in range(C):
                        last = nc.tensor.matmul(ps[0][:, m * NS:(m + 1) * NS], prep_w[:, 0, c, m * P:(m + 1) * P],
                                                slotT[:, c, :], start=c == 0, stop=c == C - 1)
                last.then_inc(prep_p, 1)
                pe.wait_ge(prep_v, 3)
                for c in range(C):
                    for m in range(C):
                        last = nc.tensor.matmul(ps[1][:, c * D + m * P:c * D + (m + 1) * P],
                                                prep_w[:, 1, m, c * P:(c + 1) * P],
                                                qbd[:, m, :, :].rearrange("p h s -> p (h s)"), start=True, stop=True)
                last.then_inc(prep_p, 1)
                for m in range(C):
                    last = nc.tensor.matmul(ps[2][:, m:m + 1], qbd[:, m, :, :].rearrange("p h s -> p (h s)"),
                                            col["dbk"][:, m:m + 1], start=True, stop=True)
                last.then_inc(prep_p, 1)

            def vector(dve):
                nc.vector.memset(vaug[:, :, :, DH], 1.0)
                dve.wait_ge(prep_p, 1)
                for m in range(C):
                    nc.vector.tensor_scalar(sqT[:, m, :], ps[0][:, m * NS:(m + 1) * NS], QSCALE, qcol[:, 1, m:m + 1],
                                            ALU.mult, ALU.add).then_inc(prep_v, 1)
                dve.wait_ge(prep_v, 2)
                nc.vector.tensor_tensor(qbd, sqT[:, :, None, :].to_broadcast([P, C, HC, NS]),
                                        cv["mask8"][:, None, :, None].to_broadcast([P, C, HC, NS]), ALU.mult)\
                    .then_inc(prep_v, 1)
                dve.wait_ge(prep_p, 3)
                nc.vector.tensor_copy(qa.rearrange("p c d -> p (c d)"), ps[1][:, :])
                nc.vector.tensor_copy(qac, ps[2][:, 0:C])
            return sync, tensor, None, vector, None

        def moe1():
            e_p, e_a, e_v, e_g = sem("m1_p"), sem("m1_a"), sem("m1_v"), sem("m1_g")
            set_used = sem("m1_set_used")
            T = E1 // 4
            FC = F1 // P
            pj = Track(e_p, ["o", "gb", "hT"], T)
            va = Track(e_v, ["o", "stats", "mean", "hat", "gain", "h"], T)
            aj = Track(e_a, ["hT"], T)
            gj = Track(e_g, ["var", "rstd"], T)
            pe2 = track("m1_p2", "u g ta tb y o2", T)
            ac2 = track("m1_a2", "u0 u1 g0 g1 ta o2", T)
            ve2 = track("m1_v2", "m0 m1 tb y", T)
            k_p, k_a = sem("m1_k_p"), sem("m1_k_a")

            def sync(sp):
                sp.dma_start(sel[0:E1].rearrange("p t r -> p (t r)"), a["sel"]).then_inc(ld_slots, 16)
                sp.dma_start(small[0:E1].rearrange("p n d -> p (n d)"), a["small"]).then_inc(ld_slots, 16)
                sp.dma_start(bias1[0:E1].rearrange("p n f -> p (n f)"), a["bias1"]).then_inc(ld_slots, 16)
                for n in range(SETS, 6 * T):
                    sp.wait_ge(set_used, n - SETS + 1)
                    sp.dma_start(wset[:, n % SETS].rearrange("p e f -> p (e f)"), a["wset"][n])\
                        .then_inc(ld_set[n % SETS], 16)

            def tensor(pe):
                pe.wait_ge(ld_slots, 48)
                for t in range(T):
                    before(pe, va.sem, va.at(t - 1, "o"))
                    nc.tensor.matmul(ps[0][:, 0:D], sel[0:E1, t, :], small[0:E1, 0, :], start=True, stop=False)
                    for m in range(C):
                        last = nc.tensor.matmul(ps[0][:, 0:D], oT_all[:, m, 4 * t:4 * t + 4, :], w["do"][:, m, :],
                                                start=False, stop=m == C - 1)
                    last.then_inc(e_p, 1)
                    before(pe, va.sem, va.at(t - 1, "h"))
                    for n in range(2):
                        last = nc.tensor.matmul(ps[2][:, n * D:(n + 1) * D], sel[0:E1, t, :], small[0:E1, 1 + n, :],
                                                start=True, stop=True)
                    last.then_inc(e_p, 1)
                    pe.wait_ge(va.sem, va.at(t, "h"))
                    before(pe, aj.sem, aj.at(t - 1, "hT"))
                    for c in range(C):
                        last = nc.tensor.transpose(ps[3][:, c * P:(c + 1) * P], hrow[:, c * P:(c + 1) * P], cv["ident"])
                    last.then_inc(e_p, 1)
                pe.wait_ge(aj.sem, aj.at(T - 1, "hT"))
                n = 0
                for t in range(T):
                    for mat, banks in ((0, (4, 5)), (1, (6, 7))):
                        for h in range(2):
                            before(pe, ac2.sem, ac2.at(t - 1, f"{'ug'[mat]}{h}"))
                            nc.tensor.matmul(ps[banks[h]][:, :], sel[0:E1, t, :], bias1[0:E1, mat, h * 512:(h + 1) * 512],
                                             start=True, stop=False, skip_group_check=True)
                        for c in range(C):
                            pe.wait_ge(ld_set[n % SETS], 16 * (n // SETS + 1))
                            for h in range(2):
                                for e in range(4):
                                    last = nc.tensor.matmul(ps[banks[h]][32 * e:32 * e + 32, :],
                                                            hT[:, c, t, 32 * e:32 * e + 32],
                                                            wset[:, n % SETS, e, h * 512:(h + 1) * 512],
                                                            start=False, stop=c == C - 1, skip_group_check=True)
                            if c == C - 1:
                                last.then_inc(pe2.sem, 1)
                                pe.wait_ge(pe2.sem, pe2.at(t, "ug"[mat]))
                                pe.sem_inc(set_used, 1)
                            else:
                                last.then_inc(set_used, 1)
                            n += 1
                    for q in range(2):
                        pe.wait_ge(ve2.sem, ve2.at(t, f"m{q}"))
                        if q == 0:
                            before(pe, ac2.sem, ac2.at(t - 1, "ta"))
                        else:
                            before(pe, ve2.sem, ve2.at(t - 1, "tb"))
                        for f in range(4):
                            last = nc.tensor.transpose(ps[2 + q][:, f * P:(f + 1) * P],
                                                       us[:, (4 * q + f) * P:(4 * q + f + 1) * P], cv["ident"])
                        last.then_inc(pe2.sem, 1)
                    before(pe, ve2.sem, ve2.at(t - 1, "y"))
                    nc.tensor.matmul(ps[1][:, 0:D], sel[0:E1, t, :], small[0:E1, 3, :],
                                     start=True, stop=False, skip_group_check=True)
                    for q in range(2):
                        pe.wait_ge(ac2.sem, ac2.at(t, "ta"))
                        if q == 1:
                            pe.wait_ge(ve2.sem, ve2.at(t, "tb"))
                        pe.wait_ge(ld_set[n % SETS], 16 * (n // SETS + 1))
                        for f in range(4):
                            for e in range(4):
                                last = nc.tensor.matmul(ps[1][32 * e:32 * e + 32, 0:D],
                                                        ugT[:, 4 * q + f, 32 * e:32 * e + 32],
                                                        wset[:, n % SETS, e, f * D:(f + 1) * D],
                                                        start=False, stop=q == 1 and f == 3, skip_group_check=True)
                        if q == 1:
                            last.then_inc(pe2.sem, 1)
                            pe.wait_ge(pe2.sem, pe2.at(t, "y"))
                            pe.sem_inc(set_used, 1)
                        else:
                            last.then_inc(set_used, 1)
                        n += 1
                    pe.wait_ge(ve2.sem, ve2.at(t, "y"))
                    before(pe, ac2.sem, ac2.at(t - 1, "o2"))
                    for c in range(C):
                        last = nc.tensor.transpose(ps[0][:, c * P:(c + 1) * P], orow[:, t, c * P:(c + 1) * P], cv["ident"])
                    last.then_inc(pe2.sem, 1)
                pe.wait_ge(ac2.sem, ac2.at(T - 1, "o2"))
                for m in range(C):
                    for c in range(C):
                        last = nc.tensor.matmul(ps[6 + m][:, :], w["ck"][:, c, m * P:(m + 1) * P],
                                                oT2[:, c, :, :].rearrange("p s b -> p (s b)"),
                                                start=c == 0, stop=c == C - 1)
                    last.then_inc(k_p, 1)

            def scalar(act):
                for t in range(T):
                    act.wait_ge(pj.sem, pj.at(t, "hT"))
                    nc.scalar.copy(hT[:, :, t, :], ps[3][:, 0:D].rearrange("p (c r) -> p c r", c=C)).then_inc(e_a, 1)
                for t in range(T):
                    for mat, banks, dst in ((0, (4, 5), us), (1, (6, 7), gs)):
                        act.wait_ge(pe2.sem, pe2.at(t, "ug"[mat]))
                        if mat == 0:
                            before(act, pe2.sem, pe2.at(t - 1, "tb"))
                        for h in range(2):
                            nc.scalar.activation(dst[:, h * 512:(h + 1) * 512], ps[banks[h]][:, :], ACT.Silu)\
                                .then_inc(ac2.sem, 1)
                    act.wait_ge(pe2.sem, pe2.at(t, "ta"))
                    before(act, pe2.sem, pe2.at(t - 1, "y"))
                    nc.scalar.copy(ugT[:, 0:4, :].rearrange("p f r -> p (f r)"), ps[2][:, :]).then_inc(ac2.sem, 1)
                    act.wait_ge(pe2.sem, pe2.at(t, "o2"))
                    nc.scalar.copy(oT2[:, :, 4 * t:4 * t + 4, :].rearrange("p c s b -> p c (s b)"),
                                   ps[0][:, 0:D].rearrange("p (c r) -> p c r", c=C)).then_inc(ac2.sem, 1)
                for m in range(C):
                    act.wait_ge(k_p, m + 1)
                    nc.scalar.activation(kTall[:, m, :, :].rearrange("p s b -> p (s b)"), ps[6 + m][:, :], ACT.Identity,
                                         bias=col["cbk"][:, m:m + 1])

            def vector(dve):
                for t in range(T):
                    dve.wait_ge(pj.sem, pj.at(t, "o"))
                    nc.vector.tensor_tensor(orow[:, t, :], ps[0][:, 0:D], row["dbo"], ALU.add).then_inc(e_v, 1)
                    dve.wait_ge(va.sem, va.at(t, "o"))
                    settled(dve)
                    nc.vector.bn_stats(st1, orow[:, t, :]).then_inc(e_v, 1)
                    dve.wait_ge(va.sem, va.at(t, "stats"))
                    settled(dve)
                    nc.vector.bn_aggr(mv1, st1).then_inc(e_v, 1)
                    dve.wait_ge(gj.sem, gj.at(t, "rstd"))
                    before(dve, pj.sem, pj.at(t - 1, "hT"))
                    nc.vector.tensor_scalar(hrow, orow[:, t, :], mv1[:, 0:1], rs1[:, 1:2], ALU.subtract, ALU.mult)\
                        .then_inc(e_v, 1)
                    dve.wait_ge(va.sem, va.at(t, "hat"))
                    dve.wait_ge(pj.sem, pj.at(t, "gb"))
                    nc.vector.tensor_tensor(hrow, ps[2][:, 0:D], hrow, ALU.mult).then_inc(e_v, 1)
                    dve.wait_ge(va.sem, va.at(t, "gain"))
                    nc.vector.tensor_tensor(hrow, ps[2][:, D:2 * D], hrow, ALU.add).then_inc(e_v, 1)
                for t in range(T):
                    for q in range(2):
                        dve.wait_ge(ac2.sem, ac2.at(t, f"g{q}"))
                        v = us[:, q * 512:(q + 1) * 512]
                        nc.vector.tensor_tensor(v, v, gs[:, q * 512:(q + 1) * 512], ALU.mult).then_inc(ve2.sem, 1)
                    dve.wait_ge(pe2.sem, pe2.at(t, "tb"))
                    before(dve, pe2.sem, pe2.at(t - 1, "y"))
                    nc.vector.tensor_copy(ugT[:, 4:8, :].rearrange("p f r -> p (f r)"), ps[3][:, :]).then_inc(ve2.sem, 1)
                    dve.wait_ge(pe2.sem, pe2.at(t, "y"))
                    nc.vector.tensor_tensor(orow[:, t, :], ps[1][:, 0:D], orow[:, t, :], ALU.add).then_inc(ve2.sem, 1)

            def gpsimd(pool):
                for t in range(T):
                    pool.wait_ge(va.sem, va.at(t, "mean"))
                    nc.gpsimd.tensor_tensor(rs1[:, 0:1], mv1[:, 1:2], eps_sb[:, :], ALU.add).then_inc(e_g, 1)
                    pool.wait_ge(gj.sem, gj.at(t, "var"))
                    nc.gpsimd.tensor_tensor(rs1[:, 1:2], rs1[:, 0:1], mhalf[:, :], ALU.pow).then_inc(e_g, 1)
            return sync, tensor, scalar, vector, gpsimd

        def combine():
            n = "c_"
            ld_x3 = [sem(n + "ld_x3_0"), sem(n + "ld_x3_1")]
            st_out = [sem(n + "st_out0"), sem(n + "st_out1")]
            qv_p = track(n + "qv_p", "q v")
            s_p = track(n + "s_p", "s")
            t_p = track(n + "t_p", "pT av")
            o_p = track(n + "o_p", "o")
            q_a = track(n + "q_a", "q")
            t_a = track(n + "t_a", "pT aT")
            e_a = track(n + "e_a", "e")
            p_v = track(n + "p_v", "sum rs pn")
            s_v = track(n + "s_v", "v max sub")
            o_v = track(n + "o_v", "t out")
            k_g = track(n + "k_g", "rep kb")
            v_g = track(n + "v_g", "vbd")
            steady = (2, B - 2)

            def sync(sp):
                for u in range(2):
                    sp.dma_start(x3l[:, u].rearrange("p c t -> p (c t)"), x3T_dram[u]).then_inc(ld_x3[u], 16)

                def body(k, u):
                    if valid(k + 2) and (not isinstance(k, int) or k >= 0):
                        sp.wait_ge(qv_p.sem, qv_p.at(k, "q"))
                        sp.dma_start(x3l[:, u].rearrange("p c t -> p (c t)"), x3T_dram[k + 2]).then_inc(ld_x3[u], 16)
                    if valid(k - 2):
                        sp.wait_ge(o_v.sem, o_v.at(k - 2, "out"))
                        sp.dma_start(out[k - 2], cout[:, u, :]).then_inc(st_out[u], 16)
                pipeline(sp, body, 0, B + 2, steady)
                for s in st_out:
                    sp.wait_ge(s, 8 * B)

            def tensor(pe):
                def body(k, u):
                    if valid(k):
                        pe.wait_ge(ld_x3[u], dma_at(k, u))
                        before(pe, q_a.sem, q_a.at(k - 1, "q"))
                        for m in range(C):
                            for c in range(C):
                                last = nc.tensor.matmul(ps[0][:, m * P:(m + 1) * P], w["cq"][:, c, m * P:(m + 1) * P],
                                                        x3l[:, u, c, :], start=c == 0, stop=c == C - 1)
                        last.then_inc(qv_p.sem, 1)
                        pe.wait_ge(k_g.sem, k_g.at(k, "rep"))
                        before(pe, s_v.sem, s_v.at(k - 1, "v"))
                        for c in range(C):
                            last = nc.tensor.matmul(ps[1][:, 0:D], orep[:, u, c, :, :].rearrange("p h s -> p (h s)"),
                                                    w["cv"][:, c, :], start=c == 0, stop=c == C - 1)
                        last.then_inc(qv_p.sem, 1)
                    if valid(k - 1):
                        pe.wait_ge(p_v.sem, p_v.at(k - 1, "pn"))
                        before(pe, t_a.sem, t_a.at(k - 2, "pT"))
                        for c in range(C):
                            last = nc.tensor.transpose(ps[3][:, c * P:(c + 1) * P], cpn[:, c * P:(c + 1) * P], cv["ident"])
                        last.then_inc(t_p.sem, 1)
                    if valid(k):
                        pe.wait_ge(q_a.sem, q_a.at(k, "q"))
                        pe.wait_ge(k_g.sem, k_g.at(k, "kb"))
                        before(pe, s_v.sem, s_v.at(k - 1, "sub"))
                        for m in range(C):
                            last = nc.tensor.matmul(ps[2][:, m * P:(m + 1) * P], cqT[:, u, m, :],
                                                    ckb[:, u, m, :, :].rearrange("p h s -> p (h s)"), start=True, stop=True)
                        last.then_inc(s_p.sem, 1)
                    if valid(k - 1):
                        pe.wait_ge(t_a.sem, t_a.at(k - 1, "pT"))
                        pe.wait_ge(v_g.sem, v_g.at(k - 1, "vbd"))
                        before(pe, t_a.sem, t_a.at(k - 2, "aT"))
                        for m in range(C):
                            last = nc.tensor.matmul(ps[4][:, m * P:(m + 1) * P], cvbd[:, 1 - u, m, :], cpT[:, m, :],
                                                    start=True, stop=True)
                        last.then_inc(t_p.sem, 1)
                        pe.wait_ge(t_a.sem, t_a.at(k - 1, "aT"))
                        before(pe, o_v.sem, o_v.at(k - 2, "t"))
                        for c in range(C):
                            last = nc.tensor.matmul(ps[5][:, 0:D], caT[:, c, :], w["co"][:, c, :],
                                                    start=c == 0, stop=c == C - 1)
                        last.then_inc(o_p.sem, 1)
                pipeline(pe, body, 0, B + 1, steady)

            def scalar(act):
                def body(k, u):
                    if valid(k):
                        act.wait_ge(qv_p.sem, qv_p.at(k, "q"))
                        before(act, s_p.sem, s_p.at(k - 2, "s"))
                        for c in range(C):
                            last = nc.scalar.activation(cqT[:, u, c, :], ps[0][:, c * P:(c + 1) * P], ACT.Identity,
                                                        bias=qcol[:, 2, c:c + 1], scale=QSCALE)
                        last.then_inc(q_a.sem, 1)
                    if valid(k - 1):
                        act.wait_ge(t_p.sem, t_p.at(k - 1, "pT"))
                        nc.scalar.copy(cpT.rearrange("p c t -> p (c t)"), ps[3][:, 0:D]).then_inc(t_a.sem, 1)
                        act.wait_ge(t_p.sem, t_p.at(k - 1, "av"))
                        before(act, o_p.sem, o_p.at(k - 2, "o"))
                        nc.scalar.copy(caT.rearrange("p c t -> p (c t)"), ps[4][:, 0:D]).then_inc(t_a.sem, 1)
                    if valid(k):
                        act.wait_ge(s_v.sem, s_v.at(k, "sub"))
                        nc.scalar.activation(csc[:, u, :], csc[:, u, :], ACT.Exp).then_inc(e_a.sem, 1)
                pipeline(act, body, 0, B + 1, steady)

            def vector(dve):
                def heads(v):
                    return v.rearrange("p (h s) -> p h s", h=H)

                def body(k, u):
                    if valid(k - 1):
                        i = k - 1
                        e = csc[:, 1 - u, :]
                        dve.wait_ge(e_a.sem, e_a.at(i, "e"))
                        nc.vector.tensor_reduce(csm, heads(e), AX, ALU.add).then_inc(p_v.sem, 1)
                        dve.wait_ge(p_v.sem, p_v.at(i, "sum"))
                        nc.vector.reciprocal(csm, csm).then_inc(p_v.sem, 1)
                        dve.wait_ge(p_v.sem, p_v.at(i, "rs"))
                        before(dve, t_p.sem, t_p.at(i - 1, "pT"))
                        nc.vector.tensor_tensor(heads(cpn), heads(e), csm[:, :, None].to_broadcast([P, H, NS]), ALU.mult)\
                            .then_inc(p_v.sem, 1)
                    if valid(k):
                        dve.wait_ge(qv_p.sem, qv_p.at(k, "v"))
                        before(dve, v_g.sem, v_g.at(k - 2, "vbd"))
                        nc.vector.tensor_tensor(cvb[:, u, :], ps[1][:, 0:D], row["cbv"], ALU.add).then_inc(s_v.sem, 1)
                        dve.wait_ge(s_p.sem, s_p.at(k, "s"))
                        nc.vector.tensor_reduce(cmx, heads(ps[2][:, 0:D]), AX, ALU.max).then_inc(s_v.sem, 1)
                        dve.wait_ge(s_v.sem, s_v.at(k, "max"))
                        nc.vector.tensor_tensor(heads(csc[:, u, :]), heads(ps[2][:, 0:D]),
                                                cmx[:, :, None].to_broadcast([P, H, NS]), ALU.subtract).then_inc(s_v.sem, 1)
                    if valid(k - 2):
                        i = k - 2
                        dve.wait_ge(o_p.sem, o_p.at(i, "o"))
                        before(dve, o_v.sem, o_v.at(i - 1, "out"))
                        nc.vector.tensor_tensor(ctmp, ps[5][:, 0:D], row["cbo"], ALU.add).then_inc(o_v.sem, 1)
                        dve.wait_ge(o_v.sem, o_v.at(i, "t"))
                        before(dve, st_out[u], dma_at(k - 4, u) if not isinstance(k, int) or k >= 4 else 0)
                        nc.vector.scalar_tensor_tensor(out=cout[:, u, :], in0=ctmp, scalar=tg[:, 3:4], in1=x_all[:, i],
                                                       op0=ALU.mult, op1=ALU.add).then_inc(o_v.sem, 1)
                pipeline(dve, body, 0, B + 2, steady)

            def gpsimd(pool):
                def slots(i, u):
                    before(pool, qv_p.sem, qv_p.at(i - 2, "v"))
                    for c in range(C):
                        last = nc.gpsimd.tensor_copy(orep[:, u, c], oT2[:, c, None, :, i].to_broadcast([P, HC, NS]))
                    last.then_inc(k_g.sem, 1)
                    before(pool, s_p.sem, s_p.at(i - 2, "s"))
                    nc.gpsimd.tensor_tensor(ckb[:, u], kTall[:, :, None, :, i].to_broadcast([P, C, HC, NS]),
                                            cv["mask8"][:, None, :, None].to_broadcast([P, C, HC, NS]), ALU.mult)\
                        .then_inc(k_g.sem, 1)

                def body(k, u):
                    if valid(k + 1):
                        slots(k + 1, 1 - u)
                    if valid(k):
                        pool.wait_ge(s_v.sem, s_v.at(k, "v"))
                        before(pool, t_p.sem, t_p.at(k - 2, "av"))
                        nc.gpsimd.tensor_tensor(cvbd[:, u].rearrange("p c (h d) -> p c h d", h=HC),
                                                cvb[:, u, :].rearrange("p (c h d) -> p c h d", c=C, h=HC),
                                                cv["mask8"][:, None, :, None].to_broadcast([P, C, HC, DH]), ALU.mult)\
                            .then_inc(v_g.sem, 1)
                pipeline(pool, body, -1, B, steady)
            return sync, tensor, scalar, vector, gpsimd

        def setup():
            def sync(sp):
                n = 0
                for dst, src in ((const[:, :], a["const"]), (w_sb[:, :, :, :].rearrange("p n c d -> p (n c d)"), a["weights"]),
                                 (row_sb[:, :, :].rearrange("p n d -> p (n d)"), a["rows"].partition_broadcast(P)),
                                 (col_sb[:, :, :].rearrange("p n c -> p (n c)"), a["cols"]),
                                 (wg_sb[:, :, :].rearrange("p c e -> p (c e)"), a["wg"]),
                                 (bg_sb[:, :], a["bg"].partition_broadcast(P)),
                                 (gates[:, :], a["gates"].partition_broadcast(P))):
                    sp.dma_start(dst, src).then_inc(ld_const, 16)
                for u in range(2):
                    sp.dma_start(x_all[:, u], a["x"][u]).then_inc(ld_x[u], 16)
                for e in range(RING):
                    sp.dma_start(ring[:, e, :], a["w12"][e]).then_inc(ld_ring[e], 16)
                sp.wait_ge(setup_v, 1)
                sp.dma_start(xs_dram.rearrange("(u p) d -> p u d", p=P), zero[:, None, :].to_broadcast([P, UNITS, D]))\
                    .then_inc(zeroed, 16)

            def vector(dve):
                nc.vector.memset(zero[:, :], 0.0).then_inc(setup_v, 1)
                nc.vector.memset(ones[:, :], 1.0)
                nc.vector.memset(eps_sb[:, :], EPS)
                nc.vector.memset(mhalf[:, :], -0.5)
                nc.vector.memset(vaug[:, :, :, DH], 1.0)
                dve.wait_ge(ld_const, 16 * 7)
                for n, name in enumerate(("bq0", "dbq", "cbq")):
                    nc.vector.tensor_scalar(qcol[:, n, :], col[name], QSCALE, None, ALU.mult)

            def scalar(act):
                act.wait_ge(ld_const, 16 * 7)
                nc.scalar.activation(tg[:, :], gates[:, :], ACT.Tanh)
            return sync, None, scalar, vector, None

        def run(programs):
            with nc.Block() as block:
                sync, tensor, scalar, vector, gpsimd = programs
                if sync:
                    block.sync(lambda e: sync(e))
                if tensor:
                    block.tensor(lambda e: tensor(e))
                if scalar:
                    block.scalar(lambda e: scalar(e))
                if vector:
                    block.vector(lambda e: vector(e))
                if gpsimd:
                    block.gpsimd(lambda e: gpsimd(e))

        run(setup())
        run(attention(0))
        run(routing())
        run(moe0())
        run(prepare())
        run(attention(1))
        run(moe1())
        run(combine())


def arrange(i):
    f = {k: np.ascontiguousarray(v) for k, v in i.items()}

    def chunks(m):
        return m.reshape(-1, P, m.shape[-1]).transpose(1, 0, 2).reshape(P, -1)

    p = "L1_ffn_"
    squares = [f["L0_xattn_w_q"], f["L0_xattn_w_k"], f["L0_xattn_w_v"], f["L0_xattn_w_o"],
               f["L1_xattn_Wq"].T, f["L1_xattn_Wk"].T, f["L1_xattn_Wv"].T, f["L1_xattn_Wo"].T,
               f[p + "d_Wv"], f[p + "d_Wo"], f[p + "c_Wq"], f[p + "c_Wk"], f[p + "c_Wv"], f[p + "c_Wo"]]
    rows = [f["L0_xattn_b_v"], f["L0_xattn_b_o"], f["L0_ffn_gamma"], f["L0_ffn_beta"],
            f[p + "d_bv"], f[p + "d_bo"], f[p + "c_bv"], f[p + "c_bo"]]
    cols = [f["L0_xattn_b_q"], f["L0_xattn_b_k"], f[p + "d_bq"], f[p + "d_bk"], f[p + "c_bq"], f[p + "c_bk"]]
    t = np.arange(P)
    const = np.concatenate([np.eye(P), t[:, None] < t[None, :], t[:, None] // DH == np.arange(HC),
                            np.broadcast_to(np.arange(E0), (P, E0)), np.broadcast_to(P * np.arange(B), (P, B)),
                            np.broadcast_to(np.arange(UNITS), (P, UNITS))], axis=1).astype(np.float32)
    w12 = np.concatenate([
        f["L0_ffn_W1"].transpose(0, 2, 1).reshape(E0, C, P, F0).transpose(0, 2, 1, 3).reshape(E0, P, C * F0),
        f["L0_ffn_W2"].transpose(0, 2, 1).reshape(E0, F0 // P, P, D).transpose(0, 2, 1, 3).reshape(E0, P, -1)], axis=2)
    r = np.arange(P)
    sel = np.concatenate([4 * t4 + r[None, :] // B == np.arange(E1)[:, None] for t4 in range(E1 // 4)], axis=1)
    small = [f[p + "slot_query"][0], f[p + "e_ln_g"], f[p + "e_ln_b"], f[p + "e_b2"]]
    sets = []
    for t4 in range(E1 // 4):
        for m in (f[p + "e_W1"], f[p + "e_Wg"]):
            for c in range(C):
                sets.append(m[4 * t4:4 * t4 + 4, c * P:(c + 1) * P, :].transpose(1, 0, 2).reshape(P, -1))
        for q in range(2):
            m = f[p + "e_W2"][4 * t4:4 * t4 + 4, 512 * q:512 * (q + 1), :].reshape(4, 4, P, D)
            sets.append(m.transpose(2, 0, 1, 3).reshape(P, -1))
    s = {
        "dq": chunks(f[p + "d_Wq"]), "dkT": chunks(f[p + "d_Wk"].T),
        "slotT": f[p + "slot_query"][0].T.reshape(C, P, NS).transpose(1, 0, 2).reshape(P, -1),
        "sel": sel.astype(np.float32), "small": np.concatenate(small, axis=1),
        "bias1": np.concatenate([f[p + "e_b1"], f[p + "e_bg"]], axis=1), "wset": np.stack(sets),
        "x": f["x"], "ctxT": f["ctx_1024"].reshape(B, P, C, P).transpose(0, 3, 2, 1).reshape(B, P, C * P),
        "fside": f["fside_BxS2_0"], "gates": np.concatenate([f["g_xattn"], f["g_ffn"]]).reshape(1, 4),
        "weights": np.concatenate([chunks(m) for m in squares], axis=1),
        "rows": np.stack(rows).reshape(1, -1), "cols": np.stack(cols).reshape(-1, P).T,
        "wg": chunks(f["L0_ffn_Wg"].T), "bg": f["L0_ffn_bg"].reshape(1, E0), "const": const,
        "w12": w12, "b1": f["L0_ffn_b1"].reshape(1, -1), "b2": f["L0_ffn_b2"].reshape(1, -1),
    }
    return {k: np.ascontiguousarray(v) for k, v in s.items()}


def kernel(**inputs):
    from concourse import bacc
    from concourse.bass_utils import run_bass_kernel_spmd

    nc = bacc.Bacc("TRN2", target_bir_lowering=False, num_devices=1)
    arrays = {f"{name}_dram": v for name, v in arrange(inputs).items()}
    given = {name[:-5]: nc.dram_tensor(name, v.shape, mybir.dt.from_np(v.dtype), kind="ExternalInput").ap()
             for name, v in arrays.items()}
    out = nc.dram_tensor("out_dram", (B, P, D), F32, kind="ExternalOutput").ap()
    build(nc, given, out)
    result = run_bass_kernel_spmd(nc, [arrays], core_ids=[0])
    return result.results[0]["out_dram"]
```

```python
from contextlib import ExitStack

import numpy as np
import concourse.bass as bass
from concourse import mybir

ALU = mybir.AluOpType
ACT = mybir.ActivationFunctionType
AX = mybir.AxisListType.X
F32 = mybir.dt.float32
I32 = mybir.dt.int32
U32 = mybir.dt.uint32
F32R = mybir.dt.float32r

P = 128
B, D, H = 32, 256, 16
DH = D // H
C = D // P
HC = H // C
G = 4
E0, F0 = 8, 1024
E1, F1, NS = 16, 1024, 16
UNITS = 2 * B + E0
RING = 2
SETS = 3
STEPS = 12
ARENA = 34168
EPS = 1e-5
QSCALE = 0.25

CONSTS = {"ident": 128, "tri": 128, "mask8": 8, "iota8": 8, "thr": 32, "iotau": UNITS}
WEIGHTS = ["q0", "k0", "v0", "o0", "q1", "k1", "v1", "o1", "dv", "do", "cq", "ck", "cv", "co"]
ROWS = ["bo0", "gamma", "beta", "dbv", "dbo", "cbv", "cbo"]
COLS = ["bq0", "bk0", "bv0", "dbq", "dbk", "cbq", "cbk"]


class Track:

    def __init__(self, sem, steps, items, base=0):
        self.sem, self.steps, self.items, self.base = sem, steps, items, base

    def at(self, item, step):
        if isinstance(item, int):
            item = min(item, self.items - 1)
        return item * len(self.steps) + (self.steps.index(step) + 1 + self.base)


def build(nc, a, out):
    ctx = ExitStack()
    with ctx:
        def sb(name, shape, dt=F32):
            return ctx.enter_context(nc.sbuf_tensor(name, shape, dt))

        def sem(name):
            return ctx.enter_context(nc.semaphore(name))

        def track(name, steps, items=B, base=0):
            return Track(sem(name), steps.split(), items, base)

        x_all = sb("x_all", [P, B, D])
        w_sb = sb("w_sb", [P, len(WEIGHTS), C, D])
        row_sb = sb("row_sb", [P, len(ROWS), D])
        col_sb = sb("col_sb", [P, len(COLS), C])
        const = sb("const", [P, sum(CONSTS.values())])
        wg_sb = sb("wg_sb", [P, C, E0])
        bg_sb = sb("bg_sb", [P, E0])
        gates = sb("gates", [P, 4])
        tg = sb("tg", [P, 4])
        qcol = sb("qcol", [P, 3, C])
        eps_sb = sb("eps_sb", [P, 1])
        mhalf = sb("mhalf", [P, 1])
        ones = sb("ones", [P, P])
        one_zero = sb("one_zero", [P, 3, DH])
        top_val = sb("top_val", [P, B, 8])
        top_idx = sb("top_idx", [P, B, 2])
        top8 = sb("top8", [P, 8])
        idx8 = sb("idx8", [P, 8], U32)
        slot_i = sb("slot_i", [P, 2, B], I32)
        wts = sb("wts", [P, 2, B])
        unit_e = sb("unit_e", [1, UNITS], I32)
        unit_r = sb("unit_r", [1, UNITS], I32)
        cend_i = sb("cend_i", [1, E0], I32)
        zero = sb("zero", [P, D])
        arena_at = nc.sbuf_base
        arena = sb("arena", [P, ARENA])
        cv = {}
        at = 0
        for n, w in CONSTS.items():
            cv[n] = const[:, at:at + w]
            at += w
        w = {n: w_sb[:, i] for i, n in enumerate(WEIGHTS)}
        row = {n: row_sb[:, i] for i, n in enumerate(ROWS)}
        col = {n: col_sb[:, i] for i, n in enumerate(COLS)}

        place = [0]

        def carve(*shape):
            n = int(np.prod(shape))
            v = arena[:, place[0]:place[0] + n]
            place[0] += n
            if len(shape) > 1:
                names = [f"d{i}" for i in range(len(shape))]
                v = v.rearrange(f"p ({' '.join(names)}) -> p {' '.join(names)}", **dict(zip(names[1:], shape[1:])))
            return v

        def rounded(name, first, *shape):
            return nc.alloc_sbuf_tensor_at(name, [P, *shape], F32R, offset=arena_at + 4 * first)

        ctxT = carve(2, C, P)
        xh = carve(2, D)
        xT = carve(C, P)
        kT = carve(C, P)
        qT = carve(2, C, P)
        kbd = carve(2 * C, HC, P)
        pr = carve(2, G, 512)
        pT = carve(2, 512)
        vz = carve(2, H // 2, 3, DH)
        aT = carve(C, P)
        rden = carve(C, P)
        xo = carve(D)
        xh3 = carve(D)
        xg = xh3
        xnT = carve(C, P)
        xc = carve(D)
        stat = carve(3, 6)
        mv = carve(3, 2)
        rstd = carve(3, 2)
        mx = carve(2, G)
        lg = carve(E0)
        carve(2)
        attention_end = place[0]
        ring_lo = rounded("ring_lo", place[0], RING, 2 * C * F0)
        ring_raw = carve(RING, 2 * C * F0)
        place_hi = place[0]
        ring_hi = rounded("ring_hi", place[0], RING, 2 * C * F0)
        carve(RING, 2 * C * F0)
        ring_end = place[0]
        place[0] = place_hi + 2 * C * F0
        xn_all = carve(B, D)
        assert place[0] <= ARENA, place[0]
        place[0] = ring_end
        hid = carve(2, F0)
        xT_hi = rounded("xT_hi", place[0], 2, C, P)
        carve(2, C, P)
        xT_lo = rounded("xT_lo", place[0], 2, C, P)
        carve(2, C, P)
        assert place[0] <= ARENA, place[0]
        place[0] = 0
        b1_sb = carve(E0, F0)
        b2_sb = carve(E0, D)
        moe_rows_end = place[0]
        xs = carve(2, D)
        yb = carve(2, D)
        hT_hi = rounded("hT_hi", place[0], F0 // P, P)
        carve(F0 // P, P)
        hT_lo = rounded("hT_lo", place[0], F0 // P, P)
        carve(F0 // P, P)
        assert place[0] <= attention_end, place[0]
        place[0] = moe_rows_end
        idxf = carve(B, 2)
        oh = carve(2, B, E0)
        msk = carve(B, E0)
        tot = carve(B, E0)
        inc = carve(B, E0)
        pos = carve(B, E0)
        ohp = carve(B, E0)
        posf = carve(2, B)
        blk = carve(E0, B)
        nblk = carve(E0)
        cend = carve(E0)
        basev = carve(E0)
        ucmp = carve(UNITS, E0)
        uexp = carve(UNITS)
        urng = carve(UNITS)
        ex = carve(B, 8)
        zs = carve(B)
        s2 = carve(B)
        den = carve(B)
        rr = carve(B)
        urng2 = carve(UNITS)
        assert place[0] <= attention_end, (place[0], attention_end)
        place[0] = attention_end
        wset = carve(SETS, 4, F1)
        oT_all = carve(C, NS, B)
        layer1_shared_end = place[0]
        yg = carve(2, 2, D)
        idx_cur = carve(2, 2).bitcast(I32)
        fs = carve(2, P)
        sbias = carve(2, 512)
        dVb = carve(2, D)
        sc = carve(C, P)
        pn = carve(C, P)
        pnT = carve(C, P)
        mk = carve(C, HC, NS)
        smx = carve(2)
        snx = carve(2)
        sz = carve(2)
        srz = carve(2)
        qa = carve(C, D)
        qac = carve(C)
        x3T = carve(C, P)
        assert place[0] <= ARENA, place[0]
        prep_w = pr.rearrange("p u g t -> p (u g t)")[:, 0:2 * C * D].rearrange("p (n c d) -> p n c d", n=2, c=C)
        slotT = ctxT[:, 0, 0, 0:C * NS].rearrange("p (c s) -> p c s", c=C)
        sqT = ctxT[:, 0, 1, 0:C * NS].rearrange("p (c s) -> p c s", c=C)
        qbd = kbd[:, 0:C, 0, :].rearrange("p c (h s) -> p c h s", h=HC)
        place[0] = 0
        sel = carve(4, P)
        small = carve(4, D)
        bias1 = carve(2, F1)
        orow = carve(4, D)
        hrow = carve(D)
        hT = carve(C, 4, P)
        us = carve(F1)
        gs = carve(F1)
        ugT = carve(F1 // P, P)
        oT2 = carve(C, NS, B)
        kTall = carve(C, NS, B)
        st1 = carve(6)
        mv1 = carve(2)
        rs1 = carve(2)
        slots_end = place[0]
        assert slots_end <= attention_end, (slots_end, attention_end)
        place[0] = attention_end
        x3l = carve(2, C, P)
        cqT = carve(2, C, P)
        orep = carve(2, C, HC, NS)
        ckb = carve(2, C, HC, NS)
        cvb = carve(2, D)
        cvbd = carve(2, C, P)
        csc = carve(2, D)
        cpn = carve(D)
        cpT = carve(C, P)
        caT = carve(C, P)
        ctmp = carve(D)
        cout = carve(2, D)
        cmx = carve(H)
        csm = carve(H)
        assert place[0] <= layer1_shared_end

        ps = [ctx.enter_context(nc.psum_tensor(f"ps{i}", [P, 512], F32)) for i in range(8)]

        xs_dram = nc.dram_tensor("xs_rows", (UNITS * P, D), F32, kind="Internal").ap()
        x3T_dram = nc.dram_tensor("x3_transposed", (B, P, C * P), F32, kind="Internal").ap()
        ys_dram = nc.dram_tensor("ys_rows", (UNITS * P, D), F32, kind="Internal").ap()

        ld_const, zeroed, zdone, scattered = sem("ld_const"), sem("zeroed"), sem("zdone"), sem("scattered")
        ld_w = sem("ld_w")
        passed = sem("passed")
        setup_v, setup_a, setup_p = sem("setup_v"), sem("setup_a"), sem("setup_p")
        ld_x = [sem("ld_x0"), sem("ld_x1")]

        def before(eng, s, value):
            if not isinstance(value, int) or value > 0:
                eng.wait_ge(s, value)

        def settled(eng):
            eng.sem_inc(passed, 1)

        def dma_at(i, u, n=1):
            return (i - u) * (8 * n) + 16 * n

        def pipeline(eng, body, first=-2, last=B + 4, steady=(4, B - 2)):
            for k in range(first, steady[0]):
                body(k, k % 2)
            with eng.Fori(steady[0] // 2, steady[1] // 2) as j:
                body(2 * j, 0)
                body(2 * j + 1, 1)
            for k in range(steady[1], last):
                body(k, k % 2)

        def valid(i):
            return not isinstance(i, int) or 0 <= i < B

        def attention(L):
            n = f"a{L}_"
            A = L == 0
            last_k, steady = (B + 4, (4, B - 2)) if A else (B + 5, (6, B - 2))
            wq, wk, wv, wo = (w[f"{c}{L}"] for c in "qkvo")
            ld_ctx = [sem(n + "ld_ctx0"), sem(n + "ld_ctx1")]
            pre_p = track(n + "pre_p", "xT K Q V")
            sc_p = track(n + "sc_p", "0 1 2 3")
            tr_p = track(n + "tr_p", "0 1 2 3")
            pv_p = track(n + "pv_p", "0 1 2 3")
            out_p = track(n + "out_p", "O")
            pre_a = track(n + "pre_a", "xT K Q")
            ex_a = track(n + "ex_a", "0 1 2 3")
            tr_a = track(n + "tr_a", "0 1 2 3")
            ln_v = track(n + "ln_v", "stats mean xh")
            v_a = track(n + "v_a", "V")
            sc_v = track(n + "sc_v", "m0 s0 m1 s1 m2 s2 m3 s3" if A else "a0 m0 a1 m1 a2 m2 a3 m3")
            out_v = track(n + "out_v", "den att x")
            ln_g = track(n + "ln_g", "var rstd")
            keep_a = track(n + "keep_a", "x")
            kb_g = track(n + "kb_g", "0 1")
            rd = ("s" if A else "a")
            if A:
                rt_p = track(n + "rt_p", "xnT lg")
                rt_a = track(n + "rt_a", "xnT")
                rt_v = track(n + "rt_v", "lg top idx keep_top keep_idx")
                bias_g = track(n + "bias_g", "x")
                n2_v = track(n + "n2_v", "stats mean xo stats3 res mean3 xh3")
                n2_g = track(n + "n2_g", "var rstd var3 rstd3 gamma xn")
            else:
                sub_g = track(n + "sub_g", "0 1 2 3")
                gidx_g = track(n + "gidx_g", "idx")
                ld_y = [sem(n + "ld_y0"), sem(n + "ld_y1")]
                ld_fs = [sem(n + "ld_fs0"), sem(n + "ld_fs1")]
                mix_v = track(n + "mix_v", "y0 y1")
                n4_v = track(n + "n4_v", "stats mean xh")
                n4_g = track(n + "n4_g", "var rstd")
                x1_p = track(n + "x1_p", "xT s V")
                x1_a = track(n + "x1_a", "xT e0 e1")
                x1_v = track(n + "x1_v", "s0 s1 neg V")
                x2_p = track(n + "x2_p", "pT av")
                x2_a = track(n + "x2_a", "pT")
                x2_v = track(n + "x2_v", "rz pn mask sum")
                st_x3 = [sem(n + "st_x3_0"), sem(n + "st_x3_1")]

            def flat(t, i, g, back):
                return i * 4 + g + 1 - back

            def sync(sp):
                for u in range(2):
                    sp.dma_start(ctxT[:, u].rearrange("p c t -> p (c t)"), a["ctxT"][u]).then_inc(ld_ctx[u], 16)
                    if not A:
                        sp.dma_start(fs[:, u], a["fside"][u:u + 1, :].partition_broadcast(P)).then_inc(ld_fs[u], 16)

                def later_loads(k, u):
                    if isinstance(k, int):
                        if 0 <= k < RING:
                            sp.dma_start(ring_raw[:, k, :], a["w12"][k]).then_inc(ld_ring[k], 16)
                        if k == RING:
                            sp.dma_start(w_sb[:, 4:].rearrange("p n c d -> p (n c d)"), a["weights"][:, 4 * C * D:])\
                                .then_inc(ld_w, 16)
                    elif u == 0:
                        rows = UNITS * P // STEPS
                        sp.dma_start(xs_dram[bass.ds((k - 4) * (rows // 2), rows), :].rearrange("(u p) d -> p u d", p=P),
                                     zero[:, None, :].to_broadcast([P, UNITS // STEPS, D])).then_inc(zeroed, 16)

                def body(k, u):
                    if A:
                        later_loads(k, u)
                    if not A and valid(k + 1) and (not isinstance(k, int) or k >= 1):
                        sp.wait_ge(sc_v.sem, sc_v.at(k - 1, "a3"))
                        sp.dma_start(fs[:, 1 - u], a["fside"][bass.ds(k + 1, 1), :].partition_broadcast(P))\
                            .then_inc(ld_fs[1 - u], 16)
                    if not A and valid(k - 4):
                        sp.wait_ge(x1_a.sem, x1_a.at(k - 4, "xT"))
                        sp.dma_start(x3T_dram[k - 4], x3T.rearrange("p c t -> p (c t)")).then_inc(st_x3[u], 16)
                    if A and valid(k + 4) and (not isinstance(k, int) or k >= -2):
                        i = k + 4
                        before(sp, ln_v.sem, ln_v.at(k + 2, "stats"))
                        sp.dma_start(x_all[:, i], a["x"][i]).then_inc(ld_x[u], 16)
                    if valid(k + 3) and (not isinstance(k, int) or k + 3 >= 2):
                        i = k + 3
                        before(sp, pre_p.sem, pre_p.at(k + 1, "V"))
                        sp.dma_start(ctxT[:, 1 - u].rearrange("p c t -> p (c t)"), a["ctxT"][i]).then_inc(ld_ctx[1 - u], 16)
                pipeline(sp, body, first=-2, last=B - 2 if A else B + 4, steady=(4 if A else 6, B - 4))
                if not A:
                    for s in st_x3:
                        sp.wait_ge(s, 8 * B)

            def tensor(pe):
                def weighted_values(k, u, g):
                    pe.wait_ge(tr_a.sem, tr_a.at(k, str(g)))
                    if g == 0:
                        pe.wait_ge(v_a.sem, v_a.at(k, "V"))
                        before(pe, out_v.sem, out_v.at(k - 1, "att"))
                    c, odd = g // 2, g % 2
                    for what in range(2):
                        for h in range(G):
                            vals = vz[:, u, c * G + h] if what == 0 else one_zero[:, :, :]
                            o = what * D + c * P
                            last = nc.tensor.matmul(ps[4][32 * h:32 * (h + 1), o:o + P], vals[:, odd:odd + 2, :],
                                                    pT[:, g % 2, h * P:(h + 1) * P],
                                                    start=g == 0 and what == 0, stop=g == 3 and what == 1)
                    last.then_inc(pv_p.sem, 1)

                def body(k, u):
                    for g in range(G):
                        if valid(k - 1):
                            pe.wait_ge(ex_a.sem, ex_a.at(k - 1, str(g)))
                            before(pe, tr_a.sem, flat(tr_a, k - 1, g, 2))
                            for h in range(G):
                                last = nc.tensor.transpose(ps[2 + g % 2][:, h * P:(h + 1) * P],
                                                           pr[:, 1 - u, g, h * P:(h + 1) * P], cv["ident"])
                            last.then_inc(tr_p.sem, 1)
                        if valid(k):
                            pe.wait_ge(pre_a.sem, pre_a.at(k, "Q"))
                            pe.wait_ge(kb_g.sem, kb_g.at(k, str(g // 2)))
                            before(pe, sc_v.sem, sc_v.at(k, f"{rd}{g}") - 4)
                            c = g // 2
                            nc.tensor.matmul(ps[g % 2][:, :], qT[:, u, c, :],
                                             kbd[:, C * u + c, bass.ds(g % 2, G, 2), :],
                                             start=True, stop=True).then_inc(sc_p.sem, 1)
                        if g > 0 and valid(k - 1):
                            weighted_values(k - 1, 1 - u, g - 1)
                        if valid(k + 1):
                            i, o = k + 1, 1 - u
                            if g == 0:
                                pe.wait_ge(ln_v.sem, ln_v.at(i, "xh"))
                                before(pe, v_a.sem, v_a.at(k, "V"))
                                if not A:
                                    before(pe, x2_v.sem, x2_v.at(k - 6, "mask"))
                                for c in range(C):
                                    last = nc.tensor.transpose(ps[5][:, c * P:(c + 1) * P],
                                                               xh[:, o, c * P:(c + 1) * P], cv["ident"])
                                last.then_inc(pre_p.sem, 1)
                                pe.wait_ge(ld_ctx[o], dma_at(i, o))
                                before(pe, pre_a.sem, pre_a.at(k, "Q"))
                                for m in range(C):
                                    for c in range(C):
                                        last = nc.tensor.matmul(ps[6][:, m * P:(m + 1) * P],
                                                                wk[:, c, m * P:(m + 1) * P], ctxT[:, o, c, :],
                                                                start=c == 0, stop=c == C - 1)
                                last.then_inc(pre_p.sem, 1)
                            if g == 2:
                                pe.wait_ge(pre_a.sem, pre_a.at(i, "K"))
                                if not A:
                                    before(pe, x2_a.sem, x2_a.at(k - 5, "pT"))
                                for m in range(C):
                                    for c in range(C):
                                        last = nc.tensor.matmul(ps[6][:, m * P:(m + 1) * P],
                                                                wq[:, c, m * P:(m + 1) * P], xT[:, c, :],
                                                                start=c == 0, stop=c == C - 1)
                                last.then_inc(pre_p.sem, 1)
                            if g == 3:
                                pe.wait_ge(pre_a.sem, pre_a.at(i, "xT"))
                                if not A:
                                    before(pe, x1_v.sem, x1_v.at(k - 4, "V"))
                                for c in range(C):
                                    last = nc.tensor.matmul(ps[5][:, 0:D], ctxT[:, o, c, :], wv[:, c, :],
                                                            start=c == 0, stop=c == C - 1)
                                last.then_inc(pre_p.sem, 1)
                        if A and valid(k - 4):
                            i = k - 4
                            if g == 1:
                                pe.wait_ge(n2_g.sem, n2_g.at(i, "xn"))
                                before(pe, out_v.sem, out_v.at(k - 3, "x"))
                                for c in range(C):
                                    last = nc.tensor.transpose(ps[7][:, c * P:(c + 1) * P],
                                                               xc[:, c * P:(c + 1) * P], cv["ident"])
                                last.then_inc(rt_p.sem, 1)
                            if g == 2:
                                pe.wait_ge(rt_a.sem, rt_a.at(i, "xnT"))
                                for c in range(C):
                                    last = nc.tensor.matmul(ps[7][:, 0:E0], xnT[:, c, :], wg_sb[:, c, :],
                                                            start=c == 0, stop=c == C - 1)
                                last.then_inc(rt_p.sem, 1)
                        if not A and valid(k - 4):
                            i = k - 4
                            if g == 0:
                                pe.wait_ge(n4_v.sem, n4_v.at(i, "xh"))
                                before(pe, out_v.sem, out_v.at(k - 3, "x"))
                                for c in range(C):
                                    last = nc.tensor.transpose(ps[7][:, c * P:(c + 1) * P],
                                                               xc[:, c * P:(c + 1) * P], cv["ident"])
                                last.then_inc(x1_p.sem, 1)
                            if g == 1:
                                pe.wait_ge(x1_a.sem, x1_a.at(i, "xT"))
                                for m in range(C):
                                    for c in range(C):
                                        last = nc.tensor.matmul(ps[7][:, D + m * P:D + (m + 1) * P],
                                                                qa[:, c, m * P:(m + 1) * P], x3T[:, c, :],
                                                                start=c == 0, stop=c == C - 1)
                                last.then_inc(x1_p.sem, 1)
                                before(pe, pre_a.sem, pre_a.at(k + 1, "xT"))
                                before(pe, v_a.sem, v_a.at(k, "V"))
                                before(pe, x2_v.sem, x2_v.at(k - 6, "mask"))
                                for c in range(C):
                                    last = nc.tensor.matmul(ps[5][:, D:2 * D], x3T[:, c, :], w["dv"][:, c, :],
                                                            start=c == 0, stop=c == C - 1)
                                last.then_inc(x1_p.sem, 1)
                        if not A and valid(k - 5):
                            i = k - 5
                            if g == 1:
                                pe.wait_ge(x2_v.sem, x2_v.at(i, "pn"))
                                before(pe, pre_a.sem, pre_a.at(k + 1, "K"))
                                for c in range(C):
                                    last = nc.tensor.transpose(ps[6][:, D + c * P:D + (c + 1) * P],
                                                               pn[:, c, :], cv["ident"])
                                last.then_inc(x2_p.sem, 1)
                            if g == 3:
                                pe.wait_ge(x2_a.sem, x2_a.at(i, "pT"))
                                before(pe, x1_v.sem, x1_v.at(k - 4, "V"))
                                before(pe, pre_a.sem, pre_a.at(k + 1, "xT"))
                                for m in range(C):
                                    last = nc.tensor.matmul(ps[5][:, D + m * P:D + (m + 1) * P],
                                                            dVb[:, 1 - u, m * P:(m + 1) * P],
                                                            pnT[:, m, :], start=True, stop=True)
                                last.then_inc(x2_p.sem, 1)
                        if valid(k - 2):
                            i = k - 2
                            if g == 3:
                                pe.wait_ge(out_v.sem, out_v.at(i, "att"))
                                if A:
                                    before(pe, rt_v.sem, rt_v.at(k - 4, "lg"))
                                else:
                                    before(pe, x1_v.sem, x1_v.at(k - 4, "s1"))
                                for c in range(C):
                                    last = nc.tensor.matmul(ps[7][:, D:2 * D], aT[:, c, :], wo[:, c, :],
                                                            start=c == 0, stop=c == C - 1)
                                last.then_inc(out_p.sem, 1)
                        if g == 3 and valid(k - 1):
                            weighted_values(k - 1, 1 - u, 3)
                pipeline(pe, body, last=last_k, steady=steady)

            def scalar(act):
                def body(k, u):
                    if valid(k):
                        act.wait_ge(pre_p.sem, pre_p.at(k, "V"))
                        before(act, pv_p.sem, pv_p.at(k - 2, "3"))
                        if not A:
                            before(act, x2_v.sem, x2_v.at(k - 6, "mask"))
                        nc.scalar.copy(vz[:, u, :, bass.ds(0, 2, 2), :],
                                       ps[5][:, 0:D].rearrange("p (j h d) -> p j h d", h=2, d=DH)).then_inc(v_a.sem, 1)
                    for g in range(G):
                        if valid(k - 1):
                            act.wait_ge(tr_p.sem, tr_p.at(k - 1, str(g)))
                            before(act, pv_p.sem, flat(pv_p, k - 1, g, 2))
                            nc.scalar.copy(pT[:, g % 2, :], ps[2 + g % 2][:, :]).then_inc(tr_a.sem, 1)
                        i, e, v = (k, g - 1, u) if g else (k - 1, G - 1, 1 - u)
                        if valid(i):
                            if A:
                                act.wait_ge(sc_v.sem, sc_v.at(i, f"s{e}"))
                            else:
                                act.wait_ge(sub_g.sem, sub_g.at(i, str(e)))
                            nc.scalar.activation(pr[:, v, e, :], pr[:, v, e, :], ACT.Exp).then_inc(ex_a.sem, 1)
                        if valid(k + 1):
                            i, o = k + 1, 1 - u
                            if g == 0:
                                act.wait_ge(pre_p.sem, pre_p.at(i, "xT"))
                                before(act, pre_p.sem, pre_p.at(k, "Q"))
                                nc.scalar.copy(xT.rearrange("p c t -> p (c t)"), ps[5][:, 0:D]).then_inc(pre_a.sem, 1)
                                act.wait_ge(pre_p.sem, pre_p.at(i, "K"))
                                before(act, kb_g.sem, kb_g.at(k, "1"))
                                for c in range(C):
                                    last = nc.scalar.activation(kT[:, c, :], ps[6][:, c * P:(c + 1) * P], ACT.Identity,
                                                                bias=col["bk0"][:, c:c + 1] if A else 0.0)
                                last.then_inc(pre_a.sem, 1)
                        if not A and g == 1 and valid(k - 5):
                            act.wait_ge(x2_p.sem, x2_p.at(k - 5, "pT"))
                            before(act, pre_p.sem, pre_p.at(k + 1, "K"))
                            before(act, x2_p.sem, x2_p.at(k - 6, "av"))
                            nc.scalar.copy(pnT.rearrange("p c t -> p (c t)"), ps[6][:, D:2 * D]).then_inc(x2_a.sem, 1)
                        if A and g == 1 and valid(k - 4):
                            act.wait_ge(rt_p.sem, rt_p.at(k - 4, "xnT"))
                            nc.scalar.copy(xnT.rearrange("p c t -> p (c t)"), ps[7][:, 0:D]).then_inc(rt_a.sem, 1)
                            nc.scalar.copy(xn_all[:, k - 4, :], xc).then_inc(keep_a.sem, 1)
                        if not A and g == 0 and valid(k - 4):
                            act.wait_ge(x1_p.sem, x1_p.at(k - 4, "xT"))
                            before(act, x1_p.sem, x1_p.at(k - 5, "V"))
                            before(act, st_x3[1 - u], dma_at(k - 5, 1 - u) if not isinstance(k, int) or k >= 5 else 0)
                            nc.scalar.copy(x3T.rearrange("p c t -> p (c t)"), ps[7][:, 0:D]).then_inc(x1_a.sem, 1)
                        if g == 2 and valid(k + 1):
                            i, o = k + 1, 1 - u
                            act.wait_ge(pre_p.sem, pre_p.at(i, "Q"))
                            before(act, sc_p.sem, sc_p.at(k - 1, "3"))
                            for c in range(C):
                                last = nc.scalar.activation(qT[:, o, c, :], ps[6][:, c * P:(c + 1) * P], ACT.Identity,
                                                            bias=qcol[:, 0, c:c + 1] if A else 0.0, scale=QSCALE)
                            last.then_inc(pre_a.sem, 1)
                        if not A and g == 3 and valid(k - 4):
                            act.wait_ge(x1_v.sem, x1_v.at(k - 4, "neg"))
                            before(act, x2_v.sem, x2_v.at(k - 5, "pn"))
                            for c in range(C):
                                nc.scalar.activation(sc[:, c, :], sc[:, c, :], ACT.Exp, bias=snx[:, c:c + 1],
                                                     accum_out=sz[:, c:c + 1]).then_inc(x1_a.sem, 1)
                pipeline(act, body, last=last_k, steady=steady)

            def vector(dve):
                def body(k, u):
                    nxt, cur, out_i, ln_i, rt_i, sl_i = k + 2, k, k - 2, k - 3, k - 4, k - 5
                    for g in range(G):
                        if g == 0 and valid(out_i):
                            dve.wait_ge(pv_p.sem, pv_p.at(out_i, "3"))
                            nc.vector.reciprocal(rden.rearrange("p c t -> p (c t)"), ps[4][:, D:2 * D])\
                                .then_inc(out_v.sem, 1)
                        if g == 0 and valid(ln_i):
                            t = n2_v if A else n4_v
                            dve.wait_ge(out_v.sem, out_v.at(ln_i, "x"))
                            settled(dve)
                            nc.vector.bn_stats(stat[:, 1, :], x_all[:, ln_i]).then_inc(t.sem, 1)
                        if g == 0 and valid(out_i):
                            dve.wait_ge(out_v.sem, out_v.at(out_i, "den"))
                            before(dve, out_p.sem, out_p.at(k - 3, "O"))
                            nc.vector.tensor_tensor(aT.rearrange("p c t -> p (c t)"), ps[4][:, 0:D],
                                                    rden.rearrange("p c t -> p (c t)"), ALU.mult).then_inc(out_v.sem, 1)
                        if g == 0 and valid(ln_i):
                            dve.wait_ge(t.sem, t.at(ln_i, "stats"))
                            settled(dve)
                            nc.vector.bn_aggr(mv[:, 1, :], stat[:, 1, :]).then_inc(t.sem, 1)
                        if g == 3 and valid(ln_i) and A:
                            dve.wait_ge(n2_g.sem, n2_g.at(ln_i, "rstd3"))
                            before(dve, n2_g.sem, n2_g.at(ln_i - 1, "xn"))
                            nc.vector.tensor_scalar(xh3, xo, mv[:, 2, 0:1], rstd[:, 2, 1:2],
                                                    ALU.subtract, ALU.mult).then_inc(n2_v.sem, 1)
                        if valid(cur):
                            s = ps[g % 2][:, :].rearrange("p (h t) -> p h t", h=G)
                            sbv = sbias[:, g % 2, :].rearrange("p (h t) -> p h t", h=G)
                            dst = pr[:, u, g, :].rearrange("p (h t) -> p h t", h=G)
                            m = mx[:, g % 2, :]
                            dve.wait_ge(sc_p.sem, sc_p.at(k, str(g)))
                            if A:
                                nc.vector.tensor_reduce(m, s, AX, ALU.max).then_inc(sc_v.sem, 1)
                            else:
                                if g == 0:
                                    dve.wait_ge(ld_fs[u], dma_at(k, u))
                                before(dve, sub_g.sem, flat(sub_g, k, g, 2))
                                nc.vector.tensor_tensor(sbv, s, fs[:, u, None, :].to_broadcast([P, G, P]),
                                                        ALU.add).then_inc(sc_v.sem, 1)
                        if A and g == 0 and valid(nxt):
                            dve.wait_ge(ld_x[u], dma_at(nxt, u))
                            settled(dve)
                            nc.vector.bn_stats(stat[:, 0, :], x_all[:, nxt]).then_inc(ln_v.sem, 1)
                        if A and g == 1 and valid(ln_i):
                            dve.wait_ge(n2_g.sem, n2_g.at(ln_i, "rstd"))
                            nc.vector.tensor_scalar(xo, x_all[:, ln_i], mv[:, 1, 0:1], rstd[:, 1, 1:2],
                                                    ALU.subtract, ALU.mult).then_inc(n2_v.sem, 1)
                        if A and g == 2 and valid(rt_i):
                            dve.wait_ge(rt_p.sem, rt_p.at(rt_i, "lg"))
                            nc.vector.tensor_tensor(lg, ps[7][:, 0:E0], bg_sb[:, :], ALU.add).then_inc(rt_v.sem, 1)
                        if not A and g == 0 and valid(sl_i):
                            dve.wait_ge(x1_a.sem, x1_a.at(sl_i, "e1"))
                            nc.vector.reciprocal(srz, sz).then_inc(x2_v.sem, 1)
                        if not A and g == 1 and valid(nxt):
                            settled(dve)
                            nc.vector.bn_stats(stat[:, 0, :], x_all[:, nxt]).then_inc(ln_v.sem, 1)
                        if not A and g == 2 and valid(rt_i):
                            dve.wait_ge(x1_v.sem, x1_v.at(rt_i, "s1"))
                            nc.vector.tensor_scalar(snx, smx, -1.0, None, ALU.mult).then_inc(x1_v.sem, 1)
                        if valid(cur):
                            if A:
                                dve.wait_ge(sc_v.sem, sc_v.at(k, f"m{g}"))
                                before(dve, tr_p.sem, tr_p.at(k - 2, str(g)))
                                nc.vector.tensor_tensor(dst, s, m[:, :, None].to_broadcast([P, G, P]),
                                                        ALU.subtract).then_inc(sc_v.sem, 1)
                            else:
                                dve.wait_ge(sc_v.sem, sc_v.at(k, f"a{g}"))
                                nc.vector.tensor_reduce(m, sbv, AX, ALU.max).then_inc(sc_v.sem, 1)
                        if g == (0 if A else 1) and valid(nxt):
                            dve.wait_ge(ln_v.sem, ln_v.at(nxt, "stats"))
                            settled(dve)
                            nc.vector.bn_aggr(mv[:, 0, :], stat[:, 0, :]).then_inc(ln_v.sem, 1)
                        if A and g == 1 and valid(ln_i):
                            dve.wait_ge(n2_v.sem, n2_v.at(ln_i, "xo"))
                            settled(dve)
                            nc.vector.bn_stats(stat[:, 2, :], xo).then_inc(n2_v.sem, 1)
                            nc.vector.scalar_tensor_tensor(out=x_all[:, ln_i], in0=xo, scalar=tg[:, 2:3],
                                                           in1=x_all[:, ln_i], op0=ALU.mult, op1=ALU.add)\
                                .then_inc(n2_v.sem, 1)
                            dve.wait_ge(n2_v.sem, n2_v.at(ln_i, "stats3"))
                            settled(dve)
                            nc.vector.bn_aggr(mv[:, 2, :], stat[:, 2, :]).then_inc(n2_v.sem, 1)
                        if A and g == 2 and valid(rt_i):
                            dve.wait_ge(rt_v.sem, rt_v.at(rt_i, "lg"))
                            settled(dve)
                            nc.vector.max(top8[:, :], lg).then_inc(rt_v.sem, 1)
                        if g == 2 and valid(nxt):
                            dve.wait_ge(ln_g.sem, ln_g.at(nxt, "rstd"))
                            before(dve, pre_p.sem, pre_p.at(k, "xT"))
                            nc.vector.tensor_scalar(xh[:, u, :], x_all[:, nxt], mv[:, 0, 0:1], rstd[:, 0, 1:2],
                                                    ALU.subtract, ALU.mult).then_inc(ln_v.sem, 1)
                        if A and g == 2 and valid(rt_i):
                            dve.wait_ge(rt_v.sem, rt_v.at(rt_i, "top"))
                            settled(dve)
                            nc.vector.max_index(idx8[:, :], top8[:, :], lg).then_inc(rt_v.sem, 1)
                            nc.vector.tensor_copy(top_val[:, rt_i, :], top8[:, :]).then_inc(rt_v.sem, 1)
                            dve.wait_ge(rt_v.sem, rt_v.at(rt_i, "idx"))
                            nc.vector.tensor_copy(top_idx[:, rt_i, :], idx8[:, 0:2]).then_inc(rt_v.sem, 1)
                        if not A and g == 0 and valid(nxt):
                            dve.wait_ge(ld_y[u], dma_at(nxt, u, 2))
                            nc.vector.scalar_tensor_tensor(out=x_all[:, nxt], in0=yg[:, u, 0, :],
                                                           scalar=wts[:, 0, bass.ds(nxt, 1)], in1=x_all[:, nxt],
                                                           op0=ALU.mult, op1=ALU.add).then_inc(mix_v.sem, 1)
                        if not A and g == 0 and valid(sl_i):
                            dve.wait_ge(x2_v.sem, x2_v.at(sl_i, "rz"))
                            nc.vector.tensor_tensor(pn, sc, srz[:, :, None].to_broadcast([P, C, P]), ALU.mult)\
                                .then_inc(x2_v.sem, 1)
                        if not A and g == 0 and valid(nxt):
                            dve.wait_ge(mix_v.sem, mix_v.at(nxt, "y0"))
                            nc.vector.scalar_tensor_tensor(out=x_all[:, nxt], in0=yg[:, u, 1, :],
                                                           scalar=wts[:, 1, bass.ds(nxt, 1)], in1=x_all[:, nxt],
                                                           op0=ALU.mult, op1=ALU.add).then_inc(mix_v.sem, 1)
                            dve.wait_ge(mix_v.sem, mix_v.at(nxt, "y1"))
                        if not A and g == 1 and valid(rt_i):
                            dve.wait_ge(x1_p.sem, x1_p.at(rt_i, "s"))
                            before(dve, x2_v.sem, x2_v.at(sl_i, "pn"))
                            for c in range(C):
                                nc.vector.tensor_scalar(sc[:, c, :], ps[7][:, D + c * P:D + (c + 1) * P],
                                                        qac[:, c:c + 1], None, ALU.add, ALU.max,
                                                        accum_out=smx[:, c:c + 1]).then_inc(x1_v.sem, 1)
                        if not A and g == 2 and valid(ln_i):
                            dve.wait_ge(n4_g.sem, n4_g.at(ln_i, "rstd"))
                            before(dve, x1_p.sem, x1_p.at(ln_i - 1, "xT"))
                            nc.vector.tensor_scalar(xc, x_all[:, ln_i], mv[:, 1, 0:1], rstd[:, 1, 1:2],
                                                    ALU.subtract, ALU.mult).then_inc(n4_v.sem, 1)
                        if not A and g == 2 and valid(rt_i):
                            dve.wait_ge(x1_p.sem, x1_p.at(rt_i, "V"))
                            nc.vector.tensor_tensor(dVb[:, u, :], ps[5][:, D:2 * D], row["dbv"], ALU.add)\
                                .then_inc(x1_v.sem, 1)
                        if not A and g == 3 and valid(sl_i):
                            dve.wait_ge(x2_p.sem, x2_p.at(sl_i, "av"))
                            before(dve, pre_p.sem, pre_p.at(k + 1, "V"))
                            nc.vector.tensor_tensor(mk, ps[5][:, D:2 * D].rearrange("p (c h s) -> p c h s", c=C, h=HC),
                                                    cv["mask8"][:, None, :, None].to_broadcast([P, C, HC, NS]),
                                                    ALU.mult).then_inc(x2_v.sem, 1)
                        if g == 3 and valid(out_i):
                            dve.wait_ge(out_p.sem, out_p.at(out_i, "O"))
                            if A:
                                dve.wait_ge(bias_g.sem, bias_g.at(out_i, "x"))
                            nc.vector.scalar_tensor_tensor(out=x_all[:, out_i], in0=ps[7][:, D:2 * D],
                                                           scalar=tg[:, L:L + 1], in1=x_all[:, out_i],
                                                           op0=ALU.mult, op1=ALU.add).then_inc(out_v.sem, 1)
                        if not A and g == 3 and valid(sl_i):
                            dve.wait_ge(x2_v.sem, x2_v.at(sl_i, "mask"))
                            nc.vector.tensor_reduce(oT_all[:, :, :, sl_i], mk.rearrange("p c h s -> p c s h"), AX,
                                                    ALU.add).then_inc(x2_v.sem, 1)
                pipeline(dve, body, last=last_k, steady=steady)

            def gpsimd(pool):
                def rsqrt(t, j, i, vname, rname):
                    nc.gpsimd.tensor_tensor(rstd[:, j, 0:1], mv[:, j, 1:2], eps_sb[:, :], ALU.add).then_inc(t.sem, 1)
                    pool.wait_ge(t.sem, t.at(i, vname))
                    nc.gpsimd.tensor_tensor(rstd[:, j, 1:2], rstd[:, j, 0:1], mhalf[:, :], ALU.pow).then_inc(t.sem, 1)

                def gather(i, u):
                    before(pool, mix_v.sem, mix_v.at(i - 2, "y1"))
                    nc.gpsimd.tensor_copy(idx_cur[:, u, :], slot_i[:, :, i]).then_inc(gidx_g.sem, 1)
                    pool.wait_ge(gidx_g.sem, gidx_g.at(i, "idx"))
                    settled(pool)
                    for c in range(2):
                        nc.gpsimd.indirect_dma_start(out=yg[:, u, c, :], out_offset=None, in_=ys_dram[:, :],
                                                     in_offset=bass.IndirectOffsetOnAxis(ap=idx_cur[:, u, c:c + 1].bitcast(U32), axis=0))\
                            .then_inc(ld_y[u], 16)

                def body(k, u):
                    if A:
                        if valid(k - 3):
                            pool.wait_ge(n2_v.sem, n2_v.at(k - 3, "mean"))
                            rsqrt(n2_g, 1, k - 3, "var", "rstd")
                        if valid(k + 2):
                            pool.wait_ge(ln_v.sem, ln_v.at(k + 2, "mean"))
                            rsqrt(ln_g, 0, k + 2, "var", "rstd")
                        if valid(k + 1):
                            kblock(k + 1, 1 - u, 0)
                        if valid(k - 3):
                            pool.wait_ge(n2_v.sem, n2_v.at(k - 3, "mean3"))
                            rsqrt(n2_g, 2, k - 3, "var3", "rstd3")
                        if valid(k + 1):
                            kblock(k + 1, 1 - u, 1)
                            pool.wait_ge(ln_v.sem, ln_v.at(k + 1, "xh"))
                            nc.gpsimd.tensor_tensor(x_all[:, k + 1], x_all[:, k + 1], row["bo0"], ALU.add)\
                                .then_inc(bias_g.sem, 1)
                        if valid(k - 3):
                            pool.wait_ge(n2_v.sem, n2_v.at(k - 3, "xh3"))
                            nc.gpsimd.tensor_tensor(xg, xh3, row["gamma"], ALU.mult).then_inc(n2_g.sem, 1)
                            pool.wait_ge(n2_g.sem, n2_g.at(k - 3, "gamma"))
                            before(pool, rt_p.sem, rt_p.at(k - 4, "xnT"))
                            before(pool, keep_a.sem, keep_a.at(k - 4, "x"))
                            nc.gpsimd.tensor_tensor(xc, xg, row["beta"], ALU.add).then_inc(n2_g.sem, 1)
                        return
                    if valid(k):
                        sub(k, u, 0)
                    if valid(k + 3) and (not isinstance(k, int) or k >= -1):
                        gather(k + 3, 1 - u)
                    if valid(k - 3):
                        pool.wait_ge(n4_v.sem, n4_v.at(k - 3, "mean"))
                        rsqrt(n4_g, 1, k - 3, "var", "rstd")
                    if valid(k):
                        sub(k, u, 1)
                    if valid(k + 2):
                        pool.wait_ge(ln_v.sem, ln_v.at(k + 2, "mean"))
                        rsqrt(ln_g, 0, k + 2, "var", "rstd")
                    if valid(k + 1):
                        kblock(k + 1, 1 - u, 0)
                    if valid(k):
                        sub(k, u, 2)
                    if valid(k + 1):
                        kblock(k + 1, 1 - u, 1)
                    if valid(k):
                        sub(k, u, 3)

                def sub(k, u, g):
                    pool.wait_ge(sc_v.sem, sc_v.at(k, f"m{g}"))
                    before(pool, tr_p.sem, tr_p.at(k - 2, str(g)))
                    nc.gpsimd.tensor_tensor(pr[:, u, g, :].rearrange("p (h t) -> p h t", h=G),
                                            sbias[:, g % 2, :].rearrange("p (h t) -> p h t", h=G),
                                            mx[:, g % 2, :, None].to_broadcast([P, G, P]), ALU.subtract)\
                        .then_inc(sub_g.sem, 1)

                def kblock(i, u, c):
                    pool.wait_ge(pre_a.sem, pre_a.at(i, "K"))
                    before(pool, sc_p.sem, sc_p.at(i - 2, str(2 * c + 1)))
                    nc.gpsimd.tensor_tensor(kbd[:, C * u + c], kT[:, c, None, :].to_broadcast([P, HC, P]),
                                            cv["mask8"][:, :, None].to_broadcast([P, HC, P]), ALU.mult)\
                        .then_inc(kb_g.sem, 1)

                if not A:
                    gather(0, 0)
                    gather(1, 1)
                pipeline(pool, body, last=last_k, steady=(4 if A else 6, B - 2 if A else B - 4))

            return sync, tensor, scalar, vector, gpsimd

        ld_ring = [sem(f"ld_ring{i}") for i in range(RING)]
        ld_ring_sw = [sem(f"ld_ring_sw{i}") for i in range(RING)]
        ld_rows = sem("ld_rows")
        route_v, route_p, route_a = sem("route_v"), sem("route_p"), sem("route_a")
        dn_p = track("m0_dn_p", "y", UNITS, base=1)

        def routing():
            def sync(sp):
                sp.wait_ge(ld_w, 16)
                sp.dma_start(b1_sb.rearrange("p e f -> p (e f)"), a["b1"].partition_broadcast(P)).then_inc(ld_rows, 16)
                sp.dma_start(b2_sb.rearrange("p e f -> p (e f)"), a["b2"].partition_broadcast(P)).then_inc(ld_rows, 16)

            def vector(dve):
                n = [0]

                def link(ins):
                    n[0] += 1
                    ins.then_inc(route_v, 1)
                    dve.wait_ge(route_v, n[0])

                def be(v):
                    return v[:, :, None].to_broadcast([P, B, E0])

                tt = nc.vector.tensor_tensor
                link(nc.vector.tensor_copy(idxf, top_idx[:, :, :]))
                for c in range(2):
                    link(tt(oh[:, c], idxf[:, :, c:c + 1].to_broadcast([P, B, E0]),
                            cv["iota8"][:, None, :].to_broadcast([P, B, E0]), ALU.is_equal))
                link(tt(msk, oh[:, 0], oh[:, 1], ALU.add))
                link(tt(ex, top_val[:, :, :], be(top_val[:, :, 0]), ALU.subtract))
                mask_ready = n[0]
                dve.wait_ge(route_a, 1)
                link(nc.vector.tensor_reduce(zs, ex, AX, ALU.add))
                link(tt(s2, ex[:, :, 0], ex[:, :, 1], ALU.add))
                link(nc.vector.scalar_tensor_tensor(out=den, in0=zs, scalar=1e-8, in1=s2, op0=ALU.mult, op1=ALU.add))
                link(nc.vector.reciprocal(rr, den))
                link(nc.vector.tensor_scalar(rr, rr, tg[:, 2:3], None, ALU.mult))
                for c in range(2):
                    link(tt(wts[:, c, :], ex[:, :, c], rr, ALU.mult))
                dve.wait_ge(route_p, 2)
                link(nc.vector.tensor_copy(tot.rearrange("p b e -> p (b e)"), ps[1][:, 0:B * E0]))
                for e in range(E0):
                    link(nc.vector.tensor_tensor_scan(inc[:, :, e], ones[:, 0:B], tot[:, :, e], 0.0, ALU.mult, ALU.add))
                link(tt(blk, inc[:, B - 1, :, None].to_broadcast([P, E0, B]),
                        cv["thr"][:, None, :].to_broadcast([P, E0, B]), ALU.is_gt))
                link(nc.vector.tensor_reduce(nblk, blk, AX, ALU.add))
                link(nc.vector.tensor_tensor_scan(cend, ones[:, 0:E0], nblk, 0.0, ALU.mult, ALU.add))
                link(tt(basev, cend, nblk, ALU.subtract))
                link(nc.vector.tensor_scalar(basev, basev, float(P), None, ALU.mult))
                link(nc.vector.tensor_scalar(cend_i[:, :], cend[0:1, :], float(dn_p.base), None, ALU.add))
                link(tt(pos, inc, tot, ALU.subtract))
                link(tt(pos, ps[0][:, 0:B * E0].rearrange("p (b e) -> p b e", e=E0), pos, ALU.add))
                link(tt(pos, pos, basev[:, None, :].to_broadcast([P, B, E0]), ALU.add))
                for c in range(2):
                    link(tt(ohp, oh[:, c], pos, ALU.mult))
                    link(nc.vector.tensor_reduce(posf[:, c, :], ohp, AX, ALU.add))
                link(nc.vector.tensor_copy(slot_i[:, :, :], posf))
                link(tt(ucmp, cv["iotau"][:, :, None].to_broadcast([P, UNITS, E0]),
                        cend[:, None, :].to_broadcast([P, UNITS, E0]), ALU.is_ge))
                link(nc.vector.tensor_reduce(uexp, ucmp, AX, ALU.add))
                link(nc.vector.tensor_scalar(uexp, uexp, float(E0 - 1), None, ALU.min))
                link(nc.vector.tensor_copy(unit_e[:, :], uexp[0:1, :]))
                link(nc.vector.tensor_scalar(urng, uexp, float(RING), None, ALU.is_ge))
                for m in range(2 * RING, E0, RING):
                    link(nc.vector.tensor_scalar(urng2, uexp, float(m), None, ALU.is_ge))
                    link(tt(urng, urng, urng2, ALU.add))
                link(nc.vector.scalar_tensor_tensor(out=urng, in0=urng, scalar=-float(RING), in1=uexp,
                                                    op0=ALU.mult, op1=ALU.add))
                link(nc.vector.tensor_copy(unit_r[:, :], urng[0:1, :]))
                nc.vector.tensor_copy(zs, rr).then_inc(route_done, 1)
                dve.wait_ge(route_a, 2)
                tt(ring_lo[:, 0, :], ring_raw[:, 0, :], ring_hi[:, 0, :], ALU.subtract)

            def tensor(pe):
                pe.wait_ge(route_v, 4)
                m = msk.rearrange("p b e -> p (b e)")
                nc.tensor.matmul(ps[0][:, 0:B * E0], cv["tri"], m, start=True, stop=True).then_inc(route_p, 1)
                nc.tensor.matmul(ps[1][:, 0:B * E0], ones[:, :], m, start=True, stop=True).then_inc(route_p, 1)

            def scalar(act):
                act.wait_ge(route_v, 5)
                nc.scalar.activation(ex.rearrange("p b e -> p (b e)"), ex.rearrange("p b e -> p (b e)"), ACT.Exp)\
                    .then_inc(route_a, 1)
                act.wait_ge(ld_ring[0], 16)
                nc.scalar.copy(ring_hi[:, 0, :], ring_raw[:, 0, :]).then_inc(route_a, 1)

            def gpsimd(pool):
                pool.sem_inc(dn_p.sem, dn_p.base)
                pool.wait_ge(route_done, 1)
                pool.wait_ge(zeroed, 16 * STEPS)
                for c in range(2):
                    for b in range(B):
                        nc.gpsimd.indirect_dma_start(
                            out=xs_dram[:, :], out_offset=bass.IndirectOffsetOnAxis(ap=slot_i[:, c, b:b + 1].bitcast(U32), axis=0),
                            in_=xn_all[:, b, :], in_offset=None).then_inc(scattered, 16)
                pool.wait_ge(scattered, 16 * 2 * B)
            return sync, tensor, scalar, vector, gpsimd

        route_done = sem("route_done")

        def moe0():
            ld_xs = [sem("ld_xs0"), sem("ld_xs1")]
            st_ys = [sem("st_ys0"), sem("st_ys1")]
            ring_ready = sem("ring_ready")
            x_p = track("m0_x_p", "x", UNITS)
            up_p = track("m0_up_p", "h0 h1", UNITS)
            tp_p = track("m0_tp_p", "a b", UNITS)
            x_a = track("m0_x_a", "hi", UNITS)
            x_v = track("m0_x_v", "lo", UNITS)
            ge_a = track("m0_ge_a", "h0 h1", UNITS)
            tp_a = track("m0_tp_a", "a b", UNITS)
            b1_v = track("m0_b1_v", "h0 h1", UNITS)
            tp_v = track("m0_tp_v", "a b", UNITS)
            y_v = track("m0_y_v", "y", UNITS)
            split_g = sem("m0_split_g")
            up_banks = [(1, 2), (6, 7)]
            FC = F0 // P

            def ok(i):
                return not isinstance(i, int) or 0 <= i < UNITS

            def units(eng, body, first=-1, last=UNITS + 1, steady=(2, UNITS - 2)):
                pipeline(eng, body, first, last, steady)

            def sync(sp):
                for u in range(2):
                    sp.dma_start(xs[:, u, :], xs_dram[u * P:(u + 1) * P, :]).then_inc(ld_xs[u], 16)

                def body(j, u):
                    if ok(j + 2) and (not isinstance(j, int) or j >= 0):
                        before(sp, x_p.sem, x_p.at(j, "x"))
                        sp.dma_start(xs[:, u, :], xs_dram[bass.ds((j + 2) * P, P), :]).then_inc(ld_xs[u], 16)
                    if ok(j - 1):
                        sp.wait_ge(y_v.sem, y_v.at(j - 1, "y"))
                        sp.dma_start(ys_dram[bass.ds((j - 1) * P, P), :], yb[:, 1 - u, :]).then_inc(st_ys[1 - u], 16)
                units(sp, body)
                for u in range(2):
                    sp.wait_ge(st_ys[u], 8 * UNITS)

            def gpsimd(pool):
                pool.sem_inc(ring_ready, 1)
                for e in range(1, E0):
                    r = e % RING
                    if e >= RING:
                        units_done = pool.value_load(cend_i[0:1, e - RING:e - RING + 1], min_val=1, max_val=UNITS + 1)
                        pool.wait_ge(dn_p.sem, units_done)
                        settled(pool)
                        pool.dma_start(ring_raw[:, r, :], a["w12"][e]).then_inc(ld_ring_sw[r], 16)
                        pool.wait_ge(ld_ring_sw[r], 16 * (e // RING))
                    else:
                        pool.wait_ge(ld_ring[e], 16)
                    nc.gpsimd.tensor_scalar(ring_hi[:, r, :], ring_raw[:, r, :], 1.0, 0.0,
                                            ALU.mult, ALU.add).then_inc(split_g, 1)
                    pool.wait_ge(split_g, e)
                    nc.gpsimd.tensor_tensor(ring_lo[:, r, :], ring_raw[:, r, :], ring_hi[:, r, :],
                                            ALU.subtract).then_inc(ring_ready, 1)

            def tensor(pe):
                def body(j, u):
                    if ok(j):
                        e = pe.value_load(unit_e[0:1, bass.ds(j, 1)], min_val=0, max_val=E0 - 1)
                        r = pe.value_load(unit_r[0:1, bass.ds(j, 1)], min_val=0, max_val=RING - 1)
                        pe.wait_ge(x_v.sem, x_v.at(j, "lo"))
                        pe.wait_ge(ring_ready, e + 1)
                        for h in range(2):
                            before(pe, b1_v.sem, b1_v.at(j - 2, f"h{h}"))
                            for n, (xp, wp) in enumerate(((xT_hi, ring_hi), (xT_hi, ring_lo), (xT_lo, ring_hi))):
                                for c in range(C):
                                    o = c * F0 + h * 512
                                    last = nc.tensor.matmul(ps[up_banks[u][h]][:, :], xp[:, u, c, :],
                                                            wp[:, bass.ds(r, 1), o:o + 512],
                                                            start=n == 0 and c == 0, stop=n == 2 and c == C - 1)
                            last.then_inc(up_p.sem, 1)
                    if ok(j - 1):
                        for q, bank in ((0, 3), (1, 4)):
                            pe.wait_ge(ge_a.sem, ge_a.at(j - 1, f"h{q}"))
                            before(pe, tp_v.sem, tp_v.at(j - 2, "ab"[q]))
                            for f in range(4):
                                last = nc.tensor.transpose(ps[bank][:, f * P:(f + 1) * P],
                                                           hid[:, 1 - u, (4 * q + f) * P:(4 * q + f + 1) * P], cv["ident"])
                            last.then_inc(tp_p.sem, 1)
                    if ok(j + 1):
                        pe.wait_ge(ld_xs[1 - u], dma_at(j + 1, 1 - u))
                        before(pe, x_v.sem, x_v.at(j, "lo"))
                        for c in range(C):
                            last = nc.tensor.transpose(ps[0][:, c * P:(c + 1) * P], xs[:, 1 - u, c * P:(c + 1) * P],
                                                       cv["ident"])
                        last.then_inc(x_p.sem, 1)
                    if ok(j - 1):
                        r = pe.value_load(unit_r[0:1, bass.ds(j - 1, 1)], min_val=0, max_val=RING - 1)
                        before(pe, y_v.sem, y_v.at(j - 2, "y"))
                        for n, (hp, parts) in enumerate(((hT_hi, (ring_hi, ring_lo)), (hT_lo, (ring_hi,)))):
                            done = tp_v if n else tp_a
                            for f in range(FC):
                                if f == 0:
                                    pe.wait_ge(done.sem, done.at(j - 1, "a"))
                                if f == FC // 2:
                                    pe.wait_ge(done.sem, done.at(j - 1, "b"))
                                o = C * F0 + f * D
                                for wp in parts:
                                    last = nc.tensor.matmul(ps[5][:, 0:D], hp[:, f, :],
                                                            wp[:, bass.ds(r, 1), o:o + D],
                                                            start=n == 0 and f == 0 and wp is ring_hi,
                                                            stop=n == 1 and f == FC - 1)
                        last.then_inc(dn_p.sem, 1)
                units(pe, body)

            def scalar(act):
                def body(j, u):
                    if ok(j - 1):
                        for q, bank in ((0, 3), (1, 4)):
                            act.wait_ge(tp_p.sem, tp_p.at(j - 1, "ab"[q]))
                            before(act, dn_p.sem, dn_p.at(j - 2, "y") if not isinstance(j, int) or j >= 2 else 0)
                            nc.scalar.copy(hT_hi[:, 4 * q:4 * q + 4, :], ps[bank][:, :])\
                                .then_inc(tp_a.sem, 1)
                    if ok(j + 1):
                        act.wait_ge(x_p.sem, x_p.at(j + 1, "x"))
                        before(act, up_p.sem, up_p.at(j - 1, "h1"))
                        nc.scalar.copy(xT_hi[:, 1 - u, :, :], ps[0][:, 0:D]).then_inc(x_a.sem, 1)
                    if ok(j):
                        for h in range(2):
                            act.wait_ge(b1_v.sem, b1_v.at(j, f"h{h}"))
                            v = hid[:, u, h * 512:(h + 1) * 512]
                            nc.scalar.activation(v, v, ACT.Gelu).then_inc(ge_a.sem, 1)
                units(act, body)

            def vector(dve):
                dve.wait_ge(ld_rows, 32)

                def body(j, u):
                    if ok(j):
                        e = dve.value_load(unit_e[0:1, bass.ds(j, 1)], min_val=0, max_val=E0 - 1)
                        for h in range(2):
                            dve.wait_ge(up_p.sem, up_p.at(j, f"h{h}"))
                            before(dve, tp_p.sem, tp_p.at(j - 2, "ab"[h]))
                            nc.vector.tensor_tensor(hid[:, u, h * 512:(h + 1) * 512], ps[up_banks[u][h]][:, :],
                                                    b1_sb[:, bass.ds(e, 1), h * 512:(h + 1) * 512].rearrange("p o f -> p (o f)"),
                                                    ALU.add).then_inc(b1_v.sem, 1)
                    if ok(j - 1):
                        for q, bank in ((0, 3), (1, 4)):
                            dve.wait_ge(tp_a.sem, tp_a.at(j - 1, "ab"[q]))
                            nc.vector.tensor_tensor(hT_lo[:, 4 * q:4 * q + 4, :].rearrange("p f t -> p (f t)"),
                                                    ps[bank][:, :], hT_hi[:, 4 * q:4 * q + 4, :].rearrange("p f t -> p (f t)"),
                                                    ALU.subtract).then_inc(tp_v.sem, 1)
                    if ok(j + 1):
                        dve.wait_ge(x_a.sem, x_a.at(j + 1, "hi"))
                        nc.vector.tensor_tensor(xT_lo[:, 1 - u, :, :].rearrange("p c t -> p (c t)"),
                                                ps[0][:, 0:D], xT_hi[:, 1 - u, :, :].rearrange("p c t -> p (c t)"),
                                                ALU.subtract).then_inc(x_v.sem, 1)
                    if ok(j - 1):
                        e = dve.value_load(unit_e[0:1, bass.ds(j - 1, 1)], min_val=0, max_val=E0 - 1)
                        dve.wait_ge(dn_p.sem, dn_p.at(j - 1, "y"))
                        before(dve, st_ys[1 - u], dma_at(j - 3, 1 - u) if not isinstance(j, int) or j >= 3 else 0)
                        nc.vector.tensor_tensor(yb[:, 1 - u, :], ps[5][:, 0:D],
                                                b2_sb[:, bass.ds(e, 1), :].rearrange("p o f -> p (o f)"), ALU.add)\
                            .then_inc(y_v.sem, 1)
                units(dve, body)
            return sync, tensor, scalar, vector, gpsimd

        ld_prep, ld_set, ld_slots = sem("ld_prep"), [sem(f"ld_set{i}") for i in range(SETS)], sem("ld_slots")
        prep_p, prep_v = sem("prep_p"), sem("prep_v")

        def prepare():
            def sync(sp):
                for n, name in enumerate(("dq", "dkT")):
                    sp.dma_start(prep_w[:, n].rearrange("p c d -> p (c d)"), a[name]).then_inc(ld_prep, 16)
                sp.dma_start(slotT, a["slotT"].rearrange("p (c s) -> p c s", c=C)).then_inc(ld_prep, 16)
                for n in range(SETS):
                    sp.dma_start(wset[:, n].rearrange("p e f -> p (e f)"), a["wset"][n]).then_inc(ld_set[n], 16)

            def tensor(pe):
                pe.wait_ge(ld_prep, 48)
                for m in range(C):
                    for c in range(C):
                        last = nc.tensor.matmul(ps[0][:, m * NS:(m + 1) * NS], prep_w[:, 0, c, m * P:(m + 1) * P],
                                                slotT[:, c, :], start=c == 0, stop=c == C - 1)
                last.then_inc(prep_p, 1)
                pe.wait_ge(prep_v, 3)
                for c in range(C):
                    for m in range(C):
                        last = nc.tensor.matmul(ps[1][:, c * D + m * P:c * D + (m + 1) * P],
                                                prep_w[:, 1, m, c * P:(c + 1) * P],
                                                qbd[:, m, :, :].rearrange("p h s -> p (h s)"), start=True, stop=True)
                last.then_inc(prep_p, 1)
                for m in range(C):
                    last = nc.tensor.matmul(ps[2][:, m:m + 1], qbd[:, m, :, :].rearrange("p h s -> p (h s)"),
                                            col["dbk"][:, m:m + 1], start=True, stop=True)
                last.then_inc(prep_p, 1)

            def vector(dve):
                nc.vector.memset(vz[:, :, :, 1, :], 0.0)
                dve.wait_ge(prep_p, 1)
                for m in range(C):
                    nc.vector.tensor_scalar(sqT[:, m, :], ps[0][:, m * NS:(m + 1) * NS], QSCALE, qcol[:, 1, m:m + 1],
                                            ALU.mult, ALU.add).then_inc(prep_v, 1)
                dve.wait_ge(prep_v, 2)
                nc.vector.tensor_tensor(qbd, sqT[:, :, None, :].to_broadcast([P, C, HC, NS]),
                                        cv["mask8"][:, None, :, None].to_broadcast([P, C, HC, NS]), ALU.mult)\
                    .then_inc(prep_v, 1)
                dve.wait_ge(prep_p, 3)
                nc.vector.tensor_copy(qa.rearrange("p c d -> p (c d)"), ps[1][:, :])
                nc.vector.tensor_copy(qac, ps[2][:, 0:C])
            return sync, tensor, None, vector, None

        def moe1():
            e_p, e_a, e_v, e_g = sem("m1_p"), sem("m1_a"), sem("m1_v"), sem("m1_g")
            set_used = sem("m1_set_used")
            T = E1 // 4
            FC = F1 // P
            pj = Track(e_p, ["o", "gb", "hT"], T)
            va = Track(e_v, ["o", "stats", "mean", "hat", "gain", "h"], T)
            aj = Track(e_a, ["hT"], T)
            gj = Track(e_g, ["var", "rstd"], T)
            pe2 = track("m1_p2", "u g ta tb y o2", T)
            ac2 = track("m1_a2", "u0 u1 g0 g1 ta o2", T)
            ve2 = track("m1_v2", "m0 m1 tb y", T)
            k_p, k_a = sem("m1_k_p"), sem("m1_k_a")

            def sync(sp):
                sp.dma_start(sel[0:E1].rearrange("p t r -> p (t r)"), a["sel"]).then_inc(ld_slots, 16)
                sp.dma_start(small[0:E1].rearrange("p n d -> p (n d)"), a["small"]).then_inc(ld_slots, 16)
                sp.dma_start(bias1[0:E1].rearrange("p n f -> p (n f)"), a["bias1"]).then_inc(ld_slots, 16)
                for n in range(SETS, 6 * T):
                    sp.wait_ge(set_used, n - SETS + 1)
                    sp.dma_start(wset[:, n % SETS].rearrange("p e f -> p (e f)"), a["wset"][n])\
                        .then_inc(ld_set[n % SETS], 16)

            def tensor(pe):
                pe.wait_ge(ld_slots, 48)
                for t in range(T):
                    before(pe, va.sem, va.at(t - 1, "o"))
                    nc.tensor.matmul(ps[0][:, 0:D], sel[0:E1, t, :], small[0:E1, 0, :], start=True, stop=False)
                    for m in range(C):
                        last = nc.tensor.matmul(ps[0][:, 0:D], oT_all[:, m, 4 * t:4 * t + 4, :], w["do"][:, m, :],
                                                start=False, stop=m == C - 1)
                    last.then_inc(e_p, 1)
                    before(pe, va.sem, va.at(t - 1, "h"))
                    for n in range(2):
                        last = nc.tensor.matmul(ps[2][:, n * D:(n + 1) * D], sel[0:E1, t, :], small[0:E1, 1 + n, :],
                                                start=True, stop=True)
                    last.then_inc(e_p, 1)
                    pe.wait_ge(va.sem, va.at(t, "h"))
                    before(pe, aj.sem, aj.at(t - 1, "hT"))
                    for c in range(C):
                        last = nc.tensor.transpose(ps[3][:, c * P:(c + 1) * P], hrow[:, c * P:(c + 1) * P], cv["ident"])
                    last.then_inc(e_p, 1)
                pe.wait_ge(aj.sem, aj.at(T - 1, "hT"))
                n = 0
                for t in range(T):
                    for mat, banks in ((0, (4, 5)), (1, (6, 7))):
                        for h in range(2):
                            before(pe, ac2.sem, ac2.at(t - 1, f"{'ug'[mat]}{h}"))
                            nc.tensor.matmul(ps[banks[h]][:, :], sel[0:E1, t, :], bias1[0:E1, mat, h * 512:(h + 1) * 512],
                                             start=True, stop=False, skip_group_check=True)
                        for c in range(C):
                            pe.wait_ge(ld_set[n % SETS], 16 * (n // SETS + 1))
                            for h in range(2):
                                for e in range(4):
                                    last = nc.tensor.matmul(ps[banks[h]][32 * e:32 * e + 32, :],
                                                            hT[:, c, t, 32 * e:32 * e + 32],
                                                            wset[:, n % SETS, e, h * 512:(h + 1) * 512],
                                                            start=False, stop=c == C - 1, skip_group_check=True)
                            if c == C - 1:
                                last.then_inc(pe2.sem, 1)
                                pe.wait_ge(pe2.sem, pe2.at(t, "ug"[mat]))
                                pe.sem_inc(set_used, 1)
                            else:
                                last.then_inc(set_used, 1)
                            n += 1
                    for q in range(2):
                        pe.wait_ge(ve2.sem, ve2.at(t, f"m{q}"))
                        if q == 0:
                            before(pe, ac2.sem, ac2.at(t - 1, "ta"))
                        else:
                            before(pe, ve2.sem, ve2.at(t - 1, "tb"))
                        for f in range(4):
                            last = nc.tensor.transpose(ps[2 + q][:, f * P:(f + 1) * P],
                                                       us[:, (4 * q + f) * P:(4 * q + f + 1) * P], cv["ident"])
                        last.then_inc(pe2.sem, 1)
                    before(pe, ve2.sem, ve2.at(t - 1, "y"))
                    nc.tensor.matmul(ps[1][:, 0:D], sel[0:E1, t, :], small[0:E1, 3, :],
                                     start=True, stop=False, skip_group_check=True)
                    for q in range(2):
                        pe.wait_ge(ac2.sem, ac2.at(t, "ta"))
                        if q == 1:
                            pe.wait_ge(ve2.sem, ve2.at(t, "tb"))
                        pe.wait_ge(ld_set[n % SETS], 16 * (n // SETS + 1))
                        for f in range(4):
                            for e in range(4):
                                last = nc.tensor.matmul(ps[1][32 * e:32 * e + 32, 0:D],
                                                        ugT[:, 4 * q + f, 32 * e:32 * e + 32],
                                                        wset[:, n % SETS, e, f * D:(f + 1) * D],
                                                        start=False, stop=q == 1 and f == 3, skip_group_check=True)
                        if q == 1:
                            last.then_inc(pe2.sem, 1)
                            pe.wait_ge(pe2.sem, pe2.at(t, "y"))
                            pe.sem_inc(set_used, 1)
                        else:
                            last.then_inc(set_used, 1)
                        n += 1
                    pe.wait_ge(ve2.sem, ve2.at(t, "y"))
                    before(pe, ac2.sem, ac2.at(t - 1, "o2"))
                    for c in range(C):
                        last = nc.tensor.transpose(ps[0][:, c * P:(c + 1) * P], orow[:, t, c * P:(c + 1) * P], cv["ident"])
                    last.then_inc(pe2.sem, 1)
                pe.wait_ge(ac2.sem, ac2.at(T - 1, "o2"))
                for m in range(C):
                    for c in range(C):
                        last = nc.tensor.matmul(ps[6 + m][:, :], w["ck"][:, c, m * P:(m + 1) * P],
                                                oT2[:, c, :, :].rearrange("p s b -> p (s b)"),
                                                start=c == 0, stop=c == C - 1)
                    last.then_inc(k_p, 1)

            def scalar(act):
                for t in range(T):
                    act.wait_ge(pj.sem, pj.at(t, "hT"))
                    nc.scalar.copy(hT[:, :, t, :], ps[3][:, 0:D].rearrange("p (c r) -> p c r", c=C)).then_inc(e_a, 1)
                for t in range(T):
                    for mat, banks, dst in ((0, (4, 5), us), (1, (6, 7), gs)):
                        act.wait_ge(pe2.sem, pe2.at(t, "ug"[mat]))
                        if mat == 0:
                            before(act, pe2.sem, pe2.at(t - 1, "tb"))
                        for h in range(2):
                            nc.scalar.activation(dst[:, h * 512:(h + 1) * 512], ps[banks[h]][:, :], ACT.Silu)\
                                .then_inc(ac2.sem, 1)
                    act.wait_ge(pe2.sem, pe2.at(t, "ta"))
                    before(act, pe2.sem, pe2.at(t - 1, "y"))
                    nc.scalar.copy(ugT[:, 0:4, :].rearrange("p f r -> p (f r)"), ps[2][:, :]).then_inc(ac2.sem, 1)
                    act.wait_ge(pe2.sem, pe2.at(t, "o2"))
                    nc.scalar.copy(oT2[:, :, 4 * t:4 * t + 4, :].rearrange("p c s b -> p c (s b)"),
                                   ps[0][:, 0:D].rearrange("p (c r) -> p c r", c=C)).then_inc(ac2.sem, 1)
                for m in range(C):
                    act.wait_ge(k_p, m + 1)
                    nc.scalar.activation(kTall[:, m, :, :].rearrange("p s b -> p (s b)"), ps[6 + m][:, :], ACT.Identity,
                                         bias=col["cbk"][:, m:m + 1])

            def vector(dve):
                for t in range(T):
                    dve.wait_ge(pj.sem, pj.at(t, "o"))
                    nc.vector.tensor_tensor(orow[:, t, :], ps[0][:, 0:D], row["dbo"], ALU.add).then_inc(e_v, 1)
                    dve.wait_ge(va.sem, va.at(t, "o"))
                    settled(dve)
                    nc.vector.bn_stats(st1, orow[:, t, :]).then_inc(e_v, 1)
                    dve.wait_ge(va.sem, va.at(t, "stats"))
                    settled(dve)
                    nc.vector.bn_aggr(mv1, st1).then_inc(e_v, 1)
                    dve.wait_ge(gj.sem, gj.at(t, "rstd"))
                    before(dve, pj.sem, pj.at(t - 1, "hT"))
                    nc.vector.tensor_scalar(hrow, orow[:, t, :], mv1[:, 0:1], rs1[:, 1:2], ALU.subtract, ALU.mult)\
                        .then_inc(e_v, 1)
                    dve.wait_ge(va.sem, va.at(t, "hat"))
                    dve.wait_ge(pj.sem, pj.at(t, "gb"))
                    nc.vector.tensor_tensor(hrow, ps[2][:, 0:D], hrow, ALU.mult).then_inc(e_v, 1)
                    dve.wait_ge(va.sem, va.at(t, "gain"))
                    nc.vector.tensor_tensor(hrow, ps[2][:, D:2 * D], hrow, ALU.add).then_inc(e_v, 1)
                for t in range(T):
                    for q in range(2):
                        dve.wait_ge(ac2.sem, ac2.at(t, f"g{q}"))
                        v = us[:, q * 512:(q + 1) * 512]
                        nc.vector.tensor_tensor(v, v, gs[:, q * 512:(q + 1) * 512], ALU.mult).then_inc(ve2.sem, 1)
                    dve.wait_ge(pe2.sem, pe2.at(t, "tb"))
                    before(dve, pe2.sem, pe2.at(t - 1, "y"))
                    nc.vector.tensor_copy(ugT[:, 4:8, :].rearrange("p f r -> p (f r)"), ps[3][:, :]).then_inc(ve2.sem, 1)
                    dve.wait_ge(pe2.sem, pe2.at(t, "y"))
                    nc.vector.tensor_tensor(orow[:, t, :], ps[1][:, 0:D], orow[:, t, :], ALU.add).then_inc(ve2.sem, 1)

            def gpsimd(pool):
                for t in range(T):
                    pool.wait_ge(va.sem, va.at(t, "mean"))
                    nc.gpsimd.tensor_tensor(rs1[:, 0:1], mv1[:, 1:2], eps_sb[:, :], ALU.add).then_inc(e_g, 1)
                    pool.wait_ge(gj.sem, gj.at(t, "var"))
                    nc.gpsimd.tensor_tensor(rs1[:, 1:2], rs1[:, 0:1], mhalf[:, :], ALU.pow).then_inc(e_g, 1)
            return sync, tensor, scalar, vector, gpsimd

        def combine():
            n = "c_"
            ld_x3 = [sem(n + "ld_x3_0"), sem(n + "ld_x3_1")]
            st_out = [sem(n + "st_out0"), sem(n + "st_out1")]
            qv_p = track(n + "qv_p", "q v")
            s_p = track(n + "s_p", "s")
            t_p = track(n + "t_p", "pT av")
            o_p = track(n + "o_p", "o")
            q_a = track(n + "q_a", "q")
            t_a = track(n + "t_a", "pT aT")
            e_a = track(n + "e_a", "e")
            p_v = track(n + "p_v", "sum rs pn")
            s_v = track(n + "s_v", "v max sub")
            o_v = track(n + "o_v", "t out")
            k_g = track(n + "k_g", "rep kb")
            v_g = track(n + "v_g", "vbd")
            steady = (2, B - 2)

            def sync(sp):
                for u in range(2):
                    sp.dma_start(x3l[:, u].rearrange("p c t -> p (c t)"), x3T_dram[u]).then_inc(ld_x3[u], 16)

                def body(k, u):
                    if valid(k + 2) and (not isinstance(k, int) or k >= 0):
                        sp.wait_ge(qv_p.sem, qv_p.at(k, "q"))
                        sp.dma_start(x3l[:, u].rearrange("p c t -> p (c t)"), x3T_dram[k + 2]).then_inc(ld_x3[u], 16)
                    if valid(k - 2):
                        sp.wait_ge(o_v.sem, o_v.at(k - 2, "out"))
                        sp.dma_start(out[k - 2], cout[:, u, :]).then_inc(st_out[u], 16)
                pipeline(sp, body, 0, B + 2, steady)
                for s in st_out:
                    sp.wait_ge(s, 8 * B)

            def tensor(pe):
                def body(k, u):
                    if valid(k):
                        pe.wait_ge(ld_x3[u], dma_at(k, u))
                        before(pe, q_a.sem, q_a.at(k - 1, "q"))
                        for m in range(C):
                            for c in range(C):
                                last = nc.tensor.matmul(ps[0][:, m * P:(m + 1) * P], w["cq"][:, c, m * P:(m + 1) * P],
                                                        x3l[:, u, c, :], start=c == 0, stop=c == C - 1)
                        last.then_inc(qv_p.sem, 1)
                        pe.wait_ge(k_g.sem, k_g.at(k, "rep"))
                        before(pe, s_v.sem, s_v.at(k - 1, "v"))
                        for c in range(C):
                            last = nc.tensor.matmul(ps[1][:, 0:D], orep[:, u, c, :, :].rearrange("p h s -> p (h s)"),
                                                    w["cv"][:, c, :], start=c == 0, stop=c == C - 1)
                        last.then_inc(qv_p.sem, 1)
                    if valid(k - 1):
                        pe.wait_ge(p_v.sem, p_v.at(k - 1, "pn"))
                        before(pe, t_a.sem, t_a.at(k - 2, "pT"))
                        for c in range(C):
                            last = nc.tensor.transpose(ps[3][:, c * P:(c + 1) * P], cpn[:, c * P:(c + 1) * P], cv["ident"])
                        last.then_inc(t_p.sem, 1)
                    if valid(k):
                        pe.wait_ge(q_a.sem, q_a.at(k, "q"))
                        pe.wait_ge(k_g.sem, k_g.at(k, "kb"))
                        before(pe, s_v.sem, s_v.at(k - 1, "sub"))
                        for m in range(C):
                            last = nc.tensor.matmul(ps[2][:, m * P:(m + 1) * P], cqT[:, u, m, :],
                                                    ckb[:, u, m, :, :].rearrange("p h s -> p (h s)"), start=True, stop=True)
                        last.then_inc(s_p.sem, 1)
                    if valid(k - 1):
                        pe.wait_ge(t_a.sem, t_a.at(k - 1, "pT"))
                        pe.wait_ge(v_g.sem, v_g.at(k - 1, "vbd"))
                        before(pe, t_a.sem, t_a.at(k - 2, "aT"))
                        for m in range(C):
                            last = nc.tensor.matmul(ps[4][:, m * P:(m + 1) * P], cvbd[:, 1 - u, m, :], cpT[:, m, :],
                                                    start=True, stop=True)
                        last.then_inc(t_p.sem, 1)
                        pe.wait_ge(t_a.sem, t_a.at(k - 1, "aT"))
                        before(pe, o_v.sem, o_v.at(k - 2, "t"))
                        for c in range(C):
                            last = nc.tensor.matmul(ps[5][:, 0:D], caT[:, c, :], w["co"][:, c, :],
                                                    start=c == 0, stop=c == C - 1)
                        last.then_inc(o_p.sem, 1)
                pipeline(pe, body, 0, B + 1, steady)

            def scalar(act):
                def body(k, u):
                    if valid(k):
                        act.wait_ge(qv_p.sem, qv_p.at(k, "q"))
                        before(act, s_p.sem, s_p.at(k - 2, "s"))
                        for c in range(C):
                            last = nc.scalar.activation(cqT[:, u, c, :], ps[0][:, c * P:(c + 1) * P], ACT.Identity,
                                                        bias=qcol[:, 2, c:c + 1], scale=QSCALE)
                        last.then_inc(q_a.sem, 1)
                    if valid(k - 1):
                        act.wait_ge(t_p.sem, t_p.at(k - 1, "pT"))
                        nc.scalar.copy(cpT.rearrange("p c t -> p (c t)"), ps[3][:, 0:D]).then_inc(t_a.sem, 1)
                        act.wait_ge(t_p.sem, t_p.at(k - 1, "av"))
                        before(act, o_p.sem, o_p.at(k - 2, "o"))
                        nc.scalar.copy(caT.rearrange("p c t -> p (c t)"), ps[4][:, 0:D]).then_inc(t_a.sem, 1)
                    if valid(k):
                        act.wait_ge(s_v.sem, s_v.at(k, "sub"))
                        nc.scalar.activation(csc[:, u, :], csc[:, u, :], ACT.Exp).then_inc(e_a.sem, 1)
                pipeline(act, body, 0, B + 1, steady)

            def vector(dve):
                def heads(v):
                    return v.rearrange("p (h s) -> p h s", h=H)

                def body(k, u):
                    if valid(k - 1):
                        i = k - 1
                        e = csc[:, 1 - u, :]
                        dve.wait_ge(e_a.sem, e_a.at(i, "e"))
                        nc.vector.tensor_reduce(csm, heads(e), AX, ALU.add).then_inc(p_v.sem, 1)
                        dve.wait_ge(p_v.sem, p_v.at(i, "sum"))
                        nc.vector.reciprocal(csm, csm).then_inc(p_v.sem, 1)
                        dve.wait_ge(p_v.sem, p_v.at(i, "rs"))
                        before(dve, t_p.sem, t_p.at(i - 1, "pT"))
                        nc.vector.tensor_tensor(heads(cpn), heads(e), csm[:, :, None].to_broadcast([P, H, NS]), ALU.mult)\
                            .then_inc(p_v.sem, 1)
                    if valid(k):
                        dve.wait_ge(qv_p.sem, qv_p.at(k, "v"))
                        before(dve, v_g.sem, v_g.at(k - 2, "vbd"))
                        nc.vector.tensor_tensor(cvb[:, u, :], ps[1][:, 0:D], row["cbv"], ALU.add).then_inc(s_v.sem, 1)
                        dve.wait_ge(s_p.sem, s_p.at(k, "s"))
                        nc.vector.tensor_reduce(cmx, heads(ps[2][:, 0:D]), AX, ALU.max).then_inc(s_v.sem, 1)
                        dve.wait_ge(s_v.sem, s_v.at(k, "max"))
                        nc.vector.tensor_tensor(heads(csc[:, u, :]), heads(ps[2][:, 0:D]),
                                                cmx[:, :, None].to_broadcast([P, H, NS]), ALU.subtract).then_inc(s_v.sem, 1)
                    if valid(k - 2):
                        i = k - 2
                        dve.wait_ge(o_p.sem, o_p.at(i, "o"))
                        before(dve, o_v.sem, o_v.at(i - 1, "out"))
                        nc.vector.tensor_tensor(ctmp, ps[5][:, 0:D], row["cbo"], ALU.add).then_inc(o_v.sem, 1)
                        dve.wait_ge(o_v.sem, o_v.at(i, "t"))
                        before(dve, st_out[u], dma_at(k - 4, u) if not isinstance(k, int) or k >= 4 else 0)
                        nc.vector.scalar_tensor_tensor(out=cout[:, u, :], in0=ctmp, scalar=tg[:, 3:4], in1=x_all[:, i],
                                                       op0=ALU.mult, op1=ALU.add).then_inc(o_v.sem, 1)
                pipeline(dve, body, 0, B + 2, steady)

            def gpsimd(pool):
                def slots(i, u):
                    before(pool, qv_p.sem, qv_p.at(i - 2, "v"))
                    for c in range(C):
                        last = nc.gpsimd.tensor_copy(orep[:, u, c], oT2[:, c, None, :, i].to_broadcast([P, HC, NS]))
                    last.then_inc(k_g.sem, 1)
                    before(pool, s_p.sem, s_p.at(i - 2, "s"))
                    nc.gpsimd.tensor_tensor(ckb[:, u], kTall[:, :, None, :, i].to_broadcast([P, C, HC, NS]),
                                            cv["mask8"][:, None, :, None].to_broadcast([P, C, HC, NS]), ALU.mult)\
                        .then_inc(k_g.sem, 1)

                def body(k, u):
                    if valid(k + 1):
                        slots(k + 1, 1 - u)
                    if valid(k):
                        pool.wait_ge(s_v.sem, s_v.at(k, "v"))
                        before(pool, t_p.sem, t_p.at(k - 2, "av"))
                        nc.gpsimd.tensor_tensor(cvbd[:, u].rearrange("p c (h d) -> p c h d", h=HC),
                                                cvb[:, u, :].rearrange("p (c h d) -> p c h d", c=C, h=HC),
                                                cv["mask8"][:, None, :, None].to_broadcast([P, C, HC, DH]), ALU.mult)\
                            .then_inc(v_g.sem, 1)
                pipeline(pool, body, -1, B, steady)
            return sync, tensor, scalar, vector, gpsimd

        def setup():
            def sync(sp):
                sp.dma_start(x_all[:, 0], a["x"][0]).then_inc(ld_x[0], 16)
                sp.dma_start(x_all[:, 1], a["x"][1]).then_inc(ld_x[1], 16)
                for dst, src in ((const[:, :], a["const"]),
                                 (w_sb[:, 0:4].rearrange("p n c d -> p (n c d)"), a["weights"][:, 0:4 * C * D]),
                                 (col_sb[:, :, :].rearrange("p n c -> p (n c)"), a["cols"]),
                                 (wg_sb[:, :, :].rearrange("p c e -> p (c e)"), a["wg"]),
                                 (row_sb[:, :, :].rearrange("p n d -> p (n d)"), a["rows"].partition_broadcast(P)),
                                 (bg_sb[:, :], a["bg"].partition_broadcast(P)),
                                 (gates[:, :], a["gates"].partition_broadcast(P))):
                    sp.dma_start(dst, src).then_inc(ld_const, 16)

            def vector(dve):
                nc.vector.memset(zero[:, :], 0.0).then_inc(setup_v, 1)
                nc.vector.memset(ones[:, :], 1.0).then_inc(setup_v, 1)
                nc.vector.memset(eps_sb[:, :], EPS)
                for part in range(3):
                    nc.vector.memset(one_zero[:, part, :], 1.0 if part != 1 else 0.0)
                nc.vector.memset(mhalf[:, :], -0.5)
                nc.vector.memset(vz[:, :, :, 1, :], 0.0)
                dve.wait_ge(ld_const, 16 * 7)
                for n, name in enumerate(("bq0", "dbq", "cbq")):
                    nc.vector.tensor_scalar(qcol[:, n, :], col[name], QSCALE, None, ALU.mult)
                dve.wait_ge(setup_v, 2)
                for c in range(C):
                    last = nc.vector.tensor_scalar(pr[:, 0, c, 0:P], ones[:, :], col["bv0"][:, c:c + 1], None, ALU.mult)
                last.then_inc(setup_v, 1)
                dve.wait_ge(setup_p, 1)
                nc.vector.tensor_tensor(row["bo0"], ps[0][:, 0:D], row["bo0"], ALU.add).then_inc(setup_v, 1)
                dve.wait_ge(setup_v, 4)
                dve.wait_ge(setup_a, 1)
                nc.vector.tensor_scalar(row["bo0"], row["bo0"], tg[:, 0:1], None, ALU.mult)

            def tensor(pe):
                pe.wait_ge(setup_v, 3)
                pe.wait_ge(ld_const, 16 * 7)
                for c in range(C):
                    last = nc.tensor.matmul(ps[0][:, 0:D], pr[:, 0, c, 0:P], w["o0"][:, c, :], start=c == 0, stop=c == C - 1)
                last.then_inc(setup_p, 1)

            def scalar(act):
                act.wait_ge(ld_const, 16 * 7)
                nc.scalar.activation(tg[:, :], gates[:, :], ACT.Tanh).then_inc(setup_a, 1)
            return sync, tensor, scalar, vector, None

        def run(programs):
            with nc.Block() as block:
                sync, tensor, scalar, vector, gpsimd = programs
                if sync:
                    block.sync(lambda e: sync(e))
                if tensor:
                    block.tensor(lambda e: tensor(e))
                if scalar:
                    block.scalar(lambda e: scalar(e))
                if vector:
                    block.vector(lambda e: vector(e))
                if gpsimd:
                    block.gpsimd(lambda e: gpsimd(e))

        run(setup())
        run(attention(0))
        run(routing())
        run(moe0())
        run(prepare())
        run(attention(1))
        run(moe1())
        run(combine())


def arrange(i):
    f = {k: np.ascontiguousarray(v) for k, v in i.items()}

    def chunks(m):
        return m.reshape(-1, P, m.shape[-1]).transpose(1, 0, 2).reshape(P, -1)

    p = "L1_ffn_"
    squares = [f["L0_xattn_w_q"], f["L0_xattn_w_k"], f["L0_xattn_w_v"], f["L0_xattn_w_o"],
               f["L1_xattn_Wq"].T, f["L1_xattn_Wk"].T, f["L1_xattn_Wv"].T, f["L1_xattn_Wo"].T,
               f[p + "d_Wv"], f[p + "d_Wo"], f[p + "c_Wq"], f[p + "c_Wk"], f[p + "c_Wv"], f[p + "c_Wo"]]
    rows = [f["L0_xattn_b_o"], f["L0_ffn_gamma"], f["L0_ffn_beta"],
            f[p + "d_bv"], f[p + "d_bo"], f[p + "c_bv"], f[p + "c_bo"]]
    cols = [f["L0_xattn_b_q"], f["L0_xattn_b_k"], f["L0_xattn_b_v"], f[p + "d_bq"], f[p + "d_bk"], f[p + "c_bq"], f[p + "c_bk"]]
    t = np.arange(P)
    const = np.concatenate([np.eye(P), t[:, None] < t[None, :], t[:, None] // DH == np.arange(HC),
                            np.broadcast_to(np.arange(E0), (P, E0)), np.broadcast_to(P * np.arange(B), (P, B)),
                            np.broadcast_to(np.arange(UNITS), (P, UNITS))], axis=1).astype(np.float32)
    w12 = np.concatenate([
        f["L0_ffn_W1"].transpose(0, 2, 1).reshape(E0, C, P, F0).transpose(0, 2, 1, 3).reshape(E0, P, C * F0),
        f["L0_ffn_W2"].transpose(0, 2, 1).reshape(E0, F0 // P, P, D).transpose(0, 2, 1, 3).reshape(E0, P, -1)], axis=2)
    r = np.arange(P)
    sel = np.concatenate([4 * t4 + r[None, :] // B == np.arange(E1)[:, None] for t4 in range(E1 // 4)], axis=1)
    small = [f[p + "slot_query"][0], f[p + "e_ln_g"], f[p + "e_ln_b"], f[p + "e_b2"]]
    sets = []
    for t4 in range(E1 // 4):
        for m in (f[p + "e_W1"], f[p + "e_Wg"]):
            for c in range(C):
                sets.append(m[4 * t4:4 * t4 + 4, c * P:(c + 1) * P, :].transpose(1, 0, 2).reshape(P, -1))
        for q in range(2):
            m = f[p + "e_W2"][4 * t4:4 * t4 + 4, 512 * q:512 * (q + 1), :].reshape(4, 4, P, D)
            sets.append(m.transpose(2, 0, 1, 3).reshape(P, -1))
    s = {
        "dq": chunks(f[p + "d_Wq"]), "dkT": chunks(f[p + "d_Wk"].T),
        "slotT": f[p + "slot_query"][0].T.reshape(C, P, NS).transpose(1, 0, 2).reshape(P, -1),
        "sel": sel.astype(np.float32), "small": np.concatenate(small, axis=1),
        "bias1": np.concatenate([f[p + "e_b1"], f[p + "e_bg"]], axis=1), "wset": np.stack(sets),
        "x": f["x"], "ctxT": f["ctx_1024"].reshape(B, P, C, P).transpose(0, 3, 2, 1).reshape(B, P, C * P),
        "fside": f["fside_BxS2_0"], "gates": np.concatenate([f["g_xattn"], f["g_ffn"]]).reshape(1, 4),
        "weights": np.concatenate([chunks(m) for m in squares], axis=1),
        "rows": np.stack(rows).reshape(1, -1), "cols": np.stack(cols).reshape(-1, P).T,
        "wg": chunks(f["L0_ffn_Wg"].T), "bg": f["L0_ffn_bg"].reshape(1, E0), "const": const,
        "w12": w12, "b1": f["L0_ffn_b1"].reshape(1, -1), "b2": f["L0_ffn_b2"].reshape(1, -1),
    }
    return {k: np.ascontiguousarray(v) for k, v in s.items()}


def kernel(**inputs):
    from concourse import bacc
    from concourse.bass_utils import run_bass_kernel_spmd

    nc = bacc.Bacc("TRN2", target_bir_lowering=False, num_devices=1)
    arrays = {f"{name}_dram": v for name, v in arrange(inputs).items()}
    given = {name[:-5]: nc.dram_tensor(name, v.shape, mybir.dt.from_np(v.dtype), kind="ExternalInput").ap()
             for name, v in arrays.items()}
    out = nc.dram_tensor("out_dram", (B, P, D), F32, kind="ExternalOutput").ap()
    build(nc, given, out)
    result = run_bass_kernel_spmd(nc, [arrays], core_ids=[0])
    return result.results[0]["out_dram"]
```

```python
from contextlib import ExitStack

import numpy as np
import concourse.bass as bass
from concourse import mybir

ALU = mybir.AluOpType
ACT = mybir.ActivationFunctionType
AX = mybir.AxisListType.X
F32 = mybir.dt.float32
I32 = mybir.dt.int32
U32 = mybir.dt.uint32
F32R = mybir.dt.float32r

P = 128
B, D, H = 32, 256, 16
DH = D // H
C = D // P
HC = H // C
G = 4
E0, F0 = 8, 1024
E1, F1, NS = 16, 1024, 16
UNITS = 2 * B + E0
RING = 2
SETS = 3
TOKENS = B * P
DUMP = E0 * TOKENS
ARENA = 34168
EPS = 1e-5
QSCALE = 0.25

CONSTS = {"ident": 128, "tri": 128, "mask8": 8, "iota8": 8, "thr": 32, "iotau": UNITS, "first": 8, "part": 1}
WEIGHTS = ["q0", "k0", "v0", "o0", "q1", "k1", "v1", "o1", "dv", "do", "cq", "ck", "cv", "co"]
ROWS = ["bo0", "gamma", "beta", "dbv", "dbo", "cbv", "cbo"]
COLS = ["bq0", "bk0", "bv0", "dbq", "dbk", "cbq", "cbk"]


class Track:

    def __init__(self, sem, steps, items, base=0):
        self.sem, self.steps, self.items, self.base = sem, steps, items, base

    def at(self, item, step):
        if isinstance(item, int):
            item = min(item, self.items - 1)
        return item * len(self.steps) + (self.steps.index(step) + 1 + self.base)


def build(nc, a, out):
    ctx = ExitStack()
    with ctx:
        def sb(name, shape, dt=F32):
            return ctx.enter_context(nc.sbuf_tensor(name, shape, dt))

        def sem(name):
            return ctx.enter_context(nc.semaphore(name))

        def track(name, steps, items=B, base=0):
            return Track(sem(name), steps.split(), items, base)

        x_all = sb("x_all", [P, B, D])
        w_sb = sb("w_sb", [P, len(WEIGHTS), C, D])
        row_sb = sb("row_sb", [P, len(ROWS), D])
        col_sb = sb("col_sb", [P, len(COLS), C])
        const = sb("const", [P, sum(CONSTS.values())])
        wg_sb = sb("wg_sb", [P, C, E0])
        bg_sb = sb("bg_sb", [P, E0])
        gates = sb("gates", [P, 4])
        tg = sb("tg", [P, 4])
        qcol = sb("qcol", [P, 3, C])
        eps_sb = sb("eps_sb", [P, 1])
        mhalf = sb("mhalf", [P, 1])
        ones = sb("ones", [P, P])
        one_zero = sb("one_zero", [P, 3, DH])
        top_val = sb("top_val", [P, B, 8])
        top_idx = sb("top_idx", [P, B, 2])
        top8 = sb("top8", [P, 8])
        idx8 = sb("idx8", [P, 8], U32)
        slot_f = sb("slot_f", [P, 2, B])
        slot_i = sb("slot_i", [P, 2, B], I32)
        next_row = sb("next_row", [P, E0])
        wts = sb("wts", [P, 2, B])
        unit_e = sb("unit_e", [1, UNITS], I32)
        unit_s = sb("unit_s", [1, UNITS], I32)
        cend_i = sb("cend_i", [1, E0], I32)
        zero = sb("zero", [P, D])
        arena_at = nc.sbuf_base
        arena = sb("arena", [P, ARENA])
        cv = {}
        at = 0
        for n, w in CONSTS.items():
            cv[n] = const[:, at:at + w]
            at += w
        w = {n: w_sb[:, i] for i, n in enumerate(WEIGHTS)}
        row = {n: row_sb[:, i] for i, n in enumerate(ROWS)}
        col = {n: col_sb[:, i] for i, n in enumerate(COLS)}

        place = [0]

        def carve(*shape):
            n = int(np.prod(shape))
            v = arena[:, place[0]:place[0] + n]
            place[0] += n
            if len(shape) > 1:
                names = [f"d{i}" for i in range(len(shape))]
                v = v.rearrange(f"p ({' '.join(names)}) -> p {' '.join(names)}", **dict(zip(names[1:], shape[1:])))
            return v

        def rounded(name, first, *shape):
            return nc.alloc_sbuf_tensor_at(name, [P, *shape], F32R, offset=arena_at + 4 * first)

        ctxT = carve(2, C, P)
        xh = carve(2, D)
        xT = carve(C, P)
        kT = carve(C, P)
        qT = carve(2, C, P)
        kbd = carve(2 * C, HC, P)
        pr = carve(2, G, 512)
        pT = carve(2, 512)
        vz = carve(2, H // 2, 3, DH)
        aT = carve(C, P)
        rden = carve(C, P)
        xo = carve(D)
        xh3 = carve(D)
        xg = xh3
        xnT = carve(C, P)
        xc = carve(D)
        stat = carve(3, 6)
        mv = carve(3, 2)
        rstd = carve(3, 2)
        mx = carve(2, G)
        lg = carve(E0)
        oh2 = carve(2, E0)
        ohp2 = carve(2, E0)
        both = carve(E0)
        pos2 = carve(E0)
        posf2 = carve(2)
        xkeep = carve(2, D)
        idx_put = carve(2, 2).bitcast(I32)
        place[0] += -place[0] % 8
        attention_end = place[0]
        ring_lo = rounded("ring_lo", place[0], RING, 2 * C * F0)
        ring_raw = carve(RING, 2 * C * F0)
        place_hi = place[0]
        ring_hi = rounded("ring_hi", place[0], RING, 2 * C * F0)
        carve(RING, 2 * C * F0)
        ring_end = place[0]
        place[0] = ring_end
        hid = carve(2, F0)
        xT_hi = rounded("xT_hi", place[0], 2, C, P)
        carve(2, C, P)
        xT_lo = rounded("xT_lo", place[0], 2, C, P)
        carve(2, C, P)
        assert place[0] <= ARENA, place[0]
        place[0] = 0
        b1_sb = carve(E0, F0)
        b2_sb = carve(E0, D)
        moe_rows_end = place[0]
        xs = carve(2, D)
        yb = carve(2, D)
        hT_hi = rounded("hT_hi", place[0], F0 // P, P)
        carve(F0 // P, P)
        hT_lo = rounded("hT_lo", place[0], F0 // P, P)
        carve(F0 // P, P)
        assert place[0] <= attention_end, place[0]
        place[0] = moe_rows_end
        cnt = carve(E0)
        blk = carve(E0, B)
        nblk = carve(E0)
        cend = carve(E0)
        lim = carve(E0)
        tail = carve(E0)
        past = carve(E0)
        inside = carve(E0)
        tail_i = carve(E0).bitcast(I32)
        shift = carve(E0)
        ucmp = carve(UNITS, E0)
        uexp = carve(UNITS)
        ustart = carve(UNITS)
        used = carve(UNITS)
        ohb = carve(B, E0)
        off = carve(B)
        ex = carve(B, 8)
        zs = carve(B)
        s2 = carve(B)
        den = carve(B)
        rr = carve(B)
        assert place[0] <= attention_end, (place[0], attention_end)
        place[0] = attention_end
        wset = carve(SETS, 4, F1)
        oT_all = carve(C, NS, B)
        layer1_shared_end = place[0]
        yg = carve(2, 2, D)
        idx_cur = carve(2, 2).bitcast(I32)
        fs = carve(2, P)
        sbias = carve(2, 512)
        dVb = carve(2, D)
        sc = carve(C, P)
        pn = carve(C, P)
        pnT = carve(C, P)
        mk = carve(C, HC, NS)
        smx = carve(2)
        snx = carve(2)
        sz = carve(2)
        srz = carve(2)
        qa = carve(C, D)
        qac = carve(C)
        x3T = carve(C, P)
        assert place[0] <= ARENA, place[0]
        prep_w = pr.rearrange("p u g t -> p (u g t)")[:, 0:2 * C * D].rearrange("p (n c d) -> p n c d", n=2, c=C)
        slotT = ctxT[:, 0, 0, 0:C * NS].rearrange("p (c s) -> p c s", c=C)
        sqT = ctxT[:, 0, 1, 0:C * NS].rearrange("p (c s) -> p c s", c=C)
        qbd = kbd[:, 0:C, 0, :].rearrange("p c (h s) -> p c h s", h=HC)
        place[0] = 0
        sel = carve(4, P)
        small = carve(4, D)
        bias1 = carve(2, F1)
        orow = carve(4, D)
        hrow = carve(D)
        hT = carve(C, 4, P)
        us = carve(F1)
        gs = carve(F1)
        ugT = carve(F1 // P, P)
        oT2 = carve(C, NS, B)
        kTall = carve(C, NS, B)
        st1 = carve(6)
        mv1 = carve(2)
        rs1 = carve(2)
        slots_end = place[0]
        assert slots_end <= attention_end, (slots_end, attention_end)
        place[0] = attention_end
        x3l = carve(2, C, P)
        cqT = carve(2, C, P)
        orep = carve(2, C, HC, NS)
        ckb = carve(2, C, HC, NS)
        cvb = carve(2, D)
        cvbd = carve(2, C, P)
        csc = carve(2, D)
        cpn = carve(D)
        cpT = carve(C, P)
        caT = carve(C, P)
        ctmp = carve(D)
        cout = carve(2, D)
        cmx = carve(H)
        csm = carve(H)
        assert place[0] <= layer1_shared_end

        ps = [ctx.enter_context(nc.psum_tensor(f"ps{i}", [P, 512], F32)) for i in range(8)]

        xs_dram = nc.dram_tensor("xs_rows", (DUMP + E0 * P, D), F32, kind="Internal").ap()
        x3T_dram = nc.dram_tensor("x3_transposed", (B, P, C * P), F32, kind="Internal").ap()
        ys_dram = nc.dram_tensor("ys_rows", (UNITS * P, D), F32, kind="Internal").ap()

        ld_const, zeroed, tails = sem("ld_const"), sem("zeroed"), sem("tails")
        ld_w = sem("ld_w")
        passed = sem("passed")
        setup_v, setup_a, setup_p = sem("setup_v"), sem("setup_a"), sem("setup_p")
        ld_x = [sem("ld_x0"), sem("ld_x1")]
        scat = [sem("scat0"), sem("scat1")]
        first_split = sem("first_split")

        def before(eng, s, value):
            if not isinstance(value, int) or value > 0:
                eng.wait_ge(s, value)

        def settled(eng):
            eng.sem_inc(passed, 1)

        def dma_at(i, u, n=1):
            return (i - u) * (8 * n) + 16 * n

        def pipeline(eng, body, first=-2, last=B + 4, steady=(4, B - 2)):
            for k in range(first, steady[0]):
                body(k, k % 2)
            with eng.Fori(steady[0] // 2, steady[1] // 2) as j:
                body(2 * j, 0)
                body(2 * j + 1, 1)
            for k in range(steady[1], last):
                body(k, k % 2)

        def valid(i):
            return not isinstance(i, int) or 0 <= i < B

        def attention(L):
            n = f"a{L}_"
            A = L == 0
            last_k, steady = B + 5, (6, B - 2)
            wq, wk, wv, wo = (w[f"{c}{L}"] for c in "qkvo")
            ld_ctx = [sem(n + "ld_ctx0"), sem(n + "ld_ctx1")]
            pre_p = track(n + "pre_p", "xT K Q V")
            sc_p = track(n + "sc_p", "0 1 2 3")
            tr_p = track(n + "tr_p", "0 1 2 3")
            pv_p = track(n + "pv_p", "0 1 2 3")
            out_p = track(n + "out_p", "O")
            pre_a = track(n + "pre_a", "xT K Q")
            ex_a = track(n + "ex_a", "0 1 2 3")
            tr_a = track(n + "tr_a", "0 1 2 3")
            ln_v = track(n + "ln_v", "stats mean xh")
            v_a = track(n + "v_a", "V")
            sc_v = track(n + "sc_v", "m0 s0 m1 s1 m2 s2 m3 s3" if A else "a0 m0 a1 m1 a2 m2 a3 m3")
            out_v = track(n + "out_v", "den att x")
            ln_g = track(n + "ln_g", "var rstd")
            keep_a = track(n + "keep_a", "x")
            kb_g = track(n + "kb_g", "0 1")
            rd = ("s" if A else "a")
            if A:
                rt_p = track(n + "rt_p", "xnT lg")
                rk_p = track(n + "rk_p", "rank")
                rk_v = track(n + "rk_v", "oh both pos run ohp posf put keep")
                rt_a = track(n + "rt_a", "xnT")
                rt_v = track(n + "rt_v", "lg top idx keep_top keep_idx")
                bias_g = track(n + "bias_g", "x")
                n2_v = track(n + "n2_v", "stats mean xo stats3 res mean3 xh3")
                n2_g = track(n + "n2_g", "var rstd var3 rstd3 gamma xn")
            else:
                sub_g = track(n + "sub_g", "0 1 2 3")
                gidx_g = track(n + "gidx_g", "idx")
                ld_y = [sem(n + "ld_y0"), sem(n + "ld_y1")]
                ld_fs = [sem(n + "ld_fs0"), sem(n + "ld_fs1")]
                mix_v = track(n + "mix_v", "y0 y1")
                n4_v = track(n + "n4_v", "stats mean xh")
                n4_g = track(n + "n4_g", "var rstd")
                x1_p = track(n + "x1_p", "xT s V")
                x1_a = track(n + "x1_a", "xT e0 e1")
                x1_v = track(n + "x1_v", "s0 s1 neg V")
                x2_p = track(n + "x2_p", "pT av")
                x2_a = track(n + "x2_a", "pT")
                x2_v = track(n + "x2_v", "rz pn mask sum")
                st_x3 = [sem(n + "st_x3_0"), sem(n + "st_x3_1")]

            def flat(t, i, g, back):
                return i * 4 + g + 1 - back

            def sync(sp):
                for u in range(2):
                    sp.dma_start(ctxT[:, u].rearrange("p c t -> p (c t)"), a["ctxT"][u]).then_inc(ld_ctx[u], 16)
                    if not A:
                        sp.dma_start(fs[:, u], a["fside"][u:u + 1, :].partition_broadcast(P)).then_inc(ld_fs[u], 16)

                def later_loads(k, u):
                    if isinstance(k, int):
                        if 0 <= k < RING:
                            sp.dma_start(ring_raw[:, k, :], a["w12"][k]).then_inc(ld_ring[k], 16)
                        if k == RING:
                            sp.dma_start(w_sb[:, 4:].rearrange("p n c d -> p (n c d)"), a["weights"][:, 4 * C * D:])\
                                .then_inc(ld_w, 16)

                def body(k, u):
                    if A:
                        later_loads(k, u)
                    elif isinstance(k, int) and 0 <= k < SETS:
                        sp.dma_start(wset[:, k].rearrange("p e f -> p (e f)"), a["wset"][k]).then_inc(ld_set[k], 16)
                    if not A and valid(k + 1) and (not isinstance(k, int) or k >= 1):
                        sp.wait_ge(sc_v.sem, sc_v.at(k - 1, "a3"))
                        sp.dma_start(fs[:, 1 - u], a["fside"][bass.ds(k + 1, 1), :].partition_broadcast(P))\
                            .then_inc(ld_fs[1 - u], 16)
                    if not A and valid(k - 4):
                        sp.wait_ge(x1_a.sem, x1_a.at(k - 4, "xT"))
                        sp.dma_start(x3T_dram[k - 4], x3T.rearrange("p c t -> p (c t)")).then_inc(st_x3[u], 16)
                    if A and valid(k + 4) and (not isinstance(k, int) or k >= -2):
                        i = k + 4
                        before(sp, ln_v.sem, ln_v.at(k + 2, "stats"))
                        sp.dma_start(x_all[:, i], a["x"][i]).then_inc(ld_x[u], 16)
                    if valid(k + 3) and (not isinstance(k, int) or k + 3 >= 2):
                        i = k + 3
                        before(sp, pre_p.sem, pre_p.at(k + 1, "V"))
                        sp.dma_start(ctxT[:, 1 - u].rearrange("p c t -> p (c t)"), a["ctxT"][i]).then_inc(ld_ctx[1 - u], 16)
                pipeline(sp, body, first=-2, last=B - 2 if A else B + 4, steady=(6, B - 4))
                if not A:
                    for s in st_x3:
                        sp.wait_ge(s, 8 * B)

            def tensor(pe):
                def weighted_values(k, u, g):
                    pe.wait_ge(tr_a.sem, tr_a.at(k, str(g)))
                    if g == 0:
                        pe.wait_ge(v_a.sem, v_a.at(k, "V"))
                        before(pe, out_v.sem, out_v.at(k - 1, "att"))
                    c, odd = g // 2, g % 2
                    for what in range(2):
                        for h in range(G):
                            vals = vz[:, u, c * G + h] if what == 0 else one_zero[:, :, :]
                            o = what * D + c * P
                            last = nc.tensor.matmul(ps[4][32 * h:32 * (h + 1), o:o + P], vals[:, odd:odd + 2, :],
                                                    pT[:, g % 2, h * P:(h + 1) * P],
                                                    start=g == 0 and what == 0, stop=g == 3 and what == 1)
                    last.then_inc(pv_p.sem, 1)

                def body(k, u):
                    for g in range(G):
                        if valid(k - 1):
                            pe.wait_ge(ex_a.sem, ex_a.at(k - 1, str(g)))
                            before(pe, tr_a.sem, flat(tr_a, k - 1, g, 2))
                            for h in range(G):
                                last = nc.tensor.transpose(ps[2 + g % 2][:, h * P:(h + 1) * P],
                                                           pr[:, 1 - u, g, h * P:(h + 1) * P], cv["ident"])
                            last.then_inc(tr_p.sem, 1)
                        if valid(k):
                            pe.wait_ge(pre_a.sem, pre_a.at(k, "Q"))
                            pe.wait_ge(kb_g.sem, kb_g.at(k, str(g // 2)))
                            before(pe, sc_v.sem, sc_v.at(k, f"{rd}{g}") - 4)
                            c = g // 2
                            nc.tensor.matmul(ps[g % 2][:, :], qT[:, u, c, :],
                                             kbd[:, C * u + c, bass.ds(g % 2, G, 2), :],
                                             start=True, stop=True).then_inc(sc_p.sem, 1)
                        if g > 0 and valid(k - 1):
                            weighted_values(k - 1, 1 - u, g - 1)
                        if valid(k + 1):
                            i, o = k + 1, 1 - u
                            if g == 0:
                                pe.wait_ge(ln_v.sem, ln_v.at(i, "xh"))
                                before(pe, v_a.sem, v_a.at(k, "V"))
                                if not A:
                                    before(pe, x2_v.sem, x2_v.at(k - 6, "mask"))
                                for c in range(C):
                                    last = nc.tensor.transpose(ps[5][:, c * P:(c + 1) * P],
                                                               xh[:, o, c * P:(c + 1) * P], cv["ident"])
                                last.then_inc(pre_p.sem, 1)
                                pe.wait_ge(ld_ctx[o], dma_at(i, o))
                                before(pe, pre_a.sem, pre_a.at(k, "Q"))
                                for m in range(C):
                                    for c in range(C):
                                        last = nc.tensor.matmul(ps[6][:, m * P:(m + 1) * P],
                                                                wk[:, c, m * P:(m + 1) * P], ctxT[:, o, c, :],
                                                                start=c == 0, stop=c == C - 1)
                                last.then_inc(pre_p.sem, 1)
                            if g == 2:
                                pe.wait_ge(pre_a.sem, pre_a.at(i, "K"))
                                if A:
                                    before(pe, rk_v.sem, rk_v.at(k - 5, "run") if valid(k - 5) else 0)
                                if not A:
                                    before(pe, x2_a.sem, x2_a.at(k - 5, "pT"))
                                for m in range(C):
                                    for c in range(C):
                                        last = nc.tensor.matmul(ps[6][:, m * P:(m + 1) * P],
                                                                wq[:, c, m * P:(m + 1) * P], xT[:, c, :],
                                                                start=c == 0, stop=c == C - 1)
                                last.then_inc(pre_p.sem, 1)
                            if g == 3:
                                pe.wait_ge(pre_a.sem, pre_a.at(i, "xT"))
                                if not A:
                                    before(pe, x1_v.sem, x1_v.at(k - 4, "V"))
                                for c in range(C):
                                    last = nc.tensor.matmul(ps[5][:, 0:D], ctxT[:, o, c, :], wv[:, c, :],
                                                            start=c == 0, stop=c == C - 1)
                                last.then_inc(pre_p.sem, 1)
                        if A and valid(k - 4):
                            i = k - 4
                            if g == 1:
                                pe.wait_ge(n2_g.sem, n2_g.at(i, "xn"))
                                before(pe, out_v.sem, out_v.at(k - 3, "x"))
                                for c in range(C):
                                    last = nc.tensor.transpose(ps[7][:, c * P:(c + 1) * P],
                                                               xc[:, c * P:(c + 1) * P], cv["ident"])
                                last.then_inc(rt_p.sem, 1)
                            if g == 2:
                                pe.wait_ge(rt_a.sem, rt_a.at(i, "xnT"))
                                for c in range(C):
                                    last = nc.tensor.matmul(ps[7][:, 0:E0], xnT[:, c, :], wg_sb[:, c, :],
                                                            start=c == 0, stop=c == C - 1)
                                last.then_inc(rt_p.sem, 1)
                        if A and g == 1 and valid(k - 5):
                            pe.wait_ge(rk_v.sem, rk_v.at(k - 5, "both"))
                            before(pe, pre_a.sem, pre_a.at(k + 1, "K"))
                            for n_, m in enumerate((cv["tri"], ones[:, :])):
                                last = nc.tensor.matmul(ps[6][:, D + n_ * E0:D + (n_ + 1) * E0], m, both,
                                                        start=True, stop=True)
                            last.then_inc(rk_p.sem, 1)
                        if not A and valid(k - 4):
                            i = k - 4
                            if g == 0:
                                pe.wait_ge(n4_v.sem, n4_v.at(i, "xh"))
                                before(pe, out_v.sem, out_v.at(k - 3, "x"))
                                for c in range(C):
                                    last = nc.tensor.transpose(ps[7][:, c * P:(c + 1) * P],
                                                               xc[:, c * P:(c + 1) * P], cv["ident"])
                                last.then_inc(x1_p.sem, 1)
                            if g == 1:
                                pe.wait_ge(x1_a.sem, x1_a.at(i, "xT"))
                                for m in range(C):
                                    for c in range(C):
                                        last = nc.tensor.matmul(ps[7][:, D + m * P:D + (m + 1) * P],
                                                                qa[:, c, m * P:(m + 1) * P], x3T[:, c, :],
                                                                start=c == 0, stop=c == C - 1)
                                last.then_inc(x1_p.sem, 1)
                                before(pe, pre_a.sem, pre_a.at(k + 1, "xT"))
                                before(pe, v_a.sem, v_a.at(k, "V"))
                                before(pe, x2_v.sem, x2_v.at(k - 6, "mask"))
                                for c in range(C):
                                    last = nc.tensor.matmul(ps[5][:, D:2 * D], x3T[:, c, :], w["dv"][:, c, :],
                                                            start=c == 0, stop=c == C - 1)
                                last.then_inc(x1_p.sem, 1)
                        if not A and valid(k - 5):
                            i = k - 5
                            if g == 1:
                                pe.wait_ge(x2_v.sem, x2_v.at(i, "pn"))
                                before(pe, pre_a.sem, pre_a.at(k + 1, "K"))
                                for c in range(C):
                                    last = nc.tensor.transpose(ps[6][:, D + c * P:D + (c + 1) * P],
                                                               pn[:, c, :], cv["ident"])
                                last.then_inc(x2_p.sem, 1)
                            if g == 3:
                                pe.wait_ge(x2_a.sem, x2_a.at(i, "pT"))
                                before(pe, x1_v.sem, x1_v.at(k - 4, "V"))
                                before(pe, pre_a.sem, pre_a.at(k + 1, "xT"))
                                for m in range(C):
                                    last = nc.tensor.matmul(ps[5][:, D + m * P:D + (m + 1) * P],
                                                            dVb[:, 1 - u, m * P:(m + 1) * P],
                                                            pnT[:, m, :], start=True, stop=True)
                                last.then_inc(x2_p.sem, 1)
                        if valid(k - 2):
                            i = k - 2
                            if g == 3:
                                pe.wait_ge(out_v.sem, out_v.at(i, "att"))
                                if A:
                                    before(pe, rt_v.sem, rt_v.at(k - 4, "lg"))
                                else:
                                    before(pe, x1_v.sem, x1_v.at(k - 4, "s1"))
                                for c in range(C):
                                    last = nc.tensor.matmul(ps[7][:, D:2 * D], aT[:, c, :], wo[:, c, :],
                                                            start=c == 0, stop=c == C - 1)
                                last.then_inc(out_p.sem, 1)
                        if g == 3 and valid(k - 1):
                            weighted_values(k - 1, 1 - u, 3)
                pipeline(pe, body, last=last_k, steady=steady)

            def scalar(act):
                def body(k, u):
                    if A and isinstance(k, int) and k > B:
                        if k == B + 1:
                            act.wait_ge(ld_ring[0], 16)
                        o = (k - B - 1) * C * F0 // 2
                        nc.scalar.copy(ring_hi[:, 0, o:o + C * F0 // 2], ring_raw[:, 0, o:o + C * F0 // 2])\
                            .then_inc(first_split, 1)
                    if valid(k):
                        act.wait_ge(pre_p.sem, pre_p.at(k, "V"))
                        before(act, pv_p.sem, pv_p.at(k - 2, "3"))
                        if not A:
                            before(act, x2_v.sem, x2_v.at(k - 6, "mask"))
                        nc.scalar.copy(vz[:, u, :, bass.ds(0, 2, 2), :],
                                       ps[5][:, 0:D].rearrange("p (j h d) -> p j h d", h=2, d=DH)).then_inc(v_a.sem, 1)
                    for g in range(G):
                        if valid(k - 1):
                            act.wait_ge(tr_p.sem, tr_p.at(k - 1, str(g)))
                            before(act, pv_p.sem, flat(pv_p, k - 1, g, 2))
                            nc.scalar.copy(pT[:, g % 2, :], ps[2 + g % 2][:, :]).then_inc(tr_a.sem, 1)
                        i, e, v = (k, g - 1, u) if g else (k - 1, G - 1, 1 - u)
                        if valid(i):
                            if A:
                                act.wait_ge(sc_v.sem, sc_v.at(i, f"s{e}"))
                            else:
                                act.wait_ge(sub_g.sem, sub_g.at(i, str(e)))
                            nc.scalar.activation(pr[:, v, e, :], pr[:, v, e, :], ACT.Exp).then_inc(ex_a.sem, 1)
                        if valid(k + 1):
                            i, o = k + 1, 1 - u
                            if g == 0:
                                act.wait_ge(pre_p.sem, pre_p.at(i, "xT"))
                                before(act, pre_p.sem, pre_p.at(k, "Q"))
                                nc.scalar.copy(xT.rearrange("p c t -> p (c t)"), ps[5][:, 0:D]).then_inc(pre_a.sem, 1)
                                act.wait_ge(pre_p.sem, pre_p.at(i, "K"))
                                before(act, kb_g.sem, kb_g.at(k, "1"))
                                for c in range(C):
                                    last = nc.scalar.activation(kT[:, c, :], ps[6][:, c * P:(c + 1) * P], ACT.Identity,
                                                                bias=col["bk0"][:, c:c + 1] if A else 0.0)
                                last.then_inc(pre_a.sem, 1)
                        if not A and g == 1 and valid(k - 5):
                            act.wait_ge(x2_p.sem, x2_p.at(k - 5, "pT"))
                            before(act, pre_p.sem, pre_p.at(k + 1, "K"))
                            before(act, x2_p.sem, x2_p.at(k - 6, "av"))
                            nc.scalar.copy(pnT.rearrange("p c t -> p (c t)"), ps[6][:, D:2 * D]).then_inc(x2_a.sem, 1)
                        if A and g == 1 and valid(k - 4):
                            act.wait_ge(rt_p.sem, rt_p.at(k - 4, "xnT"))
                            nc.scalar.copy(xnT.rearrange("p c t -> p (c t)"), ps[7][:, 0:D]).then_inc(rt_a.sem, 1)
                            before(act, scat[u], dma_at(k - 6, u, 2) if valid(k - 6) else 0)
                            nc.scalar.copy(xkeep[:, u, :], xc).then_inc(keep_a.sem, 1)
                        if not A and g == 0 and valid(k - 4):
                            act.wait_ge(x1_p.sem, x1_p.at(k - 4, "xT"))
                            before(act, x1_p.sem, x1_p.at(k - 5, "V"))
                            before(act, st_x3[1 - u], dma_at(k - 5, 1 - u) if not isinstance(k, int) or k >= 5 else 0)
                            nc.scalar.copy(x3T.rearrange("p c t -> p (c t)"), ps[7][:, 0:D]).then_inc(x1_a.sem, 1)
                        if g == 2 and valid(k + 1):
                            i, o = k + 1, 1 - u
                            act.wait_ge(pre_p.sem, pre_p.at(i, "Q"))
                            before(act, sc_p.sem, sc_p.at(k - 1, "3"))
                            for c in range(C):
                                last = nc.scalar.activation(qT[:, o, c, :], ps[6][:, c * P:(c + 1) * P], ACT.Identity,
                                                            bias=qcol[:, 0, c:c + 1] if A else 0.0, scale=QSCALE)
                            last.then_inc(pre_a.sem, 1)
                        if not A and g == 3 and valid(k - 4):
                            act.wait_ge(x1_v.sem, x1_v.at(k - 4, "neg"))
                            before(act, x2_v.sem, x2_v.at(k - 5, "pn"))
                            for c in range(C):
                                nc.scalar.activation(sc[:, c, :], sc[:, c, :], ACT.Exp, bias=snx[:, c:c + 1],
                                                     accum_out=sz[:, c:c + 1]).then_inc(x1_a.sem, 1)
                pipeline(act, body, last=last_k, steady=steady)

            def vector(dve):
                def body(k, u):
                    nxt, cur, out_i, ln_i, rt_i, sl_i = k + 2, k, k - 2, k - 3, k - 4, k - 5
                    for g in range(G):
                        if g == 0 and valid(out_i):
                            dve.wait_ge(pv_p.sem, pv_p.at(out_i, "3"))
                            nc.vector.reciprocal(rden.rearrange("p c t -> p (c t)"), ps[4][:, D:2 * D])\
                                .then_inc(out_v.sem, 1)
                        if g == 0 and valid(ln_i):
                            t = n2_v if A else n4_v
                            dve.wait_ge(out_v.sem, out_v.at(ln_i, "x"))
                            settled(dve)
                            nc.vector.bn_stats(stat[:, 1, :], x_all[:, ln_i]).then_inc(t.sem, 1)
                        if g == 0 and valid(out_i):
                            dve.wait_ge(out_v.sem, out_v.at(out_i, "den"))
                            before(dve, out_p.sem, out_p.at(k - 3, "O"))
                            nc.vector.tensor_tensor(aT.rearrange("p c t -> p (c t)"), ps[4][:, 0:D],
                                                    rden.rearrange("p c t -> p (c t)"), ALU.mult).then_inc(out_v.sem, 1)
                        if g == 0 and valid(ln_i):
                            dve.wait_ge(t.sem, t.at(ln_i, "stats"))
                            settled(dve)
                            nc.vector.bn_aggr(mv[:, 1, :], stat[:, 1, :]).then_inc(t.sem, 1)
                        if g == 3 and valid(ln_i) and A:
                            dve.wait_ge(n2_g.sem, n2_g.at(ln_i, "rstd3"))
                            before(dve, n2_g.sem, n2_g.at(ln_i - 1, "xn"))
                            nc.vector.tensor_scalar(xh3, xo, mv[:, 2, 0:1], rstd[:, 2, 1:2],
                                                    ALU.subtract, ALU.mult).then_inc(n2_v.sem, 1)
                        if valid(cur):
                            s = ps[g % 2][:, :].rearrange("p (h t) -> p h t", h=G)
                            sbv = sbias[:, g % 2, :].rearrange("p (h t) -> p h t", h=G)
                            dst = pr[:, u, g, :].rearrange("p (h t) -> p h t", h=G)
                            m = mx[:, g % 2, :]
                            dve.wait_ge(sc_p.sem, sc_p.at(k, str(g)))
                            if A:
                                nc.vector.tensor_reduce(m, s, AX, ALU.max).then_inc(sc_v.sem, 1)
                            else:
                                if g == 0:
                                    dve.wait_ge(ld_fs[u], dma_at(k, u))
                                before(dve, sub_g.sem, flat(sub_g, k, g, 2))
                                nc.vector.tensor_tensor(sbv, s, fs[:, u, None, :].to_broadcast([P, G, P]),
                                                        ALU.add).then_inc(sc_v.sem, 1)
                        if A and g == 0 and valid(nxt):
                            dve.wait_ge(ld_x[u], dma_at(nxt, u))
                            settled(dve)
                            nc.vector.bn_stats(stat[:, 0, :], x_all[:, nxt]).then_inc(ln_v.sem, 1)
                        if A and g == 1 and valid(ln_i):
                            dve.wait_ge(n2_g.sem, n2_g.at(ln_i, "rstd"))
                            nc.vector.tensor_scalar(xo, x_all[:, ln_i], mv[:, 1, 0:1], rstd[:, 1, 1:2],
                                                    ALU.subtract, ALU.mult).then_inc(n2_v.sem, 1)
                        if A and g == 2 and valid(rt_i):
                            dve.wait_ge(rt_p.sem, rt_p.at(rt_i, "lg"))
                            nc.vector.tensor_tensor(lg, ps[7][:, 0:E0], bg_sb[:, :], ALU.add).then_inc(rt_v.sem, 1)
                        if A and g == 0 and valid(sl_i):
                            nc.vector.tensor_tensor(oh2, top_idx[:, sl_i, :, None].to_broadcast([P, 2, E0]),
                                                    cv["iota8"][:, None, :].to_broadcast([P, 2, E0]), ALU.is_equal)\
                                .then_inc(rk_v.sem, 1)
                        if A and g == 2 and valid(sl_i):
                            dve.wait_ge(rk_v.sem, rk_v.at(sl_i, "run"))
                            nc.vector.tensor_tensor(ohp2, oh2, pos2[:, None, :].to_broadcast([P, 2, E0]), ALU.mult)\
                                .then_inc(rk_v.sem, 1)
                        if A and g == 3 and valid(sl_i):
                            dve.wait_ge(rk_v.sem, rk_v.at(sl_i, "ohp"))
                            nc.vector.tensor_reduce(posf2, ohp2, AX, ALU.add).then_inc(rk_v.sem, 1)
                        if not A and g == 0 and valid(sl_i):
                            dve.wait_ge(x1_a.sem, x1_a.at(sl_i, "e1"))
                            nc.vector.reciprocal(srz, sz).then_inc(x2_v.sem, 1)
                        if not A and g == 1 and valid(nxt):
                            settled(dve)
                            nc.vector.bn_stats(stat[:, 0, :], x_all[:, nxt]).then_inc(ln_v.sem, 1)
                        if not A and g == 2 and valid(rt_i):
                            dve.wait_ge(x1_v.sem, x1_v.at(rt_i, "s1"))
                            nc.vector.tensor_scalar(snx, smx, -1.0, None, ALU.mult).then_inc(x1_v.sem, 1)
                        if valid(cur):
                            if A:
                                dve.wait_ge(sc_v.sem, sc_v.at(k, f"m{g}"))
                                before(dve, tr_p.sem, tr_p.at(k - 2, str(g)))
                                nc.vector.tensor_tensor(dst, s, m[:, :, None].to_broadcast([P, G, P]),
                                                        ALU.subtract).then_inc(sc_v.sem, 1)
                            else:
                                dve.wait_ge(sc_v.sem, sc_v.at(k, f"a{g}"))
                                nc.vector.tensor_reduce(m, sbv, AX, ALU.max).then_inc(sc_v.sem, 1)
                        if g == (0 if A else 1) and valid(nxt):
                            dve.wait_ge(ln_v.sem, ln_v.at(nxt, "stats"))
                            settled(dve)
                            nc.vector.bn_aggr(mv[:, 0, :], stat[:, 0, :]).then_inc(ln_v.sem, 1)
                        if A and g == 1 and valid(ln_i):
                            dve.wait_ge(n2_v.sem, n2_v.at(ln_i, "xo"))
                            settled(dve)
                            nc.vector.bn_stats(stat[:, 2, :], xo).then_inc(n2_v.sem, 1)
                            nc.vector.scalar_tensor_tensor(out=x_all[:, ln_i], in0=xo, scalar=tg[:, 2:3],
                                                           in1=x_all[:, ln_i], op0=ALU.mult, op1=ALU.add)\
                                .then_inc(n2_v.sem, 1)
                            dve.wait_ge(n2_v.sem, n2_v.at(ln_i, "stats3"))
                            settled(dve)
                            nc.vector.bn_aggr(mv[:, 2, :], stat[:, 2, :]).then_inc(n2_v.sem, 1)
                        if A and g == 0 and valid(sl_i):
                            dve.wait_ge(rk_v.sem, rk_v.at(sl_i, "oh"))
                            nc.vector.tensor_tensor(both, oh2[:, 0, :], oh2[:, 1, :], ALU.add).then_inc(rk_v.sem, 1)
                        if A and g == 1 and valid(sl_i):
                            dve.wait_ge(rk_p.sem, rk_p.at(sl_i, "rank"))
                            nc.vector.tensor_tensor(pos2, ps[6][:, D:D + E0], next_row[:, :], ALU.add).then_inc(rk_v.sem, 1)
                            nc.vector.tensor_tensor(next_row[:, :], ps[6][:, D + E0:D + 2 * E0], next_row[:, :], ALU.add)\
                                .then_inc(rk_v.sem, 1)
                        if A and g == 3 and valid(sl_i):
                            dve.wait_ge(rk_v.sem, rk_v.at(sl_i, "posf"))
                            before(dve, scat[1 - u], dma_at(k - 7, 1 - u, 2) if valid(k - 7) else 0)
                            nc.vector.tensor_copy(idx_put[:, 1 - u, :], posf2).then_inc(rk_v.sem, 1)
                            nc.vector.tensor_copy(slot_f[:, :, sl_i], posf2).then_inc(rk_v.sem, 1)
                        if A and g == 2 and valid(rt_i):
                            dve.wait_ge(rt_v.sem, rt_v.at(rt_i, "lg"))
                            settled(dve)
                            nc.vector.max(top8[:, :], lg).then_inc(rt_v.sem, 1)
                        if g == 2 and valid(nxt):
                            dve.wait_ge(ln_g.sem, ln_g.at(nxt, "rstd"))
                            before(dve, pre_p.sem, pre_p.at(k, "xT"))
                            nc.vector.tensor_scalar(xh[:, u, :], x_all[:, nxt], mv[:, 0, 0:1], rstd[:, 0, 1:2],
                                                    ALU.subtract, ALU.mult).then_inc(ln_v.sem, 1)
                        if A and g == 2 and valid(rt_i):
                            dve.wait_ge(rt_v.sem, rt_v.at(rt_i, "top"))
                            settled(dve)
                            nc.vector.max_index(idx8[:, :], top8[:, :], lg).then_inc(rt_v.sem, 1)
                            nc.vector.tensor_copy(top_val[:, rt_i, :], top8[:, :]).then_inc(rt_v.sem, 1)
                            dve.wait_ge(rt_v.sem, rt_v.at(rt_i, "idx"))
                            nc.vector.tensor_copy(top_idx[:, rt_i, :], idx8[:, 0:2]).then_inc(rt_v.sem, 1)
                        if not A and g == 0 and valid(nxt):
                            dve.wait_ge(ld_y[u], dma_at(nxt, u, 2))
                            nc.vector.scalar_tensor_tensor(out=x_all[:, nxt], in0=yg[:, u, 0, :],
                                                           scalar=wts[:, 0, bass.ds(nxt, 1)], in1=x_all[:, nxt],
                                                           op0=ALU.mult, op1=ALU.add).then_inc(mix_v.sem, 1)
                        if not A and g == 0 and valid(sl_i):
                            dve.wait_ge(x2_v.sem, x2_v.at(sl_i, "rz"))
                            nc.vector.tensor_tensor(pn, sc, srz[:, :, None].to_broadcast([P, C, P]), ALU.mult)\
                                .then_inc(x2_v.sem, 1)
                        if not A and g == 0 and valid(nxt):
                            dve.wait_ge(mix_v.sem, mix_v.at(nxt, "y0"))
                            nc.vector.scalar_tensor_tensor(out=x_all[:, nxt], in0=yg[:, u, 1, :],
                                                           scalar=wts[:, 1, bass.ds(nxt, 1)], in1=x_all[:, nxt],
                                                           op0=ALU.mult, op1=ALU.add).then_inc(mix_v.sem, 1)
                            dve.wait_ge(mix_v.sem, mix_v.at(nxt, "y1"))
                        if not A and g == 1 and valid(rt_i):
                            dve.wait_ge(x1_p.sem, x1_p.at(rt_i, "s"))
                            before(dve, x2_v.sem, x2_v.at(sl_i, "pn"))
                            for c in range(C):
                                nc.vector.tensor_scalar(sc[:, c, :], ps[7][:, D + c * P:D + (c + 1) * P],
                                                        qac[:, c:c + 1], None, ALU.add, ALU.max,
                                                        accum_out=smx[:, c:c + 1]).then_inc(x1_v.sem, 1)
                        if not A and g == 2 and valid(ln_i):
                            dve.wait_ge(n4_g.sem, n4_g.at(ln_i, "rstd"))
                            before(dve, x1_p.sem, x1_p.at(ln_i - 1, "xT"))
                            nc.vector.tensor_scalar(xc, x_all[:, ln_i], mv[:, 1, 0:1], rstd[:, 1, 1:2],
                                                    ALU.subtract, ALU.mult).then_inc(n4_v.sem, 1)
                        if not A and g == 2 and valid(rt_i):
                            dve.wait_ge(x1_p.sem, x1_p.at(rt_i, "V"))
                            nc.vector.tensor_tensor(dVb[:, u, :], ps[5][:, D:2 * D], row["dbv"], ALU.add)\
                                .then_inc(x1_v.sem, 1)
                        if not A and g == 3 and valid(sl_i):
                            dve.wait_ge(x2_p.sem, x2_p.at(sl_i, "av"))
                            before(dve, pre_p.sem, pre_p.at(k + 1, "V"))
                            nc.vector.tensor_tensor(mk, ps[5][:, D:2 * D].rearrange("p (c h s) -> p c h s", c=C, h=HC),
                                                    cv["mask8"][:, None, :, None].to_broadcast([P, C, HC, NS]),
                                                    ALU.mult).then_inc(x2_v.sem, 1)
                        if g == 3 and valid(out_i):
                            dve.wait_ge(out_p.sem, out_p.at(out_i, "O"))
                            if A:
                                dve.wait_ge(bias_g.sem, bias_g.at(out_i, "x"))
                            nc.vector.scalar_tensor_tensor(out=x_all[:, out_i], in0=ps[7][:, D:2 * D],
                                                           scalar=tg[:, L:L + 1], in1=x_all[:, out_i],
                                                           op0=ALU.mult, op1=ALU.add).then_inc(out_v.sem, 1)
                        if not A and g == 3 and valid(sl_i):
                            dve.wait_ge(x2_v.sem, x2_v.at(sl_i, "mask"))
                            nc.vector.tensor_reduce(oT_all[:, :, :, sl_i], mk.rearrange("p c h s -> p c s h"), AX,
                                                    ALU.add).then_inc(x2_v.sem, 1)
                    if A and isinstance(k, int) and k > B:
                        dve.wait_ge(first_split, k - B)
                        o = (k - B - 1) * C * F0 // 2
                        nc.vector.tensor_tensor(ring_lo[:, 0, o:o + C * F0 // 2], ring_raw[:, 0, o:o + C * F0 // 2],
                                                ring_hi[:, 0, o:o + C * F0 // 2], ALU.subtract)
                pipeline(dve, body, last=last_k, steady=(8, B - 2) if A else steady)

            def gpsimd(pool):
                def rsqrt(t, j, i, vname, rname):
                    nc.gpsimd.tensor_tensor(rstd[:, j, 0:1], mv[:, j, 1:2], eps_sb[:, :], ALU.add).then_inc(t.sem, 1)
                    pool.wait_ge(t.sem, t.at(i, vname))
                    nc.gpsimd.tensor_tensor(rstd[:, j, 1:2], rstd[:, j, 0:1], mhalf[:, :], ALU.pow).then_inc(t.sem, 1)

                def gather(i, u):
                    before(pool, mix_v.sem, mix_v.at(i - 2, "y1"))
                    nc.gpsimd.tensor_copy(idx_cur[:, u, :], slot_i[:, :, i]).then_inc(gidx_g.sem, 1)
                    pool.wait_ge(gidx_g.sem, gidx_g.at(i, "idx"))
                    settled(pool)
                    for c in range(2):
                        nc.gpsimd.indirect_dma_start(out=yg[:, u, c, :], out_offset=None, in_=ys_dram[:, :],
                                                     in_offset=bass.IndirectOffsetOnAxis(ap=idx_cur[:, u, c:c + 1].bitcast(U32), axis=0))\
                            .then_inc(ld_y[u], 16)

                def body(k, u):
                    if A:
                        if valid(k - 3):
                            pool.wait_ge(n2_v.sem, n2_v.at(k - 3, "mean"))
                            rsqrt(n2_g, 1, k - 3, "var", "rstd")
                        if valid(k + 2):
                            pool.wait_ge(ln_v.sem, ln_v.at(k + 2, "mean"))
                            rsqrt(ln_g, 0, k + 2, "var", "rstd")
                        if valid(k + 1):
                            kblock(k + 1, 1 - u, 0)
                        if valid(k - 3):
                            pool.wait_ge(n2_v.sem, n2_v.at(k - 3, "mean3"))
                            rsqrt(n2_g, 2, k - 3, "var3", "rstd3")
                        if valid(k + 1):
                            kblock(k + 1, 1 - u, 1)
                            pool.wait_ge(ln_v.sem, ln_v.at(k + 1, "xh"))
                            nc.gpsimd.tensor_tensor(x_all[:, k + 1], x_all[:, k + 1], row["bo0"], ALU.add)\
                                .then_inc(bias_g.sem, 1)
                        if valid(k - 3):
                            pool.wait_ge(n2_v.sem, n2_v.at(k - 3, "xh3"))
                            nc.gpsimd.tensor_tensor(xg, xh3, row["gamma"], ALU.mult).then_inc(n2_g.sem, 1)
                            pool.wait_ge(n2_g.sem, n2_g.at(k - 3, "gamma"))
                            before(pool, rt_p.sem, rt_p.at(k - 4, "xnT"))
                            before(pool, keep_a.sem, keep_a.at(k - 4, "x"))
                            nc.gpsimd.tensor_tensor(xc, xg, row["beta"], ALU.add).then_inc(n2_g.sem, 1)
                        if valid(k - 5):
                            if isinstance(k, int) and k == 5:
                                pool.wait_ge(zeroed, 16)
                            pool.wait_ge(keep_a.sem, keep_a.at(k - 5, "x"))
                            pool.wait_ge(rk_v.sem, rk_v.at(k - 5, "put"))
                            settled(pool)
                            for c in range(2):
                                nc.gpsimd.indirect_dma_start(
                                    out=xs_dram[:, :],
                                    out_offset=bass.IndirectOffsetOnAxis(ap=idx_put[:, 1 - u, c:c + 1].bitcast(U32), axis=0),
                                    in_=xkeep[:, 1 - u, :], in_offset=None).then_inc(scat[1 - u], 16)
                        return
                    if valid(k):
                        sub(k, u, 0)
                    if valid(k + 3) and (not isinstance(k, int) or k >= -1):
                        gather(k + 3, 1 - u)
                    if valid(k - 3):
                        pool.wait_ge(n4_v.sem, n4_v.at(k - 3, "mean"))
                        rsqrt(n4_g, 1, k - 3, "var", "rstd")
                    if valid(k):
                        sub(k, u, 1)
                    if valid(k + 2):
                        pool.wait_ge(ln_v.sem, ln_v.at(k + 2, "mean"))
                        rsqrt(ln_g, 0, k + 2, "var", "rstd")
                    if valid(k + 1):
                        kblock(k + 1, 1 - u, 0)
                    if valid(k):
                        sub(k, u, 2)
                    if valid(k + 1):
                        kblock(k + 1, 1 - u, 1)
                    if valid(k):
                        sub(k, u, 3)

                def sub(k, u, g):
                    pool.wait_ge(sc_v.sem, sc_v.at(k, f"m{g}"))
                    before(pool, tr_p.sem, tr_p.at(k - 2, str(g)))
                    nc.gpsimd.tensor_tensor(pr[:, u, g, :].rearrange("p (h t) -> p h t", h=G),
                                            sbias[:, g % 2, :].rearrange("p (h t) -> p h t", h=G),
                                            mx[:, g % 2, :, None].to_broadcast([P, G, P]), ALU.subtract)\
                        .then_inc(sub_g.sem, 1)

                def kblock(i, u, c):
                    pool.wait_ge(pre_a.sem, pre_a.at(i, "K"))
                    before(pool, sc_p.sem, sc_p.at(i - 2, str(2 * c + 1)))
                    nc.gpsimd.tensor_tensor(kbd[:, C * u + c], kT[:, c, None, :].to_broadcast([P, HC, P]),
                                            cv["mask8"][:, :, None].to_broadcast([P, HC, P]), ALU.mult)\
                        .then_inc(kb_g.sem, 1)

                if not A:
                    gather(0, 0)
                    gather(1, 1)
                pipeline(pool, body, last=last_k, steady=(6, B - 2 if A else B - 4))
                if A:
                    for s in scat:
                        pool.wait_ge(s, 16 * B)

            return sync, tensor, scalar, vector, gpsimd

        ld_ring = [sem(f"ld_ring{i}") for i in range(RING)]
        ld_ring_sw = [sem(f"ld_ring_sw{i}") for i in range(RING)]
        ld_rows = sem("ld_rows")
        route_v, route_a = sem("route_v"), sem("route_a")
        dn_p = track("m0_dn_p", "y", UNITS, base=1)

        def routing():
            def sync(sp):
                sp.wait_ge(ld_w, 16)
                sp.dma_start(b1_sb.rearrange("p e f -> p (e f)"), a["b1"].partition_broadcast(P)).then_inc(ld_rows, 16)
                sp.dma_start(b2_sb.rearrange("p e f -> p (e f)"), a["b2"].partition_broadcast(P)).then_inc(ld_rows, 16)

            def vector(dve):
                n = [0]

                def link(ins):
                    n[0] += 1
                    ins.then_inc(route_v, 1)
                    dve.wait_ge(route_v, n[0])

                def be(v):
                    return v[:, :, None].to_broadcast([P, B, E0])

                def ue(v):
                    return v[:, None, :].to_broadcast([P, UNITS, E0])

                tt, ts = nc.vector.tensor_tensor, nc.vector.tensor_scalar
                link(tt(ex, top_val[:, :, :], be(top_val[:, :, 0]), ALU.subtract))
                link(tt(cnt, next_row[:, :], cv["first"], ALU.subtract))
                link(tt(blk, cnt[:, :, None].to_broadcast([P, E0, B]), cv["thr"][:, None, :].to_broadcast([P, E0, B]),
                        ALU.is_gt))
                link(nc.vector.tensor_reduce(nblk, blk, AX, ALU.add))
                link(nc.vector.scalar_tensor_tensor(out=lim, in0=nblk, scalar=float(P), in1=cv["first"],
                                                    op0=ALU.mult, op1=ALU.add))
                link(ts(past, cv["first"], P / TOKENS, float(DUMP), ALU.mult, ALU.add))
                link(ts(past, past, cv["part"], None, ALU.add))
                link(ts(tail, next_row[:, :], cv["part"], None, ALU.add))
                link(tt(inside, tail, lim, ALU.is_lt))
                link(tt(tail, tail, past, ALU.subtract))
                link(tt(tail, tail, inside, ALU.mult))
                link(tt(tail, tail, past, ALU.add))
                link(nc.vector.tensor_copy(tail_i, tail))
                link(nc.vector.tensor_tensor_scan(cend, ones[:, 0:E0], nblk, 0.0, ALU.mult, ALU.add))
                link(ts(cend_i[:, :], cend[0:1, :], float(dn_p.base), None, ALU.add))
                link(tt(ucmp, cv["iotau"][:, :, None].to_broadcast([P, UNITS, E0]), ue(cend), ALU.is_ge))
                link(nc.vector.tensor_reduce(uexp, ucmp, AX, ALU.add))
                link(ts(uexp, uexp, float(E0 - 1), None, ALU.min))
                link(nc.vector.tensor_copy(unit_e[:, :], uexp[0:1, :]))
                link(tt(shift, nblk, cend, ALU.subtract))
                link(nc.vector.scalar_tensor_tensor(out=shift, in0=shift, scalar=float(P), in1=cv["first"],
                                                    op0=ALU.mult, op1=ALU.add))
                link(tt(ucmp, uexp[:, :, None].to_broadcast([P, UNITS, E0]), ue(cv["iota8"]), ALU.is_equal))
                link(tt(ucmp, ucmp, ue(shift), ALU.mult))
                link(nc.vector.tensor_reduce(ustart, ucmp, AX, ALU.add))
                link(nc.vector.scalar_tensor_tensor(out=ustart, in0=cv["iotau"], scalar=float(P), in1=ustart,
                                                    op0=ALU.mult, op1=ALU.add))
                link(ts(used, cv["iotau"], cend[:, E0 - 1:E0], None, ALU.is_lt))
                link(ts(ustart, ustart, float(-DUMP), None, ALU.add))
                link(tt(ustart, ustart, used, ALU.mult))
                link(ts(ustart, ustart, float(DUMP), None, ALU.add))
                link(nc.vector.tensor_copy(unit_s[:, :], ustart[0:1, :]))
                for c in range(2):
                    link(tt(ohb, top_idx[:, :, c:c + 1].to_broadcast([P, B, E0]),
                            cv["iota8"][:, None, :].to_broadcast([P, B, E0]), ALU.is_equal))
                    link(tt(ohb, ohb, shift[:, None, :].to_broadcast([P, B, E0]), ALU.mult))
                    link(nc.vector.tensor_reduce(off, ohb, AX, ALU.add))
                    link(tt(off, slot_f[:, c, :], off, ALU.subtract))
                    nc.vector.tensor_copy(slot_i[:, c, :], off)
                dve.wait_ge(route_a, 1)
                link(nc.vector.tensor_reduce(zs, ex, AX, ALU.add))
                link(tt(s2, ex[:, :, 0], ex[:, :, 1], ALU.add))
                link(nc.vector.scalar_tensor_tensor(out=den, in0=zs, scalar=1e-8, in1=s2, op0=ALU.mult, op1=ALU.add))
                link(nc.vector.reciprocal(rr, den))
                link(ts(rr, rr, tg[:, 2:3], None, ALU.mult))
                for c in range(2):
                    tt(wts[:, c, :], ex[:, :, c], rr, ALU.mult)

            def scalar(act):
                act.wait_ge(route_v, 1)
                nc.scalar.activation(ex.rearrange("p b e -> p (b e)"), ex.rearrange("p b e -> p (b e)"), ACT.Exp)\
                    .then_inc(route_a, 1)

            def gpsimd(pool):
                pool.sem_inc(dn_p.sem, dn_p.base)
                pool.wait_ge(route_v, 13)
                for e in range(E0):
                    nc.gpsimd.indirect_dma_start(
                        out=xs_dram[:, :], out_offset=bass.IndirectOffsetOnAxis(ap=tail_i[:, e:e + 1].bitcast(U32), axis=0),
                        in_=zero[:, :], in_offset=None).then_inc(tails, 16)
            return sync, None, scalar, vector, gpsimd

        def moe0():
            ld_xs = [sem("ld_xs0"), sem("ld_xs1")]
            st_ys = [sem("st_ys0"), sem("st_ys1")]
            ring_ready = sem("ring_ready")
            x_p = track("m0_x_p", "x", UNITS)
            up_p = track("m0_up_p", "h0 h1", UNITS)
            tp_p = track("m0_tp_p", "a b", UNITS)
            x_a = track("m0_x_a", "hi", UNITS)
            x_v = track("m0_x_v", "lo", UNITS)
            ge_a = track("m0_ge_a", "h0 h1", UNITS)
            tp_a = track("m0_tp_a", "a b", UNITS)
            b1_v = track("m0_b1_v", "h0 h1", UNITS)
            tp_v = track("m0_tp_v", "a b", UNITS)
            y_v = track("m0_y_v", "y", UNITS)
            split_g = sem("m0_split_g")
            up_banks = [(1, 2), (6, 7)]
            FC = F0 // P

            def ok(i):
                return not isinstance(i, int) or 0 <= i < UNITS

            def units(eng, body, first=-1, last=UNITS + 1, steady=(4, UNITS - 4)):
                pipeline(eng, body, first, last, steady)

            def units_with_experts(eng, body):
                def experts(j, n):
                    return nc.values_load_multi_w_load_instructions(unit_e[0:1, bass.ds(j, n)], engines=[eng.engine],
                                                                    min_val=0, max_val=E0 - 1)[1]

                def edge(j):
                    found = {i: experts(i, 1)[0] for i in (j - 1, j) if 0 <= i < UNITS}
                    body(j, j % 2, found.get(j), found.get(j - 1))

                for j in range(-1, 4):
                    edge(j)
                with eng.Fori(1, UNITS // 4 - 1) as i:
                    es = experts(4 * i - 1, 5)
                    for n in range(4):
                        body(4 * i + n, n % 2, es[n + 1], es[n])
                for j in range(UNITS - 4, UNITS + 1):
                    edge(j)

            def sync(sp):
                def first_row(j):
                    return sp.value_load(unit_s[0:1, bass.ds(j, 1)], min_val=0, max_val=DUMP)

                sp.wait_ge(tails, 16 * E0)
                for u in range(2):
                    sp.dma_start(xs[:, u, :], xs_dram[bass.ds(first_row(u), P), :]).then_inc(ld_xs[u], 16)

                def body(j, u):
                    if ok(j + 2) and (not isinstance(j, int) or j >= 0):
                        before(sp, x_p.sem, x_p.at(j, "x"))
                        sp.dma_start(xs[:, u, :], xs_dram[bass.ds(first_row(j + 2), P), :]).then_inc(ld_xs[u], 16)
                    if ok(j - 1):
                        sp.wait_ge(y_v.sem, y_v.at(j - 1, "y"))
                        sp.dma_start(ys_dram[bass.ds((j - 1) * P, P), :], yb[:, 1 - u, :]).then_inc(st_ys[1 - u], 16)
                units(sp, body)
                for u in range(2):
                    sp.wait_ge(st_ys[u], 8 * UNITS)

            def gpsimd(pool):
                pool.sem_inc(ring_ready, 1)
                for e in range(1, E0):
                    r = e % RING
                    if e >= RING:
                        units_done = pool.value_load(cend_i[0:1, e - RING:e - RING + 1], min_val=1, max_val=UNITS + 1)
                        pool.wait_ge(dn_p.sem, units_done)
                        settled(pool)
                        pool.dma_start(ring_raw[:, r, :], a["w12"][e]).then_inc(ld_ring_sw[r], 16)
                        pool.wait_ge(ld_ring_sw[r], 16 * (e // RING))
                    else:
                        pool.wait_ge(ld_ring[e], 16)
                    nc.gpsimd.tensor_scalar(ring_hi[:, r, :], ring_raw[:, r, :], 1.0, 0.0,
                                            ALU.mult, ALU.add).then_inc(split_g, 1)
                    pool.wait_ge(split_g, e)
                    nc.gpsimd.tensor_tensor(ring_lo[:, r, :], ring_raw[:, r, :], ring_hi[:, r, :],
                                            ALU.subtract).then_inc(ring_ready, 1)

            def tensor(pe):
                def body(j, u, e, e_before):
                    if ok(j - 1):
                        for q, bank in ((0, 3), (1, 4)):
                            pe.wait_ge(ge_a.sem, ge_a.at(j - 1, f"h{q}"))
                            before(pe, tp_v.sem, tp_v.at(j - 2, "ab"[q]))
                            for f in range(4):
                                last = nc.tensor.transpose(ps[bank][:, f * P:(f + 1) * P],
                                                           hid[:, 1 - u, (4 * q + f) * P:(4 * q + f + 1) * P], cv["ident"])
                            last.then_inc(tp_p.sem, 1)
                    if ok(j):
                        r = e % RING
                        pe.wait_ge(x_v.sem, x_v.at(j, "lo"))
                        pe.wait_ge(ring_ready, e + 1)
                        for h in range(2):
                            before(pe, b1_v.sem, b1_v.at(j - 2, f"h{h}"))
                            for n, (xp, wp) in enumerate(((xT_hi, ring_hi), (xT_hi, ring_lo), (xT_lo, ring_hi))):
                                for c in range(C):
                                    o = c * F0 + h * 512
                                    last = nc.tensor.matmul(ps[up_banks[u][h]][:, :], xp[:, u, c, :],
                                                            wp[:, bass.ds(r, 1), o:o + 512],
                                                            start=n == 0 and c == 0, stop=n == 2 and c == C - 1)
                            last.then_inc(up_p.sem, 1)
                    if ok(j + 1):
                        pe.wait_ge(ld_xs[1 - u], dma_at(j + 1, 1 - u))
                        before(pe, x_v.sem, x_v.at(j, "lo"))
                        for c in range(C):
                            last = nc.tensor.transpose(ps[0][:, c * P:(c + 1) * P], xs[:, 1 - u, c * P:(c + 1) * P],
                                                       cv["ident"])
                        last.then_inc(x_p.sem, 1)
                    if ok(j - 1):
                        r = e_before % RING
                        before(pe, y_v.sem, y_v.at(j - 2, "y"))
                        for n, (hp, parts) in enumerate(((hT_hi, (ring_hi, ring_lo)), (hT_lo, (ring_hi,)))):
                            done = tp_v if n else tp_a
                            for f in range(FC):
                                if f == 0:
                                    pe.wait_ge(done.sem, done.at(j - 1, "a"))
                                if f == FC // 2:
                                    pe.wait_ge(done.sem, done.at(j - 1, "b"))
                                o = C * F0 + f * D
                                for wp in parts:
                                    last = nc.tensor.matmul(ps[5][:, 0:D], hp[:, f, :],
                                                            wp[:, bass.ds(r, 1), o:o + D],
                                                            start=n == 0 and f == 0 and wp is ring_hi,
                                                            stop=n == 1 and f == FC - 1)
                        last.then_inc(dn_p.sem, 1)
                units_with_experts(pe, body)

            def scalar(act):
                def body(j, u):
                    if ok(j - 1):
                        for q, bank in ((0, 3), (1, 4)):
                            act.wait_ge(tp_p.sem, tp_p.at(j - 1, "ab"[q]))
                            before(act, dn_p.sem, dn_p.at(j - 2, "y") if not isinstance(j, int) or j >= 2 else 0)
                            nc.scalar.copy(hT_hi[:, 4 * q:4 * q + 4, :], ps[bank][:, :])\
                                .then_inc(tp_a.sem, 1)
                    if ok(j):
                        for h in range(2):
                            act.wait_ge(b1_v.sem, b1_v.at(j, f"h{h}"))
                            v = hid[:, u, h * 512:(h + 1) * 512]
                            nc.scalar.activation(v, v, ACT.Gelu).then_inc(ge_a.sem, 1)
                    if ok(j + 1):
                        act.wait_ge(x_p.sem, x_p.at(j + 1, "x"))
                        before(act, up_p.sem, up_p.at(j - 1, "h1"))
                        nc.scalar.copy(xT_hi[:, 1 - u, :, :], ps[0][:, 0:D]).then_inc(x_a.sem, 1)
                units(act, body)

            def vector(dve):
                dve.wait_ge(ld_rows, 32)

                def body(j, u, e, e_before):
                    if ok(j - 1):
                        for q, bank in ((0, 3), (1, 4)):
                            dve.wait_ge(tp_a.sem, tp_a.at(j - 1, "ab"[q]))
                            nc.vector.tensor_tensor(hT_lo[:, 4 * q:4 * q + 4, :].rearrange("p f t -> p (f t)"),
                                                    ps[bank][:, :], hT_hi[:, 4 * q:4 * q + 4, :].rearrange("p f t -> p (f t)"),
                                                    ALU.subtract).then_inc(tp_v.sem, 1)
                    if ok(j):
                        for h in range(2):
                            dve.wait_ge(up_p.sem, up_p.at(j, f"h{h}"))
                            before(dve, tp_p.sem, tp_p.at(j - 2, "ab"[h]))
                            nc.vector.tensor_tensor(hid[:, u, h * 512:(h + 1) * 512], ps[up_banks[u][h]][:, :],
                                                    b1_sb[:, bass.ds(e, 1), h * 512:(h + 1) * 512].rearrange("p o f -> p (o f)"),
                                                    ALU.add).then_inc(b1_v.sem, 1)
                    if ok(j + 1):
                        dve.wait_ge(x_a.sem, x_a.at(j + 1, "hi"))
                        nc.vector.tensor_tensor(xT_lo[:, 1 - u, :, :].rearrange("p c t -> p (c t)"),
                                                ps[0][:, 0:D], xT_hi[:, 1 - u, :, :].rearrange("p c t -> p (c t)"),
                                                ALU.subtract).then_inc(x_v.sem, 1)
                    if ok(j - 1):
                        dve.wait_ge(dn_p.sem, dn_p.at(j - 1, "y"))
                        before(dve, st_ys[1 - u], dma_at(j - 3, 1 - u) if not isinstance(j, int) or j >= 3 else 0)
                        nc.vector.tensor_tensor(yb[:, 1 - u, :], ps[5][:, 0:D],
                                                b2_sb[:, bass.ds(e_before, 1), :].rearrange("p o f -> p (o f)"), ALU.add)\
                            .then_inc(y_v.sem, 1)
                units_with_experts(dve, body)
            return sync, tensor, scalar, vector, gpsimd

        ld_prep, ld_set, ld_slots = sem("ld_prep"), [sem(f"ld_set{i}") for i in range(SETS)], sem("ld_slots")
        prep_p, prep_v = sem("prep_p"), sem("prep_v")

        def prepare():
            def sync(sp):
                for n, name in enumerate(("dq", "dkT")):
                    sp.dma_start(prep_w[:, n].rearrange("p c d -> p (c d)"), a[name]).then_inc(ld_prep, 16)
                sp.dma_start(slotT, a["slotT"].rearrange("p (c s) -> p c s", c=C)).then_inc(ld_prep, 16)

            def tensor(pe):
                pe.wait_ge(ld_prep, 48)
                for m in range(C):
                    for c in range(C):
                        last = nc.tensor.matmul(ps[0][:, m * NS:(m + 1) * NS], prep_w[:, 0, c, m * P:(m + 1) * P],
                                                slotT[:, c, :], start=c == 0, stop=c == C - 1)
                last.then_inc(prep_p, 1)
                pe.wait_ge(prep_v, 3)
                for c in range(C):
                    for m in range(C):
                        last = nc.tensor.matmul(ps[1][:, c * D + m * P:c * D + (m + 1) * P],
                                                prep_w[:, 1, m, c * P:(c + 1) * P],
                                                qbd[:, m, :, :].rearrange("p h s -> p (h s)"), start=True, stop=True)
                last.then_inc(prep_p, 1)
                for m in range(C):
                    last = nc.tensor.matmul(ps[2][:, m:m + 1], qbd[:, m, :, :].rearrange("p h s -> p (h s)"),
                                            col["dbk"][:, m:m + 1], start=True, stop=True)
                last.then_inc(prep_p, 1)

            def vector(dve):
                nc.vector.memset(vz[:, :, :, 1, :], 0.0)
                dve.wait_ge(prep_p, 1)
                for m in range(C):
                    nc.vector.tensor_scalar(sqT[:, m, :], ps[0][:, m * NS:(m + 1) * NS], QSCALE, qcol[:, 1, m:m + 1],
                                            ALU.mult, ALU.add).then_inc(prep_v, 1)
                dve.wait_ge(prep_v, 2)
                nc.vector.tensor_tensor(qbd, sqT[:, :, None, :].to_broadcast([P, C, HC, NS]),
                                        cv["mask8"][:, None, :, None].to_broadcast([P, C, HC, NS]), ALU.mult)\
                    .then_inc(prep_v, 1)
                dve.wait_ge(prep_p, 3)
                nc.vector.tensor_copy(qa.rearrange("p c d -> p (c d)"), ps[1][:, :])
                nc.vector.tensor_copy(qac, ps[2][:, 0:C])
            return sync, tensor, None, vector, None

        def moe1():
            e_p, e_a, e_v, e_g = sem("m1_p"), sem("m1_a"), sem("m1_v"), sem("m1_g")
            set_used = sem("m1_set_used")
            T = E1 // 4
            FC = F1 // P
            pj = Track(e_p, ["o", "gb", "hT"], T)
            va = Track(e_v, ["o", "stats", "mean", "hat", "gain", "h"], T)
            aj = Track(e_a, ["hT"], T)
            gj = Track(e_g, ["var", "rstd"], T)
            pe2 = track("m1_p2", "u g ta tb y o2", T)
            ac2 = track("m1_a2", "u0 u1 g0 g1 ta o2", T)
            ve2 = track("m1_v2", "m0 m1 tb y", T)
            k_p, k_a = sem("m1_k_p"), sem("m1_k_a")

            def sync(sp):
                sp.dma_start(sel[0:E1].rearrange("p t r -> p (t r)"), a["sel"]).then_inc(ld_slots, 16)
                sp.dma_start(small[0:E1].rearrange("p n d -> p (n d)"), a["small"]).then_inc(ld_slots, 16)
                sp.dma_start(bias1[0:E1].rearrange("p n f -> p (n f)"), a["bias1"]).then_inc(ld_slots, 16)
                for n in range(SETS, 6 * T):
                    sp.wait_ge(set_used, n - SETS + 1)
                    sp.dma_start(wset[:, n % SETS].rearrange("p e f -> p (e f)"), a["wset"][n])\
                        .then_inc(ld_set[n % SETS], 16)

            def tensor(pe):
                def slots_out(t):
                    nc.tensor.matmul(ps[0][:, 0:D], sel[0:E1, t, :], small[0:E1, 0, :], start=True, stop=False)
                    for m in range(C):
                        last = nc.tensor.matmul(ps[0][:, 0:D], oT_all[:, m, 4 * t:4 * t + 4, :], w["do"][:, m, :],
                                                start=False, stop=m == C - 1)
                    last.then_inc(pj.sem, 1)

                def gain_and_bias(t):
                    for n in range(2):
                        last = nc.tensor.matmul(ps[2][:, n * D:(n + 1) * D], sel[0:E1, t, :], small[0:E1, 1 + n, :],
                                                start=True, stop=True)
                    last.then_inc(pj.sem, 1)

                def normalised(t):
                    pe.wait_ge(va.sem, va.at(t, "h"))
                    for c in range(C):
                        last = nc.tensor.transpose(ps[3][:, c * P:(c + 1) * P], hrow[:, c * P:(c + 1) * P], cv["ident"])
                    last.then_inc(pj.sem, 1)

                pe.wait_ge(ld_slots, 48)
                slots_out(0)
                gain_and_bias(0)
                normalised(0)
                n = 0
                for t in range(T):
                    pe.wait_ge(aj.sem, aj.at(t, "hT"))
                    for mat, banks in ((0, (4, 5)), (1, (6, 7))):
                        for h in range(2):
                            before(pe, ac2.sem, ac2.at(t - 1, f"{'ug'[mat]}{h}"))
                            nc.tensor.matmul(ps[banks[h]][:, :], sel[0:E1, t, :], bias1[0:E1, mat, h * 512:(h + 1) * 512],
                                             start=True, stop=False, skip_group_check=True)
                        for c in range(C):
                            pe.wait_ge(ld_set[n % SETS], 16 * (n // SETS + 1))
                            for h in range(2):
                                for e in range(4):
                                    last = nc.tensor.matmul(ps[banks[h]][32 * e:32 * e + 32, :],
                                                            hT[:, c, t, 32 * e:32 * e + 32],
                                                            wset[:, n % SETS, e, h * 512:(h + 1) * 512],
                                                            start=False, stop=c == C - 1, skip_group_check=True)
                            if c == C - 1:
                                last.then_inc(pe2.sem, 1)
                                pe.wait_ge(pe2.sem, pe2.at(t, "ug"[mat]))
                                pe.sem_inc(set_used, 1)
                            else:
                                last.then_inc(set_used, 1)
                            n += 1
                    if t + 1 < T:
                        before(pe, ac2.sem, ac2.at(t - 1, "o2"))
                        slots_out(t + 1)
                    for q in range(2):
                        pe.wait_ge(ve2.sem, ve2.at(t, f"m{q}"))
                        if q == 0:
                            before(pe, ac2.sem, ac2.at(t - 1, "ta"))
                        else:
                            before(pe, ve2.sem, ve2.at(t - 1, "tb"))
                        for f in range(4):
                            last = nc.tensor.transpose(ps[2 + q][:, f * P:(f + 1) * P],
                                                       us[:, (4 * q + f) * P:(4 * q + f + 1) * P], cv["ident"])
                        last.then_inc(pe2.sem, 1)
                    before(pe, ve2.sem, ve2.at(t - 1, "y"))
                    nc.tensor.matmul(ps[1][:, 0:D], sel[0:E1, t, :], small[0:E1, 3, :],
                                     start=True, stop=False, skip_group_check=True)
                    for q in range(2):
                        pe.wait_ge(ac2.sem, ac2.at(t, "ta"))
                        if q == 1:
                            pe.wait_ge(ve2.sem, ve2.at(t, "tb"))
                        pe.wait_ge(ld_set[n % SETS], 16 * (n // SETS + 1))
                        for f in range(4):
                            for e in range(4):
                                last = nc.tensor.matmul(ps[1][32 * e:32 * e + 32, 0:D],
                                                        ugT[:, 4 * q + f, 32 * e:32 * e + 32],
                                                        wset[:, n % SETS, e, f * D:(f + 1) * D],
                                                        start=False, stop=q == 1 and f == 3, skip_group_check=True)
                        if q == 1:
                            last.then_inc(pe2.sem, 1)
                            pe.wait_ge(pe2.sem, pe2.at(t, "y"))
                            pe.sem_inc(set_used, 1)
                        else:
                            last.then_inc(set_used, 1)
                        n += 1
                    if t + 1 < T:
                        gain_and_bias(t + 1)
                        pe.wait_ge(va.sem, va.at(t + 1, "o"))
                    pe.wait_ge(ve2.sem, ve2.at(t, "y"))
                    before(pe, ac2.sem, ac2.at(t - 1, "o2"))
                    for c in range(C):
                        last = nc.tensor.transpose(ps[0][:, c * P:(c + 1) * P], orow[:, t, c * P:(c + 1) * P], cv["ident"])
                    last.then_inc(pe2.sem, 1)
                    if t + 1 < T:
                        normalised(t + 1)
                pe.wait_ge(ac2.sem, ac2.at(T - 1, "o2"))
                for m in range(C):
                    for c in range(C):
                        last = nc.tensor.matmul(ps[6 + m][:, :], w["ck"][:, c, m * P:(m + 1) * P],
                                                oT2[:, c, :, :].rearrange("p s b -> p (s b)"),
                                                start=c == 0, stop=c == C - 1)
                    last.then_inc(k_p, 1)

            def scalar(act):
                def normalised(t):
                    act.wait_ge(pj.sem, pj.at(t, "hT"))
                    nc.scalar.copy(hT[:, :, t, :], ps[3][:, 0:D].rearrange("p (c r) -> p c r", c=C)).then_inc(aj.sem, 1)

                normalised(0)
                for t in range(T):
                    for mat, banks, dst in ((0, (4, 5), us), (1, (6, 7), gs)):
                        act.wait_ge(pe2.sem, pe2.at(t, "ug"[mat]))
                        if mat == 0:
                            before(act, pe2.sem, pe2.at(t - 1, "tb"))
                        for h in range(2):
                            nc.scalar.activation(dst[:, h * 512:(h + 1) * 512], ps[banks[h]][:, :], ACT.Silu)\
                                .then_inc(ac2.sem, 1)
                    act.wait_ge(pe2.sem, pe2.at(t, "ta"))
                    before(act, pe2.sem, pe2.at(t - 1, "y"))
                    nc.scalar.copy(ugT[:, 0:4, :].rearrange("p f r -> p (f r)"), ps[2][:, :]).then_inc(ac2.sem, 1)
                    act.wait_ge(pe2.sem, pe2.at(t, "o2"))
                    nc.scalar.copy(oT2[:, :, 4 * t:4 * t + 4, :].rearrange("p c s b -> p c (s b)"),
                                   ps[0][:, 0:D].rearrange("p (c r) -> p c r", c=C)).then_inc(ac2.sem, 1)
                    if t + 1 < T:
                        normalised(t + 1)
                for m in range(C):
                    act.wait_ge(k_p, m + 1)
                    nc.scalar.activation(kTall[:, m, :, :].rearrange("p s b -> p (s b)"), ps[6 + m][:, :], ACT.Identity,
                                         bias=col["cbk"][:, m:m + 1])

            def vector(dve):
                def slots_out(t):
                    dve.wait_ge(pj.sem, pj.at(t, "o"))
                    nc.vector.tensor_tensor(orow[:, t, :], ps[0][:, 0:D], row["dbo"], ALU.add).then_inc(va.sem, 1)
                    dve.wait_ge(va.sem, va.at(t, "o"))
                    nc.vector.bn_stats(st1, orow[:, t, :]).then_inc(va.sem, 1)
                    dve.wait_ge(va.sem, va.at(t, "stats"))
                    nc.vector.bn_aggr(mv1, st1).then_inc(va.sem, 1)

                def hat(t):
                    dve.wait_ge(gj.sem, gj.at(t, "rstd"))
                    before(dve, pj.sem, pj.at(t - 1, "hT"))
                    nc.vector.tensor_scalar(hrow, orow[:, t, :], mv1[:, 0:1], rs1[:, 1:2], ALU.subtract, ALU.mult)\
                        .then_inc(va.sem, 1)

                def gain_and_bias(t):
                    dve.wait_ge(va.sem, va.at(t, "hat"))
                    dve.wait_ge(pj.sem, pj.at(t, "gb"))
                    nc.vector.tensor_tensor(hrow, ps[2][:, 0:D], hrow, ALU.mult).then_inc(va.sem, 1)
                    dve.wait_ge(va.sem, va.at(t, "gain"))
                    nc.vector.tensor_tensor(hrow, ps[2][:, D:2 * D], hrow, ALU.add).then_inc(va.sem, 1)

                slots_out(0)
                hat(0)
                gain_and_bias(0)
                for t in range(T):
                    for q in range(2):
                        dve.wait_ge(ac2.sem, ac2.at(t, f"g{q}"))
                        v = us[:, q * 512:(q + 1) * 512]
                        nc.vector.tensor_tensor(v, v, gs[:, q * 512:(q + 1) * 512], ALU.mult).then_inc(ve2.sem, 1)
                    if t + 1 < T:
                        slots_out(t + 1)
                    dve.wait_ge(pe2.sem, pe2.at(t, "tb"))
                    before(dve, pe2.sem, pe2.at(t - 1, "y"))
                    nc.vector.tensor_copy(ugT[:, 4:8, :].rearrange("p f r -> p (f r)"), ps[3][:, :]).then_inc(ve2.sem, 1)
                    if t + 1 < T:
                        hat(t + 1)
                    dve.wait_ge(pe2.sem, pe2.at(t, "y"))
                    nc.vector.tensor_tensor(orow[:, t, :], ps[1][:, 0:D], orow[:, t, :], ALU.add).then_inc(ve2.sem, 1)
                    if t + 1 < T:
                        gain_and_bias(t + 1)

            def gpsimd(pool):
                for t in range(T):
                    pool.wait_ge(va.sem, va.at(t, "mean"))
                    nc.gpsimd.tensor_tensor(rs1[:, 0:1], mv1[:, 1:2], eps_sb[:, :], ALU.add).then_inc(e_g, 1)
                    pool.wait_ge(gj.sem, gj.at(t, "var"))
                    nc.gpsimd.tensor_tensor(rs1[:, 1:2], rs1[:, 0:1], mhalf[:, :], ALU.pow).then_inc(e_g, 1)
            return sync, tensor, scalar, vector, gpsimd

        def combine():
            n = "c_"
            ld_x3 = [sem(n + "ld_x3_0"), sem(n + "ld_x3_1")]
            st_out = [sem(n + "st_out0"), sem(n + "st_out1")]
            qv_p = track(n + "qv_p", "q v")
            s_p = track(n + "s_p", "s")
            t_p = track(n + "t_p", "pT av")
            o_p = track(n + "o_p", "o")
            q_a = track(n + "q_a", "q")
            t_a = track(n + "t_a", "pT aT")
            e_a = track(n + "e_a", "e")
            p_v = track(n + "p_v", "sum rs pn")
            s_v = track(n + "s_v", "v max sub")
            o_v = track(n + "o_v", "t out")
            k_g = track(n + "k_g", "rep kb")
            v_g = track(n + "v_g", "vbd")
            steady = (4, B - 2)

            def sync(sp):
                for u in range(2):
                    sp.dma_start(x3l[:, u].rearrange("p c t -> p (c t)"), x3T_dram[u]).then_inc(ld_x3[u], 16)

                def body(k, u):
                    if valid(k + 2) and (not isinstance(k, int) or k >= 0):
                        sp.wait_ge(qv_p.sem, qv_p.at(k, "q"))
                        sp.dma_start(x3l[:, u].rearrange("p c t -> p (c t)"), x3T_dram[k + 2]).then_inc(ld_x3[u], 16)
                    if valid(k - 2):
                        sp.wait_ge(o_v.sem, o_v.at(k - 2, "out"))
                        sp.dma_start(out[k - 2], cout[:, u, :]).then_inc(st_out[u], 16)
                pipeline(sp, body, 0, B + 2, steady)
                for s in st_out:
                    sp.wait_ge(s, 8 * B)

            def tensor(pe):
                def body(k, u):
                    if valid(k):
                        pe.wait_ge(ld_x3[u], dma_at(k, u))
                        before(pe, q_a.sem, q_a.at(k - 1, "q"))
                        for m in range(C):
                            for c in range(C):
                                last = nc.tensor.matmul(ps[0][:, m * P:(m + 1) * P], w["cq"][:, c, m * P:(m + 1) * P],
                                                        x3l[:, u, c, :], start=c == 0, stop=c == C - 1)
                        last.then_inc(qv_p.sem, 1)
                        pe.wait_ge(k_g.sem, k_g.at(k, "rep"))
                        before(pe, s_v.sem, s_v.at(k - 1, "v"))
                        for c in range(C):
                            last = nc.tensor.matmul(ps[1][:, 0:D], orep[:, u, c, :, :].rearrange("p h s -> p (h s)"),
                                                    w["cv"][:, c, :], start=c == 0, stop=c == C - 1)
                        last.then_inc(qv_p.sem, 1)
                    if valid(k - 1):
                        pe.wait_ge(p_v.sem, p_v.at(k - 1, "pn"))
                        before(pe, t_a.sem, t_a.at(k - 2, "pT"))
                        for c in range(C):
                            last = nc.tensor.transpose(ps[3][:, c * P:(c + 1) * P], cpn[:, c * P:(c + 1) * P], cv["ident"])
                        last.then_inc(t_p.sem, 1)
                    if valid(k):
                        pe.wait_ge(q_a.sem, q_a.at(k, "q"))
                        pe.wait_ge(k_g.sem, k_g.at(k, "kb"))
                        before(pe, s_v.sem, s_v.at(k - 1, "sub"))
                        for m in range(C):
                            last = nc.tensor.matmul(ps[2][:, m * P:(m + 1) * P], cqT[:, u, m, :],
                                                    ckb[:, u, m, :, :].rearrange("p h s -> p (h s)"), start=True, stop=True)
                        last.then_inc(s_p.sem, 1)
                    if valid(k - 2):
                        pe.wait_ge(t_a.sem, t_a.at(k - 2, "aT"))
                        before(pe, o_v.sem, o_v.at(k - 3, "t") if valid(k - 3) else 0)
                        for c in range(C):
                            last = nc.tensor.matmul(ps[5][:, 0:D], caT[:, c, :], w["co"][:, c, :],
                                                    start=c == 0, stop=c == C - 1)
                        last.then_inc(o_p.sem, 1)
                    if valid(k - 1):
                        pe.wait_ge(t_a.sem, t_a.at(k - 1, "pT"))
                        pe.wait_ge(v_g.sem, v_g.at(k - 1, "vbd"))
                        before(pe, t_a.sem, t_a.at(k - 2, "aT"))
                        for m in range(C):
                            last = nc.tensor.matmul(ps[4][:, m * P:(m + 1) * P], cvbd[:, 1 - u, m, :], cpT[:, m, :],
                                                    start=True, stop=True)
                        last.then_inc(t_p.sem, 1)
                pipeline(pe, body, 0, B + 2, steady)

            def scalar(act):
                def body(k, u):
                    if valid(k):
                        act.wait_ge(qv_p.sem, qv_p.at(k, "q"))
                        before(act, s_p.sem, s_p.at(k - 2, "s"))
                        for c in range(C):
                            last = nc.scalar.activation(cqT[:, u, c, :], ps[0][:, c * P:(c + 1) * P], ACT.Identity,
                                                        bias=qcol[:, 2, c:c + 1], scale=QSCALE)
                        last.then_inc(q_a.sem, 1)
                    if valid(k - 1):
                        act.wait_ge(t_p.sem, t_p.at(k - 1, "pT"))
                        nc.scalar.copy(cpT.rearrange("p c t -> p (c t)"), ps[3][:, 0:D]).then_inc(t_a.sem, 1)
                        act.wait_ge(t_p.sem, t_p.at(k - 1, "av"))
                        before(act, o_p.sem, o_p.at(k - 2, "o"))
                        nc.scalar.copy(caT.rearrange("p c t -> p (c t)"), ps[4][:, 0:D]).then_inc(t_a.sem, 1)
                    if valid(k):
                        act.wait_ge(s_v.sem, s_v.at(k, "sub"))
                        nc.scalar.activation(csc[:, u, :], csc[:, u, :], ACT.Exp).then_inc(e_a.sem, 1)
                pipeline(act, body, 0, B + 1, steady)

            def vector(dve):
                def heads(v):
                    return v.rearrange("p (h s) -> p h s", h=H)

                def body(k, u):
                    if valid(k - 1):
                        i = k - 1
                        e = csc[:, 1 - u, :]
                        dve.wait_ge(e_a.sem, e_a.at(i, "e"))
                        nc.vector.tensor_reduce(csm, heads(e), AX, ALU.add).then_inc(p_v.sem, 1)
                        dve.wait_ge(p_v.sem, p_v.at(i, "sum"))
                        nc.vector.reciprocal(csm, csm).then_inc(p_v.sem, 1)
                        dve.wait_ge(p_v.sem, p_v.at(i, "rs"))
                        before(dve, t_p.sem, t_p.at(i - 1, "pT"))
                        nc.vector.tensor_tensor(heads(cpn), heads(e), csm[:, :, None].to_broadcast([P, H, NS]), ALU.mult)\
                            .then_inc(p_v.sem, 1)
                    if valid(k):
                        dve.wait_ge(qv_p.sem, qv_p.at(k, "v"))
                        before(dve, v_g.sem, v_g.at(k - 2, "vbd"))
                        nc.vector.tensor_tensor(cvb[:, u, :], ps[1][:, 0:D], row["cbv"], ALU.add).then_inc(s_v.sem, 1)
                        dve.wait_ge(s_p.sem, s_p.at(k, "s"))
                        nc.vector.tensor_reduce(cmx, heads(ps[2][:, 0:D]), AX, ALU.max).then_inc(s_v.sem, 1)
                        dve.wait_ge(s_v.sem, s_v.at(k, "max"))
                        nc.vector.tensor_tensor(heads(csc[:, u, :]), heads(ps[2][:, 0:D]),
                                                cmx[:, :, None].to_broadcast([P, H, NS]), ALU.subtract).then_inc(s_v.sem, 1)
                    if valid(k - 2):
                        i = k - 2
                        dve.wait_ge(o_p.sem, o_p.at(i, "o"))
                        before(dve, o_v.sem, o_v.at(i - 1, "out"))
                        nc.vector.tensor_tensor(ctmp, ps[5][:, 0:D], row["cbo"], ALU.add).then_inc(o_v.sem, 1)
                        dve.wait_ge(o_v.sem, o_v.at(i, "t"))
                        before(dve, st_out[u], dma_at(k - 4, u) if not isinstance(k, int) or k >= 4 else 0)
                        nc.vector.scalar_tensor_tensor(out=cout[:, u, :], in0=ctmp, scalar=tg[:, 3:4], in1=x_all[:, i],
                                                       op0=ALU.mult, op1=ALU.add).then_inc(o_v.sem, 1)
                pipeline(dve, body, 0, B + 2, steady)

            def gpsimd(pool):
                def slots(i, u):
                    before(pool, qv_p.sem, qv_p.at(i - 2, "v"))
                    for c in range(C):
                        last = nc.gpsimd.tensor_copy(orep[:, u, c], oT2[:, c, None, :, i].to_broadcast([P, HC, NS]))
                    last.then_inc(k_g.sem, 1)
                    before(pool, s_p.sem, s_p.at(i - 2, "s"))
                    nc.gpsimd.tensor_tensor(ckb[:, u], kTall[:, :, None, :, i].to_broadcast([P, C, HC, NS]),
                                            cv["mask8"][:, None, :, None].to_broadcast([P, C, HC, NS]), ALU.mult)\
                        .then_inc(k_g.sem, 1)

                def body(k, u):
                    if valid(k + 1):
                        slots(k + 1, 1 - u)
                    if valid(k):
                        pool.wait_ge(s_v.sem, s_v.at(k, "v"))
                        before(pool, t_p.sem, t_p.at(k - 2, "av"))
                        nc.gpsimd.tensor_tensor(cvbd[:, u].rearrange("p c (h d) -> p c h d", h=HC),
                                                cvb[:, u, :].rearrange("p (c h d) -> p c h d", c=C, h=HC),
                                                cv["mask8"][:, None, :, None].to_broadcast([P, C, HC, DH]), ALU.mult)\
                            .then_inc(v_g.sem, 1)
                pipeline(pool, body, -1, B, steady)
            return sync, tensor, scalar, vector, gpsimd

        def setup():
            def sync(sp):
                sp.dma_start(x_all[:, 0], a["x"][0]).then_inc(ld_x[0], 16)
                sp.dma_start(x_all[:, 1], a["x"][1]).then_inc(ld_x[1], 16)
                for dst, src in ((const[:, :], a["const"]),
                                 (w_sb[:, 0:4].rearrange("p n c d -> p (n c d)"), a["weights"][:, 0:4 * C * D]),
                                 (col_sb[:, :, :].rearrange("p n c -> p (n c)"), a["cols"]),
                                 (wg_sb[:, :, :].rearrange("p c e -> p (c e)"), a["wg"]),
                                 (row_sb[:, :, :].rearrange("p n d -> p (n d)"), a["rows"].partition_broadcast(P)),
                                 (bg_sb[:, :], a["bg"].partition_broadcast(P)),
                                 (gates[:, :], a["gates"].partition_broadcast(P))):
                    sp.dma_start(dst, src).then_inc(ld_const, 16)
                sp.wait_ge(setup_v, 1)
                sp.dma_start(xs_dram[DUMP:DUMP + P, :], zero[:, :]).then_inc(zeroed, 16)

            def vector(dve):
                nc.vector.memset(zero[:, :], 0.0).then_inc(setup_v, 1)
                nc.vector.memset(ones[:, :], 1.0).then_inc(setup_v, 1)
                nc.vector.memset(eps_sb[:, :], EPS)
                for part in range(3):
                    nc.vector.memset(one_zero[:, part, :], 1.0 if part != 1 else 0.0)
                nc.vector.memset(mhalf[:, :], -0.5)
                nc.vector.memset(vz[:, :, :, 1, :], 0.0)
                dve.wait_ge(ld_const, 16 * 7)
                nc.vector.tensor_copy(next_row[:, :], cv["first"])
                for n, name in enumerate(("bq0", "dbq", "cbq")):
                    nc.vector.tensor_scalar(qcol[:, n, :], col[name], QSCALE, None, ALU.mult)
                dve.wait_ge(setup_v, 2)
                for c in range(C):
                    last = nc.vector.tensor_scalar(pr[:, 0, c, 0:P], ones[:, :], col["bv0"][:, c:c + 1], None, ALU.mult)
                last.then_inc(setup_v, 1)
                dve.wait_ge(setup_p, 1)
                nc.vector.tensor_tensor(row["bo0"], ps[0][:, 0:D], row["bo0"], ALU.add).then_inc(setup_v, 1)
                dve.wait_ge(setup_v, 4)
                dve.wait_ge(setup_a, 1)
                nc.vector.tensor_scalar(row["bo0"], row["bo0"], tg[:, 0:1], None, ALU.mult)

            def tensor(pe):
                pe.wait_ge(setup_v, 3)
                pe.wait_ge(ld_const, 16 * 7)
                for c in range(C):
                    last = nc.tensor.matmul(ps[0][:, 0:D], pr[:, 0, c, 0:P], w["o0"][:, c, :], start=c == 0, stop=c == C - 1)
                last.then_inc(setup_p, 1)

            def scalar(act):
                act.wait_ge(ld_const, 16 * 7)
                nc.scalar.activation(tg[:, :], gates[:, :], ACT.Tanh).then_inc(setup_a, 1)
            return sync, tensor, scalar, vector, None

        def run(programs):
            with nc.Block() as block:
                sync, tensor, scalar, vector, gpsimd = programs
                if sync:
                    block.sync(lambda e: sync(e))
                if tensor:
                    block.tensor(lambda e: tensor(e))
                if scalar:
                    block.scalar(lambda e: scalar(e))
                if vector:
                    block.vector(lambda e: vector(e))
                if gpsimd:
                    block.gpsimd(lambda e: gpsimd(e))

        run(setup())
        run(attention(0))
        run(routing())
        run(moe0())
        run(prepare())
        run(attention(1))
        run(moe1())
        run(combine())


def arrange(i):
    f = {k: np.ascontiguousarray(v) for k, v in i.items()}

    def chunks(m):
        return m.reshape(-1, P, m.shape[-1]).transpose(1, 0, 2).reshape(P, -1)

    p = "L1_ffn_"
    squares = [f["L0_xattn_w_q"], f["L0_xattn_w_k"], f["L0_xattn_w_v"], f["L0_xattn_w_o"],
               f["L1_xattn_Wq"].T, f["L1_xattn_Wk"].T, f["L1_xattn_Wv"].T, f["L1_xattn_Wo"].T,
               f[p + "d_Wv"], f[p + "d_Wo"], f[p + "c_Wq"], f[p + "c_Wk"], f[p + "c_Wv"], f[p + "c_Wo"]]
    rows = [f["L0_xattn_b_o"], f["L0_ffn_gamma"], f["L0_ffn_beta"],
            f[p + "d_bv"], f[p + "d_bo"], f[p + "c_bv"], f[p + "c_bo"]]
    cols = [f["L0_xattn_b_q"], f["L0_xattn_b_k"], f["L0_xattn_b_v"], f[p + "d_bq"], f[p + "d_bk"], f[p + "c_bq"], f[p + "c_bk"]]
    t = np.arange(P)
    const = np.concatenate([np.eye(P), t[:, None] < t[None, :], t[:, None] // DH == np.arange(HC),
                            np.broadcast_to(np.arange(E0), (P, E0)), np.broadcast_to(P * np.arange(B), (P, B)),
                            np.broadcast_to(np.arange(UNITS), (P, UNITS)),
                            np.broadcast_to(TOKENS * np.arange(E0), (P, E0)), t[:, None]], axis=1).astype(np.float32)
    w12 = np.concatenate([
        f["L0_ffn_W1"].transpose(0, 2, 1).reshape(E0, C, P, F0).transpose(0, 2, 1, 3).reshape(E0, P, C * F0),
        f["L0_ffn_W2"].transpose(0, 2, 1).reshape(E0, F0 // P, P, D).transpose(0, 2, 1, 3).reshape(E0, P, -1)], axis=2)
    r = np.arange(P)
    sel = np.concatenate([4 * t4 + r[None, :] // B == np.arange(E1)[:, None] for t4 in range(E1 // 4)], axis=1)
    small = [f[p + "slot_query"][0], f[p + "e_ln_g"], f[p + "e_ln_b"], f[p + "e_b2"]]
    sets = []
    for t4 in range(E1 // 4):
        for m in (f[p + "e_W1"], f[p + "e_Wg"]):
            for c in range(C):
                sets.append(m[4 * t4:4 * t4 + 4, c * P:(c + 1) * P, :].transpose(1, 0, 2).reshape(P, -1))
        for q in range(2):
            m = f[p + "e_W2"][4 * t4:4 * t4 + 4, 512 * q:512 * (q + 1), :].reshape(4, 4, P, D)
            sets.append(m.transpose(2, 0, 1, 3).reshape(P, -1))
    s = {
        "dq": chunks(f[p + "d_Wq"]), "dkT": chunks(f[p + "d_Wk"].T),
        "slotT": f[p + "slot_query"][0].T.reshape(C, P, NS).transpose(1, 0, 2).reshape(P, -1),
        "sel": sel.astype(np.float32), "small": np.concatenate(small, axis=1),
        "bias1": np.concatenate([f[p + "e_b1"], f[p + "e_bg"]], axis=1), "wset": np.stack(sets),
        "x": f["x"], "ctxT": f["ctx_1024"].reshape(B, P, C, P).transpose(0, 3, 2, 1).reshape(B, P, C * P),
        "fside": f["fside_BxS2_0"], "gates": np.concatenate([f["g_xattn"], f["g_ffn"]]).reshape(1, 4),
        "weights": np.concatenate([chunks(m) for m in squares], axis=1),
        "rows": np.stack(rows).reshape(1, -1), "cols": np.stack(cols).reshape(-1, P).T,
        "wg": chunks(f["L0_ffn_Wg"].T), "bg": f["L0_ffn_bg"].reshape(1, E0), "const": const,
        "w12": w12, "b1": f["L0_ffn_b1"].reshape(1, -1), "b2": f["L0_ffn_b2"].reshape(1, -1),
    }
    return {k: np.ascontiguousarray(v) for k, v in s.items()}


def kernel(**inputs):
    from concourse import bacc
    from concourse.bass_utils import run_bass_kernel_spmd

    nc = bacc.Bacc("TRN2", target_bir_lowering=False, num_devices=1)
    arrays = {f"{name}_dram": v for name, v in arrange(inputs).items()}
    given = {name[:-5]: nc.dram_tensor(name, v.shape, mybir.dt.from_np(v.dtype), kind="ExternalInput").ap()
             for name, v in arrays.items()}
    out = nc.dram_tensor("out_dram", (B, P, D), F32, kind="ExternalOutput").ap()
    build(nc, given, out)
    result = run_bass_kernel_spmd(nc, [arrays], core_ids=[0])
    return result.results[0]["out_dram"]
```
